# Optimizing a Trainium2 kernel written in Bass

```python
import numpy as np
import jax
import jax.numpy as jnp

def _softmax(x, axis=-1):
    return jax.nn.softmax(x, axis=axis)
def _gelu(x):
    return jax.nn.gelu(x, approximate=True)
def _silu(x):
    return jax.nn.silu(x)
def _sigmoid(x):
    return jax.nn.sigmoid(x)
def _layernorm(x, axis=-1, eps=1e-5):
    m = jnp.mean(x, axis=axis, keepdims=True)
    v = jnp.var(x, axis=axis, keepdims=True)
    return (x - m) / jnp.sqrt(v + eps)
def _scatter_add(tgt, idx, src, axis=0):
    return tgt.at[idx].add(src)
def _segment_sum(src, seg, n):
    return jax.ops.segment_sum(src, seg, n)

kernel_name = 'mk_adj_resnorm_d4_adj_256_978467'

def setup_inputs(seed: int = 0):
    np.random.seed(seed)
    _w = jnp.asarray
    def _rec_inputs():
        import jax
        import jax.numpy as jnp
        _gk = jax.random.key(seed)
        x = -0.0005207 + 1.001 * jax.random.normal(jax.random.fold_in(_gk, 1), (128, 128, 256), jnp.float32)
        _w = (1.0 + jnp.arange(128, dtype=jnp.float32)) ** -0.5
        _w = _w / _w.mean()
        _pij = jnp.clip(0.0625 * _w[:, None] * _w[None, :], 0.0, 1.0)
        _a = jax.random.uniform(jax.random.fold_in(_gk, 2), (128, 128, 128)) < _pij
        adj = _a.astype(jnp.int32)
        return x, adj
    x, adj = _rec_inputs()
    def _L0_gnn_setup():
        import jax, jax.numpy as jnp
        import numpy as np
        NEG_INF = -1000000000.0
        LRELU_ALPHA = 0.2
        key = jax.random.key(seed)
        k1, k2, k3, k4, k5 = jax.random.split(key, 5)
        B, N, Din, H, F = (8, 1024, 256, 4, 64)
        X = jax.random.normal(k1, (B, N, Din), dtype=jnp.float32)
        A = jax.random.randint(k2, (B, N, N), 0, 2).astype(jnp.int32)
        W = jax.random.normal(k3, (Din, H * F), dtype=jnp.float32) * np.sqrt(2.0 / (Din + H * F))
        a_src = jax.random.normal(k4, (H, F), dtype=jnp.float32) * np.sqrt(2.0 / (1 + F))
        a_dst = jax.random.normal(k5, (H, F), dtype=jnp.float32) * np.sqrt(2.0 / (1 + F))
        return {'X': X, 'A': A, 'W': W, 'a_src': a_src, 'a_dst': a_dst}
    _L0_gnn_all = _L0_gnn_setup()
    _L0_gnn_in = {k: v for k, v in _L0_gnn_all.items() if k in ('W', 'a_src', 'a_dst', )}
    del _L0_gnn_all

    def _L1_gnn_setup():
        import jax, jax.numpy as jnp
        import numpy as np
        OUT = 256
        NUM_LAYERS = 3

        def _gru_cell(inp, h, w_ih, w_hh, b_ih, b_hh):
            gi = inp @ w_ih.T + b_ih
            gh = h @ w_hh.T + b_hh
            i_r, i_z, i_n = jnp.split(gi, 3, axis=-1)
            h_r, h_z, h_n = jnp.split(gh, 3, axis=-1)
            r = jax.nn.sigmoid(i_r + h_r)
            z = jax.nn.sigmoid(i_z + h_z)
            n = jnp.tanh(i_n + r * h_n)
            return (1.0 - z) * n + z * h
        key = jax.random.key(seed)
        ks = jax.random.split(key, 8)
        B, N, D = (32, 512, 256)
        x = jax.random.normal(ks[0], (B, N, D), dtype=jnp.float32)
        adj = jax.random.randint(ks[1], (B, N, N), 0, 2, dtype=jnp.int32)
        s = 1.0 / np.sqrt(OUT)
        weight = jax.random.uniform(ks[2], (NUM_LAYERS, OUT, OUT), jnp.float32, -s, s)
        w_ih = jax.random.uniform(ks[3], (3 * OUT, OUT), jnp.float32, -s, s)
        w_hh = jax.random.uniform(ks[4], (3 * OUT, OUT), jnp.float32, -s, s)
        b_ih = jax.random.uniform(ks[5], (3 * OUT,), jnp.float32, -s, s)
        b_hh = jax.random.uniform(ks[6], (3 * OUT,), jnp.float32, -s, s)
        return {'x': x, 'adj': adj, 'weight': weight, 'w_ih': w_ih, 'w_hh': w_hh, 'b_ih': b_ih, 'b_hh': b_hh}
    _L1_gnn_all = _L1_gnn_setup()
    _L1_gnn_in = {k: v for k, v in _L1_gnn_all.items() if k in ('weight', 'w_ih', 'w_hh', 'b_ih', 'b_hh', )}
    del _L1_gnn_all

    def _L2_gnn_setup():
        import jax, jax.numpy as jnp
        import numpy as np
        B, N, D_IN, D_OUT, R = (8, 2048, 256, 256, 4)
        key = jax.random.key(seed)
        k1, k2, k3, k4 = jax.random.split(key, 4)
        x = jax.random.normal(k1, (B, N, D_IN), dtype=jnp.float32)
        adj = jnp.zeros((1,), dtype=jnp.float32)
        relation = jax.random.randint(k2, (B, N, N), 0, R + 1, dtype=jnp.int32)
        weight = jax.random.normal(k3, (R, D_IN, D_OUT), dtype=jnp.float32) * 0.05
        bias = jax.random.normal(k4, (D_OUT,), dtype=jnp.float32) * 0.05
        return {'x': x, 'adj': adj, 'relation': relation, 'weight': weight, 'bias': bias}
    _L2_gnn_all = _L2_gnn_setup()
    _L2_gnn_in = {k: v for k, v in _L2_gnn_all.items() if k in ('adj', 'weight', 'bias', )}
    del _L2_gnn_all

    def _L3_gnn_setup():
        import jax, jax.numpy as jnp
        import numpy as np
        B, N, IN_F, OUT_F = (32, 1024, 256, 256)
        ALPHA = 0.2
        NEG_INF = -9000000000000000.0
        key = jax.random.key(seed)
        k1, k2, k3, k4 = jax.random.split(key, 4)
        h = jax.random.normal(k1, (B, N, IN_F), dtype=jnp.float32)
        adj = jax.random.randint(k2, (B, N, N), 0, 2, dtype=jnp.int32)
        W = jax.random.normal(k3, (OUT_F, IN_F), dtype=jnp.float32) * 0.05
        a = jax.random.normal(k4, (1, 2 * OUT_F), dtype=jnp.float32) * 0.05
        return {'h': h, 'adj': adj, 'W': W, 'a': a}
    _L3_gnn_all = _L3_gnn_setup()
    _L3_gnn_in = {k: v for k, v in _L3_gnn_all.items() if k in ('W', 'a', )}
    del _L3_gnn_all

    return {
        "x": x,
        "adj": adj,
        "L0_gnn_W": _L0_gnn_in["W"],
        "L0_gnn_a_src": _L0_gnn_in["a_src"],
        "L0_gnn_a_dst": _L0_gnn_in["a_dst"],
        "L1_gnn_weight": _L1_gnn_in["weight"],
        "L1_gnn_w_ih": _L1_gnn_in["w_ih"],
        "L1_gnn_w_hh": _L1_gnn_in["w_hh"],
        "L1_gnn_b_ih": _L1_gnn_in["b_ih"],
        "L1_gnn_b_hh": _L1_gnn_in["b_hh"],
        "L2_gnn_adj": _L2_gnn_in["adj"],
        "L2_gnn_weight": _L2_gnn_in["weight"],
        "L2_gnn_bias": _L2_gnn_in["bias"],
        "L3_gnn_W": _L3_gnn_in["W"],
        "L3_gnn_a": _L3_gnn_in["a"],
    }

def reference(x, adj, L0_gnn_W, L0_gnn_a_src, L0_gnn_a_dst, L1_gnn_weight, L1_gnn_w_ih, L1_gnn_w_hh, L1_gnn_b_ih, L1_gnn_b_hh, L2_gnn_adj, L2_gnn_weight, L2_gnn_bias, L3_gnn_W, L3_gnn_a):
    import jax
    import jax.numpy as jnp
    def _L0_gnn_ref(X, A, W, a_src, a_dst):
        import jax, jax.numpy as jnp
        import numpy as np
        NEG_INF = -1000000000.0
        LRELU_ALPHA = 0.2
        B, N, _ = X.shape
        H, F = a_src.shape
        Wh = (X @ W).reshape(B, N, H, F)
        e_src = jnp.einsum('bnhf,hf->bnh', Wh, a_src)
        e_dst = jnp.einsum('bjhf,hf->bjh', Wh, a_dst)
        e = jax.nn.leaky_relu(e_src[:, :, None, :] + e_dst[:, None, :, :], LRELU_ALPHA)
        mask = (A > 0)[..., None]
        e = jnp.where(mask, e, NEG_INF)
        alpha = jax.nn.softmax(e, axis=2)
        Hout = jnp.einsum('bijh,bjhf->bihf', alpha, Wh)
        Hout = jax.nn.elu(Hout)
        return Hout.reshape(B, N, H * F)

    def _L1_gnn_ref(x, adj, weight, w_ih, w_hh, b_ih, b_hh):
        import jax, jax.numpy as jnp
        import numpy as np
        OUT = 256
        NUM_LAYERS = 3

        def _gru_cell(inp, h, w_ih, w_hh, b_ih, b_hh):
            gi = inp @ w_ih.T + b_ih
            gh = h @ w_hh.T + b_hh
            i_r, i_z, i_n = jnp.split(gi, 3, axis=-1)
            h_r, h_z, h_n = jnp.split(gh, 3, axis=-1)
            r = jax.nn.sigmoid(i_r + h_r)
            z = jax.nn.sigmoid(i_z + h_z)
            n = jnp.tanh(i_n + r * h_n)
            return (1.0 - z) * n + z * h
        A = (adj != 0).astype(x.dtype)
        h = x
        L = weight.shape[0]
        for i in range(L):
            m = jnp.einsum('bnd,de->bne', h, weight[i])
            aggr = jnp.einsum('bst,bsd->btd', A, m)
            h = _gru_cell(aggr, h, w_ih, w_hh, b_ih, b_hh)
        return h

    def _L2_gnn_ref(x, adj, relation, weight, bias):
        import jax, jax.numpy as jnp
        import numpy as np
        B, N, D_IN, D_OUT, R = (8, 2048, 256, 256, 4)
        rel_ids = jnp.arange(1, weight.shape[0] + 1, dtype=relation.dtype)
        masks = (relation[None] == rel_ids[:, None, None, None]).astype(x.dtype)
        h = jnp.einsum('rbnm,bmd->rbnd', masks, x)
        y = jnp.einsum('rbnd,rdo->bno', h, weight)
        return y + bias

    def _L3_gnn_ref(h, adj, W, a):
        import jax, jax.numpy as jnp
        import numpy as np
        B, N, IN_F, OUT_F = (32, 1024, 256, 256)
        ALPHA = 0.2
        NEG_INF = -9000000000000000.0
        Wh = jnp.einsum('bni,oi->bno', h, W)
        a1 = a[0, :OUT_F]
        a2 = a[0, OUT_F:]
        si = Wh @ a1
        sj = Wh @ a2
        e = jax.nn.leaky_relu(si[:, :, None] + sj[:, None, :], negative_slope=ALPHA)
        attention = jnp.where(adj > 0, e, NEG_INF)
        attention = jax.nn.softmax(attention, axis=-1)
        h_prime = jnp.einsum('bij,bjo->bio', attention, Wh)
        return jax.nn.elu(h_prime)

    x = _layernorm(x + _L0_gnn_ref(x, adj, L0_gnn_W, L0_gnn_a_src, L0_gnn_a_dst), axis=-1)
    x = _layernorm(x + _L1_gnn_ref(x, adj, L1_gnn_weight, L1_gnn_w_ih, L1_gnn_w_hh, L1_gnn_b_ih, L1_gnn_b_hh), axis=-1)
    x = _layernorm(x + _L2_gnn_ref(x, L2_gnn_adj, adj, L2_gnn_weight, L2_gnn_bias), axis=-1)
    x = _layernorm(x + _L3_gnn_ref(x, adj, L3_gnn_W, L3_gnn_a), axis=-1)
    return x


_drawn_inputs = setup_inputs


def setup_inputs(seed=0):
    import zlib

    import numpy as np

    out = dict(_drawn_inputs(seed))
    spreads = {}
    factors = {'L2_gnn_bias': 3.477}
    for name, (base, spread) in spreads.items():
        noise = np.random.default_rng([zlib.crc32(name.encode()), seed]).standard_normal(out[name].shape)
        drawn = base * np.exp(spread * noise) if base else spread * noise
        out[name] = jnp.asarray(drawn.astype(out[name].dtype))
    for name, factor in factors.items():
        out[name] = (out[name] * factor).astype(out[name].dtype)
    return out
```

```python
from contextlib import ExitStack

import concourse.bass as bass
from concourse import mybir

F32 = mybir.dt.float32
F32R = mybir.dt.float32r
I32 = mybir.dt.int32
ALU = mybir.AluOpType
ACT = mybir.ActivationFunctionType
AX_X = mybir.AxisListType.X

P = 128
MASKED = -1.0e30
EPS = 1.0e-5
ALPHA = 0.2


class Segment:

    def __init__(self, order, first, end):
        self.order, self.first, self.end = order, first, end


class Visit:

    def __init__(self, g, seg):
        self.g, self.seg = g, seg


SLOTS = {"light": 2, "misc": 2, "adj": 2, "pen": 2, "x": 2, "xt": 1, "wh": 2, "t": 2, "pt": 2,
         "hn": 1, "ex": 1, "y": 2, "x2s": 1, "h1": 1, "mt": 1, "mr": 1, "hr": 1, "adjt": 1, "x3": 1,
         "adjg": 1, "nodes": 1, "agg": 1, "adjf": 1, "out": 1}
TAKES = {
    "pre_load": ("adj", "x", "pen"), "post_load": ("adj", "pen", "adjf"),
    "att_xt": ("light", "xt"), "att_wh": ("light",), "att_scores": ("light",),
    "att_pt": ("light",), "att_pv": ("light", "hn"), "att_exp": ("ex",), "att_res": ("y",),
    "rel_adjt": ("light", "adjt"), "rel_split": ("x2s",), "rel_mask": ("mt",),
    "rel_h1": ("light", "h1"), "rel_y1": ("light", "y"),
    "rel_hr": ("light", "mr", "hr"), "rel_yr": ("light",),
    "gru_load": ("adjg",), "gru_nodes0": ("nodes",), "gru_turn0": ("misc",),
    "gru_agg": ("misc",), "gru_turn": ("misc",), "gru_fin": ("misc", "y"),
}


def takes(step):
    name, _, args = step
    out = list(TAKES.get(name, ()))
    if name == "att_wh" and args[2] == 0:
        out.append("wh")
    if name == "att_scores" and (args[0] == "pre" or args[2] == 0):
        out.append("t")
    if name == "att_pt" :
        out.append("pt")
    if name == "gru_turn" and args[2] == 0:
        out.append("nodes")
    if name == "gru_agg" and args[2] == 0:
        out.append("agg")
    if name == "rel_norm":
        out.append("x3")
    if name == "att_norm" and args[0] == "post":
        out.append("out")
    return out


def attention_steps(kind, u, off):
    k = (kind, u)
    q_steps = (0, 1)
    out = [("att_xt", off, k)]
    out += [("att_wh", off, k + (q,)) for q in q_steps]
    out += [("att_scores", off, k + (q,)) for q in (q_steps if kind == "pre" else (0,))]
    out += [("att_soft", off, k), ("att_prob", off, k)]
    out += [("att_pt", off, k + (q,)) for q in (q_steps if kind == "pre" else (0,))]
    out += [("att_pv", off, k), ("att_exp", off, k), ("att_res", off, k), ("att_norm", off, k)]
    return out


def pre_steps(u, off):
    return [("pre_load", off, (u,))] + attention_steps("pre", u, off)


def post_steps(u, off):
    out = [("post_load", off, (u,)), ("rel_adjt", off, (u,)), ("rel_split", off, (u,)),
           ("rel_mask", off, (u,)), ("rel_h1", off, (u,)), ("rel_y1", off, (u,))]
    for r in (2, 3, 4):
        out += [("rel_hr", off, (u, r)), ("rel_yr", off, (u, r))]
    return out + [("rel_stats", off, (u,)), ("rel_norm", off, (u,))] + attention_steps("post", u, off)


def gate_steps(b, l, off, mid):
    out = []
    for c in range(2):
        out += [("gru_hn", off, (b, l, c)), ("gru_rzh", off, (b, l, c)), ("gru_r", off, (b, l, c)),
                ("gru_z", off, (b, l, c)), ("gru_in", off, (b, l, c))]
        if c == 0:
            out += mid
    return out


def init_steps(b, off):
    return [("gru_load", off, (b,)), ("gru_turn0", off, (b, 0)), ("gru_turn0", off, (b, 1)),
            ("gru_nodes0", off, (b,))]


def layer_end(b, l, off):
    if l < 2:
        return [("gru_split", off, (b, l))] + [("gru_turn", off, (b, l, hf)) for hf in range(2)]
    return [s for hf in range(2) for s in (("gru_fin", off, (b, hf)), ("gru_norm", off, (b, hf)))]


def gru_steps(first_mid, last_mid):
    out = []
    for l in range(3):
        for b in range(2):
            mid = layer_end(1, l - 1, 0) if b == 0 and l else layer_end(0, l, 0) if b else first_mid
            if (l, b) == (2, 1):
                mid = mid + last_mid
            out += [("gru_agg", 0, (b, l, 0)), ("gru_agg", 0, (b, l, 1))] + gate_steps(b, l, 0, mid)
    return out


def plain_order():
    out = []
    for u in range(4):
        out += pre_steps(u, 0)
    out += init_steps(0, 0) + gru_steps(init_steps(1, 0), []) + layer_end(1, 2, 0)
    for u in range(4):
        out += post_steps(u, 0)
    return out


def make_segments(groups):
    one = plain_order()
    return [Segment(one, 0, 1), Segment(one, 1, groups)]


def number_uses(segments):
    before = {r: 0 for r in SLOTS}
    for seg in segments:
        seg.uses, seg.takers = {}, {r: [] for r in SLOTS}
        count = {r: 0 for r in SLOTS}
        for s in seg.order:
            for r in takes(s):
                seg.uses[(r,) + s] = count[r]
                seg.takers[r].append(s)
                count[r] += 1
        seg.before, seg.per = dict(before), count
        for r in SLOTS:
            assert count[r] % SLOTS[r] == 0 and before[r] % SLOTS[r] == 0, r
            before[r] += count[r] * (seg.end - seg.first)


def bass_gnn_stack(nc, x, adj, L0_gnn_W, L0_gnn_a_src, L0_gnn_a_dst, L1_gnn_weight, L1_gnn_w_ih,
                   L1_gnn_w_hh, L1_gnn_b_ih, L1_gnn_b_hh, L2_gnn_adj, L2_gnn_weight, L2_gnn_bias,
                   L3_gnn_W, L3_gnn_a, out):
    B, N, D = x.shape
    R = L2_gnn_weight.shape[0]
    H0, F0 = L0_gnn_a_src.shape
    C = D // P
    G3 = 3 * D
    NL = L1_gnn_weight.shape[0]
    GROUPS = B // 8
    assert N == P and C == 2 and B % 8 == 0 and GROUPS >= 3 and R == 4 and NL == 3
    segments = make_segments(GROUPS)
    number_uses(segments)

    with ExitStack() as ctx:
        def sb(name, shape, dt=F32):
            return ctx.enter_context(nc.sbuf_tensor(name, shape, dt))

        def sem(name):
            return ctx.enter_context(nc.semaphore(name))

        psum = ctx.enter_context(nc.psum_tensor("psum", [P, 8, 512], F32))

        ident = sb("ident", [P, P])
        whh_h, whh_l = sb("whh_h", [P, C, G3], F32R), sb("whh_l", [P, C, G3], F32R)
        wc_h, wc_l = sb("wc_h", [P, NL, C, G3], F32R), sb("wc_l", [P, NL, C, G3], F32R)
        w0_h, w0_l = sb("w0_h", [P, C, D + 2 * H0], F32R), sb("w0_l", [P, C, D + 2 * H0], F32R)
        w3_h, w3_l = sb("w3_h", [P, C, D + 2], F32R), sb("w3_l", [P, C, D + 2], F32R)
        wr1_h, wr1_l = sb("wr1_h", [P, C, D], F32R), sb("wr1_l", [P, C, D], F32R)
        wrs = sb("wrs", [P, R - 1, C, D])
        bias_rel = sb("bias_rel", [P, D])
        bias_rz = sb("bias_rz", [P, 4])
        bias_hn = sb("bias_hn", [P, 2])
        bias_in = sb("bias_in", [P, 2])
        mhalf = sb("mhalf", [P, 2])

        with ExitStack() as early:
            def tmp(name, shape, dt=F32):
                return early.enter_context(nc.sbuf_tensor(name, shape, dt))

            hh_raw, ih_raw = tmp("hh_raw", [P, 6, D]), tmp("ih_raw", [P, 6, D])
            wl_raw = tmp("wl_raw", [P, NL, C, D])
            w0_raw, w3_raw, wr1_raw = tmp("w0_raw", [P, C, D]), tmp("w3_raw", [P, C, D]), tmp("wr1_raw", [P, C, D])
            a_src, a_dst, a3 = tmp("a_src", [P, D]), tmp("a_dst", [P, D]), tmp("a3", [P, 2 * D])
            bi, bh = tmp("bi", [P, 6]), tmp("bh", [P, 6])
            ihT = tmp("ihT", [P, C, G3])
            stage = tmp("stage", [P, C, G3])
            wlT = tmp("wlT", [P, C, D])
            aug0, aug3 = tmp("aug0", [P, C, D + 2 * H0]), tmp("aug3", [P, C, D + 2])
            prod = tmp("prod", [P, C, D])
            s_w = sem("weights_loaded")
            s_wl = sem("layer_weights_loaded")
            s_id0, s_id = sem("ident_zeroed"), sem("ident_ready")
            s_t, s_c = sem("setup_psum_ready"), sem("setup_dve_done")
            block = early.enter_context(nc.Block())
            W_LOADS = 14

            @block.sync
            def _(sp):
                with nc.allow_non_contiguous_dma(reason="a few bias columns and broadcast rows, once"):
                    for dst, src in (
                        (hh_raw[:], L1_gnn_w_hh.rearrange("(m p) d -> p m d", p=P)),
                        (ih_raw[:], L1_gnn_w_ih.rearrange("(m p) d -> p m d", p=P)),
                        (w3_raw[:], L3_gnn_W.rearrange("(o p) i -> p o i", p=P)),
                        (w0_raw[:], L0_gnn_W.rearrange("(c p) o -> p c o", p=P)),
                        (wl_raw[:], L1_gnn_weight.rearrange("l (c p) e -> p l c e", p=P)),
                        (wr1_raw[:], L2_gnn_weight[0].rearrange("(c p) o -> p c o", p=P)),
                        (wrs[:], L2_gnn_weight[1:R].rearrange("r (c p) o -> p r c o", p=P)),
                        (a_src[:], L0_gnn_a_src.rearrange("(a h) f -> a (h f)", a=1).broadcast_to([P, D])),
                        (a_dst[:], L0_gnn_a_dst.rearrange("(a h) f -> a (h f)", a=1).broadcast_to([P, D])),
                        (a3[:], L3_gnn_a.broadcast_to([P, 2 * D])),
                        (bias_rel[:], L2_gnn_bias.rearrange("(a d) -> a d", a=1).broadcast_to([P, D])),
                        (bi[:], L1_gnn_b_ih.rearrange("(m p) -> p m", p=P)),
                        (bh[:], L1_gnn_b_hh.rearrange("(m p) -> p m", p=P)),
                        (mhalf[:, 0:1], L2_gnn_adj.rearrange("(a d) -> a d", a=1).broadcast_to([P, 1])),
                    ):
                        sp.dma_start(dst, src).then_inc(s_w, 16)

            @block.gpsimd
            def _(pool):
                nc.gpsimd.memset(ident[:], 0.0).then_inc(s_id0, 1)
                pool.wait_ge(s_id0, 1)
                nc.gpsimd.affine_select(out=ident[:], in_=ident[:], compare_op=ALU.not_equal, fill=1.0,
                                        base=0, pattern=[[-1, P]], channel_multiplier=1).then_inc(s_id, 1)

            @block.tensor
            def _(pe):
                pe.wait_ge(s_w, 16 * W_LOADS)
                pe.wait_ge(s_id, 1)

                def turn(bank, raw, rows):
                    for c in range(C):
                        flat = psum[:, bank + 2 * c:bank + 2 * c + 2, :].rearrange("p a n -> p (a n)")
                        for m in range(rows):
                            last = nc.tensor.transpose(flat[:, m * P:(m + 1) * P], raw[:, m, c * P:(c + 1) * P], ident[:])
                    last.then_inc(s_t, 1)

                turn(0, hh_raw, 6)
                turn(4, ih_raw, 6)
                pe.wait_ge(s_c, 1)
                turn(0, w3_raw, 2)
                for l in range(NL):
                    pe.wait_ge(s_c, 2 + 2 * l)
                    turn(4, wl_raw[:, l], C)
                    pe.wait_ge(s_c, 3 + 2 * l)
                    for c in range(C):
                        for n0, n1 in ((0, 512), (512, G3)):
                            for e in range(C):
                                last = nc.tensor.matmul(psum[:, 4 + 2 * c + n0 // 512, 0:n1 - n0],
                                                        wlT[:, e, c * P:(c + 1) * P], ihT[:, e, n0:n1],
                                                        start=(e == 0), stop=(e == C - 1))
                    last.then_inc(s_t, 1)

            @block.vector
            def _(dve):
                chain = [0]

                def done(ins):
                    chain[0] += 1
                    ins.then_inc(s_wl, 1)
                    dve.wait_ge(s_wl, chain[0])

                def banks(bank, n):
                    return psum[:, bank:bank + 4, :].rearrange("p (c a) n -> p c (a n)", c=C)[:, :, 0:n]

                def split(hi, lo, src):
                    done(nc.vector.tensor_copy(hi, src))
                    done(nc.vector.tensor_tensor(lo, src, hi.bitcast(F32), ALU.subtract))

                dve.wait_ge(s_w, 16 * W_LOADS)
                done(nc.vector.memset(mhalf[:], -0.5))
                dve.wait_ge(s_t, 1)
                done(nc.vector.tensor_copy(stage[:, :, 0:2 * D], banks(0, 2 * D)))
                done(nc.vector.tensor_scalar(stage[:, :, 2 * D:G3], banks(0, G3)[:, :, 2 * D:G3], 0.5, None, ALU.mult))
                nc.vector.memset(prod[:], 0.0).then_inc(s_c, 1)
                split(whh_h[:], whh_l[:], stage[:])
                dve.wait_ge(s_t, 2)
                done(nc.vector.tensor_copy(ihT[:], banks(4, G3)))
                dve.wait_ge(s_t, 3)
                done(nc.vector.tensor_copy(aug3[:, :, 0:D], banks(0, D)))
                dve.wait_ge(s_c, 1)
                nc.vector.memset(bias_rz[:], 0.0).then_inc(s_c, 1)
                for l in range(NL):
                    dve.wait_ge(s_t, 4 + 2 * l)
                    done(nc.vector.tensor_copy(wlT[:], banks(4, D)))
                    nc.vector.tensor_copy(stage[:, 0, 0:1], wlT[:, 0, 0:1]).then_inc(s_c, 1)
                    dve.wait_ge(s_t, 5 + 2 * l)
                    for hi, lo in ((wc_h[:, l], wc_l[:, l]),):
                        done(nc.vector.tensor_copy(hi, banks(4, G3)))
                        done(nc.vector.tensor_tensor(lo, banks(4, G3), hi.bitcast(F32), ALU.subtract))
                    nc.vector.tensor_copy(stage[:, 0, 1:2], wlT[:, 0, 0:1]).then_inc(s_c, 1)
                done(nc.vector.tensor_copy(aug0[:, :, 0:D], w0_raw[:]))
                for k, a in enumerate((a_src, a_dst)):
                    done(nc.vector.tensor_tensor(prod[:], w0_raw[:], a[:].unsqueeze(1).to_broadcast([P, C, D]), ALU.mult))
                    for c in range(C):
                        done(nc.vector.tensor_reduce(aug0[:, c, D + k * H0:D + (k + 1) * H0],
                                                     prod[:, c].rearrange("p (h f) -> p h f", h=H0), AX_X, ALU.add))
                for k in range(2):
                    done(nc.vector.tensor_tensor(prod[:], aug3[:, :, 0:D],
                                                 a3[:, k * D:(k + 1) * D].unsqueeze(1).to_broadcast([P, C, D]), ALU.mult))
                    done(nc.vector.tensor_reduce(aug3[:, :, D + k:D + k + 1], prod[:], AX_X, ALU.add))
                split(w0_h[:], w0_l[:], aug0[:])
                split(w3_h[:], w3_l[:], aug3[:])
                split(wr1_h[:], wr1_l[:], wr1_raw[:])
                done(nc.vector.tensor_tensor(bias_rz[:], bi[:, 0:4], bh[:, 0:4], ALU.add))
                done(nc.vector.tensor_scalar(bias_rz[:], bias_rz[:], 0.5, None, ALU.mult))
                done(nc.vector.tensor_scalar(bias_hn[:], bh[:, 4:6], 0.5, None, ALU.mult))
                done(nc.vector.tensor_copy(bias_in[:], bi[:, 4:6]))

        adj_i = [sb(f"adj_i{i}", [P, 2, P], I32) for i in range(2)]
        pen = [sb(f"pen{i}", [P, 2, P]) for i in range(2)]
        x_in = [sb(f"x_in{i}", [P, 2, D]) for i in range(2)]
        xt_h, xt_l = sb("xt_h", [P, C, 2 * P], F32R), sb("xt_l", [P, C, 2 * P], F32R)
        wh = [sb(f"wh{i}", [P, 2, D + 2 * H0]) for i in range(2)]
        t_sc = [sb(f"t_sc{i}", [P, 4, P]) for i in range(2)]
        pt = [sb(f"pt{i}", [P, 4, P]) for i in range(2)]
        hn_t, ex_t = sb("hn_t", [P, 2 * D]), sb("ex_t", [P, 2 * D])
        y_t = [sb(f"y_t{i}", [P, 2, D]) for i in range(2)]
        stats = [sb(f"stats{i}", [P, 2, 6]) for i in range(2)]
        moments = [sb(f"moments{i}", [P, 2, 2]) for i in range(2)]
        rstd = [sb(f"rstd{i}", [P, 2]) for i in range(2)]
        x3 = sb("x3", [P, 2, D])
        out_t = sb("out_t", [P, 2, D])
        x2_h, x2_l = sb("x2_h", [P, 2, D], F32R), sb("x2_l", [P, 2, D], F32R)
        adj_f, adj_t = sb("adj_f", [P, 2, P]), sb("adj_t", [P, 2 * P])
        mt1, mtr = sb("mt1", [P, 2, P], F32R), sb("mtr", [P, 2, P], F32R)
        h1_h, h1_l = sb("h1_h", [P, C, 2 * P], F32R), sb("h1_l", [P, C, 2 * P], F32R)
        hr_t = sb("hr_t", [P, C, 2 * P])
        adj_g = sb("adj_g", [P, 4, P], I32)
        edges = [sb(f"edges{b}", [P, 4, P], F32R) for b in range(2)]
        x1n = [sb(f"x1n{b}", [P, 4, D]) for b in range(2)]
        x1r = [sb(f"x1r{b}", [P, 4, D]) for b in range(2)]
        x2 = [sb(f"x2{b}", [P, 4, D]) for b in range(2)]
        ht = [sb(f"ht{b}", [P, C, 4 * P]) for b in range(2)]
        ht_h = [sb(f"ht_h{b}", [P, C, 4 * P], F32R) for b in range(2)]
        ht_l = [sb(f"ht_l{b}", [P, C, 4 * P], F32R) for b in range(2)]
        hn_h, hn_l = sb("hn_h", [P, 4, D], F32R), sb("hn_l", [P, 4, D], F32R)
        ag_h, ag_l = sb("ag_h", [P, C, 4 * P], F32R), sb("ag_l", [P, C, 4 * P], F32R)
        g_hn = [sb(f"g_hn{c}", [P, 512]) for c in range(2)]
        g_r = [sb(f"g_r{c}", [P, 512]) for c in range(2)]
        g_z = [sb(f"g_z{c}", [P, 512]) for c in range(2)]
        g_n = [sb(f"g_n{c}", [P, 512]) for c in range(2)]
        g_d = sb("g_d", [P, 512])

        class Layer:

            def __init__(self, name, heads, w_h, w_l):
                self.heads, self.f, self.cols, self.qs = heads, D // heads, D + 2 * heads, 2 if heads > 1 else 1
                self.w_h, self.w_l = w_h, w_l
                self.top, self.peak, self.neg, self.sum, self.inv = (
                    sb(f"{name}_{what}", [P, 2, heads]) for what in ("top", "peak", "neg", "sum", "inv"))
                self.xt_psum = sem("%s_xt_psum" % name)
                self.xt_high = sem("%s_xt_high" % name)
                self.xt_low = sem("%s_xt_low" % name)
                self.wh_psum = sem("%s_wh_psum" % name)
                self.wh_ready = sem("%s_wh_ready" % name)
                self.sc_psum = sem("%s_sc_psum" % name)
                self.masked = sem("%s_masked" % name)
                self.top_ready = sem("%s_top_ready" % name)
                self.peak_ready = sem("%s_peak_ready" % name)
                self.neg_ready = sem("%s_neg_ready" % name)
                self.shifted = sem("%s_shifted" % name)
                self.leaky = sem("%s_leaky" % name)
                self.prob = sem("%s_prob" % name)
                self.pt_psum = sem("%s_pt_psum" % name)
                self.pt_ready = sem("%s_pt_ready" % name)
                self.pv_psum = sem("%s_pv_psum" % name)
                self.inv_ready = sem("%s_inv_ready" % name)
                self.hn_ready = sem("%s_hn_ready" % name)
                self.ex_ready = sem("%s_ex_ready" % name)
                self.min_ready = sem("%s_min_ready" % name)
                self.y_ready = sem("%s_y_ready" % name)
                self.pen_ready = sem("%s_pen_ready" % name)

        LAY = {"pre": Layer("first", H0, w0_h, w0_l), "post": Layer("last", 1, w3_h, w3_l)}

        s_x = [sem(f"x_loaded{i}") for i in range(2)]
        s_adj = [sem(f"adj_loaded{i}") for i in range(2)]
        s_adjg, s_edges, s_adjf = sem("adjg_loaded"), sem("edges_ready"), sem("adjf_ready")
        s_stats, s_mom, s_eps, s_rstd = ([sem(f"{n}{i}") for i in range(2)] for n in ("stats_ready", "moments_ready", "eps_added", "rstd_ready"))
        s_x1n = [sem(f"x1n_ready{b}") for b in range(2)]
        s_x2 = [sem(f"x2_ready{b}") for b in range(2)]
        s_x1r = sem("x1r_ready")
        s_adjt_ps, s_adjt, s_mt1, s_mtr = sem("adjt_psum"), sem("adjt_ready"), sem("mask1_ready"), sem("maskr_ready")
        s_x2h, s_x2l, s_x2b = sem("x2_high"), sem("x2_low"), sem("x2_biased")
        s_h1_ps, s_h1h, s_h1l = sem("h1_psum"), sem("h1_high"), sem("h1_low")
        s_hr_ps, s_hr, s_y_ps, s_rel_y = sem("hr_psum"), sem("hr_ready"), sem("rel_psum"), sem("rel_y_ready")
        s_x3, s_outn, s_out = sem("x3_ready"), sem("out_ready"), sem("out_stored")
        s_turn_ps, s_ht0, s_ht_h, s_ht_l = sem("turned_psum"), sem("ht_ready"), sem("ht_high"), sem("ht_low")
        s_nd_ps, s_nd_h, s_nd_l = sem("nodes_psum"), sem("nodes_high"), sem("nodes_low")
        s_ag_ps, s_ag_h, s_ag_l = sem("agg_psum"), sem("agg_high"), sem("agg_low")
        s_ph, s_pr, s_pz, s_pi = sem("hn_psum"), sem("r_psum"), sem("z_psum"), sem("in_psum")
        s_hnb, s_r, s_z, s_t1, s_t2, s_n = (sem(n) for n in ("hn_biased", "r_ready", "z_ready", "rh_ready", "cand_sum", "n_ready"))
        s_d, s_e, s_hnew = sem("diff_ready"), sem("zdiff_ready"), sem("h_new")
        s_fin_ps, s_fin_y = sem("final_psum"), sem("final_y")
        s_half = sem("exponent_ready")
        s_stood = sem("waits_stood")

        block = ctx.enter_context(nc.Block())
        LIGHT, MISC = psum[:, 0:2, :], psum[:, 2:4, :]
        HN_PS, R_PS, Z_PS, IN_PS = (psum[:, k, :] for k in range(4, 8))

        def nth(v, step, per, k):
            return v.g * per + (step[1] * per + k + 1)

        def chunk(v, step, b, l, c):
            return nth(v, step, 12, 4 * l + 2 * b + c)

        def ring(v, step, resource):
            k, n = v.seg.uses[(resource,) + step], SLOTS[resource]
            per = v.seg.per[resource] // n
            return k % n, v.g * per + (v.seg.before[resource] // n + k // n - v.seg.first * per)

        def after(eng, semaphore, value):
            if not isinstance(value, int) or value > 0:
                eng.wait_ge(semaphore, value)

        def stand(eng):
            eng.sem_inc(s_stood, 1)

        def last_read(resource, v, step):
            name, _, a = step
            if name.startswith("att"):
                L, u = LAY[a[0]], a[1]
                qth = nth(v, step, 4 * L.qs, L.qs * u + (a[2] if len(a) > 2 else 0))
                uth = nth(v, step, 4, u)
                b = u // 2
                return {
                    ("light", "att_xt"): (L.xt_low, uth), ("light", "att_scores"): (L.masked, qth),
                    ("light", "att_pt"): (L.pt_ready, qth), ("light", "att_pv"): (L.hn_ready, uth),
                    ("light", "att_wh"): (L.wh_ready, nth(v, step, 8, 2 * u + (a[2] if len(a) > 2 else 0))),
                    ("xt", "att_xt"): (L.wh_psum, nth(v, step, 8, 2 * u + 1)),
                    ("wh", "att_wh"): (L.pv_psum, uth), ("t", "att_scores"): (L.pt_psum, qth),
                    ("pt", "att_pt"): (L.pv_psum, uth), ("hn", "att_pv"): (L.y_ready, uth),
                    ("ex", "att_exp"): (L.min_ready, uth),
                    ("y", "att_res"): (s_x1n[b], nth(v, step, 2, u % 2)) if a[0] == "pre" else (s_outn, uth),
                    ("out", "att_norm"): (s_out, uth * 16),
                }[resource, name]
            if name == "pre_load":
                return {"adj": (LAY["pre"].pen_ready, nth(v, step, 4, a[0])), "x": (LAY["pre"].min_ready, nth(v, step, 4, a[0])),
                        "pen": (LAY["pre"].masked, nth(v, step, 8, 2 * a[0] + 1))}[resource]
            if name == "post_load":
                return {"adj": (s_adjf, nth(v, step, 4, a[0])), "adjf": (s_adjt_ps, nth(v, step, 4, a[0])),
                        "pen": (LAY["post"].masked, nth(v, step, 4, a[0]))}[resource]
            if name.startswith("rel"):
                u = a[0]
                r = a[1] if len(a) > 1 else 1
                return {
                    ("light", "rel_adjt"): (s_adjt, nth(v, step, 4, u)), ("adjt", "rel_adjt"): (s_mtr, nth(v, step, 12, 3 * u + 2)),
                    ("x2s", "rel_split"): (s_hr_ps, nth(v, step, 12, 3 * u + 2)), ("mt", "rel_mask"): (s_h1_ps, nth(v, step, 4, u)),
                    ("light", "rel_h1"): (s_h1l, nth(v, step, 4, u)), ("h1", "rel_h1"): (s_y_ps, nth(v, step, 16, 4 * u)),
                    ("light", "rel_y1"): (s_rel_y, nth(v, step, 16, 4 * u)), ("y", "rel_y1"): (s_x3, nth(v, step, 4, u)),
                    ("light", "rel_hr"): (s_hr, nth(v, step, 12, 3 * u + r - 2)), ("mr", "rel_hr"): (s_hr_ps, nth(v, step, 12, 3 * u + r - 2)),
                    ("hr", "rel_hr"): (s_y_ps, nth(v, step, 16, 4 * u + r - 1)), ("light", "rel_yr"): (s_rel_y, nth(v, step, 16, 4 * u + r - 1)),
                    ("x3", "rel_norm"): (LAY["post"].min_ready, nth(v, step, 4, u)),
                }[resource, name]
            b = a[0]
            if name == "gru_load":
                return s_edges, nth(v, step, 2, b)
            if name == "gru_turn0":
                return s_ht0, nth(v, step, 4, 2 * b + a[1])
            if name == "gru_nodes0":
                return s_ag_ps, nth(v, step, 12, 2 * b + 1)
            if name == "gru_agg":
                return (s_ag_l, nth(v, step, 12, 4 * a[1] + 2 * b + a[2])) if resource == "misc" else (s_pi, chunk(v, step, b, a[1], 1))
            if name == "gru_turn":
                return (s_nd_l, nth(v, step, 12, 4 * (a[1] + 1) + 2 * b + a[2])) if resource == "misc" else \
                    (s_ag_ps, nth(v, step, 12, 4 * (a[1] + 1) + 2 * b + 1))
            assert name == "gru_fin"
            return (s_fin_y, nth(v, step, 4, 2 * b + a[1])) if resource == "misc" else (s_x2[b], nth(v, step, 2, a[1]))

        def take(eng, v, step, resource):
            seg, n = v.seg, SLOTS[resource]
            k = seg.uses[(resource,) + step]
            takers = seg.takers[resource]
            if k >= n:
                eng.wait_ge(*last_read(resource, v, takers[k - n]))
                return k % n
            earlier = [s for s in segments[:segments.index(seg)] if s.takers[resource]]
            at_end = None
            if earlier:
                tail = earlier[-1]
                at_end = last_read(resource, Visit(tail.end - 1, tail), tail.takers[resource][k - n])
                at_end = (at_end[0], at_end[1])
            if seg.end - seg.first > 1:
                wrapped = takers[k - n]
                eng.wait_ge(*last_read(resource, Visit(v.g + -1, seg), wrapped))
                first = last_read(resource, Visit(seg.first - 1, seg), wrapped)
                if at_end and first[0] is at_end[0] and first[1] == at_end[1]:
                    at_end = None
            if at_end:
                eng.wait_ge(*at_end)
            return k % n

        def walk(eng, shares):
            for seg in segments:
                if seg.end - seg.first == 1:
                    for step in seg.order:
                        if step[0] in shares:
                            shares[step[0]](Visit(seg.first, seg), step, *step[2])
                else:
                    with eng.Fori(seg.first, seg.end) as g:
                        for step in seg.order:
                            if step[0] in shares:
                                shares[step[0]](Visit(g, seg), step, *step[2])

        def slot(v, step, name, args, resource):
            return v.seg.uses[(resource, name, step[1], args)] % SLOTS[resource]

        def t_slots(v, step, kind, u):
            return [(slot(v, step, "att_scores", (kind, u, q if kind == "pre" else 0), "t"), h if kind == "pre" else q, q, h)
                    for q in range(2) for h in range(LAY[kind].heads)]

        @block.sync
        def _(sp):
            def graphs(v, step, first, n):
                at = v.g * 8 + (step[1] * 8 + first)
                return slice(at, at + n) if isinstance(at, int) else bass.ds(at, n)

            def load_adj(v, step, u):
                i = take(sp, v, step, "adj")
                sp.dma_start(adj_i[i][:], adj[graphs(v, step, 2 * u, 2)].rearrange("g n m -> n g m")).then_inc(s_adj[i], 16)

            def pre_load(v, step, u):
                load_adj(v, step, u)
                i = take(sp, v, step, "x")
                sp.dma_start(x_in[i][:], x[graphs(v, step, 2 * u, 2)].rearrange("g n d -> n g d")).then_inc(s_x[i], 16)

            def gru_load(v, step, b):
                take(sp, v, step, "adjg")
                sp.dma_start(adj_g[:], adj[graphs(v, step, 4 * b, 4)].rearrange("g n m -> n g m")).then_inc(s_adjg, 16)

            def att_norm(v, step, kind, u):
                if kind == "post":
                    sp.wait_ge(s_outn, nth(v, step, 4, u))
                    sp.dma_start(out[graphs(v, step, 2 * u, 2)].rearrange("g n d -> n g d"), out_t[:]).then_inc(s_out, 16)

            walk(sp, {"pre_load": pre_load, "post_load": load_adj, "gru_load": gru_load, "att_norm": att_norm})
            sp.wait_ge(s_out, 16 * 4 * GROUPS)

        @block.tensor
        def _(pe):
            mm, turn = nc.tensor.matmul, nc.tensor.transpose

            def three(dst, pairs):
                n = 3 * len(pairs)
                terms = [t for (sh, sl), (mh, ml) in pairs for t in ((sh, mh), (sh, ml), (sl, mh))]
                for k, (s, m) in enumerate(terms):
                    last = mm(dst, s, m, start=(k == 0), stop=(k == n - 1))
                return last

            def att_xt(v, step, kind, u):
                L, i = LAY[kind], take(pe, v, step, "light")
                if kind == "pre":
                    xi, uses = ring(v, ("pre_load", step[1], (u,)), "x")
                    pe.wait_ge(s_x[xi], uses * 16 + 16)
                    src = x_in[xi]
                else:
                    pe.wait_ge(s_x3, nth(v, step, 4, u))
                    src = x3
                for c in range(C):
                    for q in range(2):
                        last = turn(LIGHT[:, i, (2 * c + q) * P:(2 * c + q + 1) * P], src[:, q, c * P:(c + 1) * P], ident[:])
                last.then_inc(L.xt_psum, 1)

            def att_wh(v, step, kind, u, q):
                L, i = LAY[kind], take(pe, v, step, "light")
                if q == 0:
                    pe.wait_ge(L.xt_high, nth(v, step, 4, u))
                    pe.wait_ge(L.xt_low, nth(v, step, 4, u))
                rows = slice(q * P, (q + 1) * P)
                three(LIGHT[:, i, 0:L.cols], [((xt_h[:, c, rows], xt_l[:, c, rows]), (L.w_h[:, c, :], L.w_l[:, c, :]))
                                              for c in range(C)]).then_inc(L.wh_psum, 1)

            def att_scores(v, step, kind, u, q):
                L, i = LAY[kind], take(pe, v, step, "light")
                w = slot(v, step, "att_wh", (kind, u, 0), "wh")
                pe.wait_ge(L.wh_ready, nth(v, step, 8, 2 * u + (q if kind == "pre" else 1)))
                cells = [(q, h) for h in range(L.heads)] if kind == "pre" else [(0, 0), (1, 0)]
                for k, (g, h) in enumerate(cells):
                    col = D + L.heads + h
                    last = turn(LIGHT[:, i, k * P:(k + 1) * P], wh[w][:, g, col:col + 1].to_broadcast([P, P]), ident[:])
                last.then_inc(L.sc_psum, 1)

            def att_pt(v, step, kind, u, q):
                L, i = LAY[kind], take(pe, v, step, "light")
                cells = [s for s in t_slots(v, step, kind, u) if kind == "post" or s[2] == q]
                pe.wait_ge(L.prob, nth(v, step, 8 * L.heads, 2 * L.heads * u + (L.heads * (q + 1) if kind == "pre" else 2) - 1))
                for k, (ti, at, _, _) in enumerate(cells):
                    last = turn(LIGHT[:, i, k * P:(k + 1) * P], t_sc[ti][:, at, :], ident[:])
                last.then_inc(L.pt_psum, 1)

            def att_pv(v, step, kind, u):
                L, i = LAY[kind], take(pe, v, step, "light")
                w = slot(v, step, "att_wh", (kind, u, 0), "wh")
                pe.wait_ge(L.pt_ready, nth(v, step, 4 * L.qs, L.qs * u + L.qs - 1))
                for q in range(2):
                    for h in range(L.heads):
                        pi = slot(v, step, "att_pt", (kind, u, q if kind == "pre" else 0), "pt")
                        at = (q * L.heads + h) * L.f
                        last = mm(LIGHT[:, i, at:at + L.f], pt[pi][:, h if kind == "pre" else q, :],
                                  wh[w][:, q, h * L.f:(h + 1) * L.f], start=True, stop=True)
                last.then_inc(L.pv_psum, 1)

            def rel_adjt(v, step, u):
                i = take(pe, v, step, "light")
                pe.wait_ge(s_adjf, nth(v, step, 4, u))
                for q in range(2):
                    last = turn(LIGHT[:, i, q * P:(q + 1) * P], adj_f[:, q, :], ident[:])
                last.then_inc(s_adjt_ps, 1)

            def neighbours(dst, mask):
                for c in range(C):
                    for q in range(2):
                        at = (2 * c + q) * P
                        mm(dst[:, at:at + P], x2_h[:, q, c * P:(c + 1) * P], mask[:, q, :], start=True, stop=False)
                        last = mm(dst[:, at:at + P], x2_l[:, q, c * P:(c + 1) * P], mask[:, q, :], start=False, stop=True)
                return last

            def rel_h1(v, step, u):
                i = take(pe, v, step, "light")
                pe.wait_ge(s_x2h, nth(v, step, 4, u))
                pe.wait_ge(s_x2l, nth(v, step, 4, u))
                pe.wait_ge(s_mt1, nth(v, step, 4, u))
                neighbours(LIGHT[:, i, :], mt1).then_inc(s_h1_ps, 1)

            def rel_y1(v, step, u):
                i = take(pe, v, step, "light")
                pe.wait_ge(s_h1h, nth(v, step, 4, u))
                pe.wait_ge(s_h1l, nth(v, step, 4, u))
                for q in range(2):
                    rows = slice(q * P, (q + 1) * P)
                    last = three(LIGHT[:, i, q * D:(q + 1) * D], [((h1_h[:, c, rows], h1_l[:, c, rows]), (wr1_h[:, c, :], wr1_l[:, c, :]))
                                                                  for c in range(C)])
                last.then_inc(s_y_ps, 1)

            def rel_hr(v, step, u, r):
                i = take(pe, v, step, "light")
                pe.wait_ge(s_mtr, nth(v, step, 12, 3 * u + r - 2))
                neighbours(LIGHT[:, i, :], mtr).then_inc(s_hr_ps, 1)

            def rel_yr(v, step, u, r):
                i = take(pe, v, step, "light")
                pe.wait_ge(s_hr, nth(v, step, 12, 3 * u + r - 2))
                for q in range(2):
                    for c in range(C):
                        last = mm(LIGHT[:, i, q * D:(q + 1) * D], hr_t[:, c, q * P:(q + 1) * P], wrs[:, r - 2, c, :],
                                  start=(c == 0), stop=(c == C - 1))
                last.then_inc(s_y_ps, 1)

            def gru_turn0(v, step, b, c):
                i = take(pe, v, step, "misc")
                pe.wait_ge(s_x1n[b], nth(v, step, 2, 1))
                for q in range(4):
                    last = turn(MISC[:, i, q * P:(q + 1) * P], x1n[b][:, q, c * P:(c + 1) * P], ident[:])
                last.then_inc(s_turn_ps, 1)

            def gru_agg(v, step, b, l, c):
                i = take(pe, v, step, "misc")
                pe.wait_ge(s_nd_h, nth(v, step, 12, 4 * l + 2 * b + 1))
                pe.wait_ge(s_nd_l, nth(v, step, 12, 4 * l + 2 * b + 1))
                if l == 0:
                    pe.wait_ge(s_edges, nth(v, step, 2, b))
                for q in range(4):
                    dst = MISC[:, i, q * P:(q + 1) * P]
                    mm(dst, hn_h[:, q, c * P:(c + 1) * P], edges[b][:, q, :], start=True, stop=False)
                    last = mm(dst, hn_l[:, q, c * P:(c + 1) * P], edges[b][:, q, :], start=False, stop=True)
                last.then_inc(s_ag_ps, 1)

            def gate_terms(rows, w_h, w_l, m_h, m_l):
                return [((w_h[:, k, rows], w_l[:, k, rows]), (m_h[:, k, :], m_l[:, k, :])) for k in range(C)]

            def rows_of(gate, c):
                return slice(gate * D + c * P, gate * D + (c + 1) * P)

            def accumulate(dst, terms, first, last_part):
                flat = [t for (sh, sl), (mh, ml) in terms for t in ((sh, mh), (sh, ml), (sl, mh))]
                for k, (s, m) in enumerate(flat):
                    last = mm(dst, s, m, start=(first and k == 0), stop=(last_part and k == len(flat) - 1))
                return last

            def gru_hn(v, step, b, l, c):
                pe.wait_ge(s_ht_h, nth(v, step, 6, 2 * l + b))
                pe.wait_ge(s_ht_l, nth(v, step, 6, 2 * l + b))
                after(pe, s_hnb, chunk(v, step, b, l, c) + -1)
                accumulate(HN_PS, gate_terms(rows_of(2, c), whh_h, whh_l, ht_h[b], ht_l[b]), True, True).then_inc(s_ph, 1)

            def gru_rzh(v, step, b, l, c):
                after(pe, s_r, chunk(v, step, b, l, c) + -1)
                accumulate(R_PS, gate_terms(rows_of(0, c), whh_h, whh_l, ht_h[b], ht_l[b]), True, False)
                after(pe, s_z, chunk(v, step, b, l, c) + -1)
                accumulate(Z_PS, gate_terms(rows_of(1, c), whh_h, whh_l, ht_h[b], ht_l[b]), True, False)

            def gru_r(v, step, b, l, c):
                if c == 0:
                    pe.wait_ge(s_ag_h, nth(v, step, 12, 4 * l + 2 * b + 1))
                    pe.wait_ge(s_ag_l, nth(v, step, 12, 4 * l + 2 * b + 1))
                accumulate(R_PS, gate_terms(rows_of(0, c), wc_h[:, l], wc_l[:, l], ag_h, ag_l), False, True).then_inc(s_pr, 1)

            def gru_z(v, step, b, l, c):
                accumulate(Z_PS, gate_terms(rows_of(1, c), wc_h[:, l], wc_l[:, l], ag_h, ag_l), False, True).then_inc(s_pz, 1)

            def gru_in(v, step, b, l, c):
                after(pe, s_t2, chunk(v, step, b, l, c) + -1)
                accumulate(IN_PS, gate_terms(rows_of(2, c), wc_h[:, l], wc_l[:, l], ag_h, ag_l), True, True).then_inc(s_pi, 1)

            def turn_back(v, step, b, hf, semaphore):
                i = take(pe, v, step, "misc")
                for q in range(2):
                    for c in range(C):
                        last = turn(MISC[:, i, q * D + c * P:q * D + (c + 1) * P],
                                    ht[b][:, c, (2 * hf + q) * P:(2 * hf + q + 1) * P], ident[:])
                last.then_inc(semaphore, 1)

            def gru_turn(v, step, b, l, hf):
                pe.wait_ge(s_hnew, chunk(v, step, b, l, 1))
                turn_back(v, step, b, hf, s_nd_ps)

            def gru_fin(v, step, b, hf):
                pe.wait_ge(s_hnew, chunk(v, step, b, NL - 1, 1))
                turn_back(v, step, b, hf, s_fin_ps)

            walk(pe, {"att_xt": att_xt, "att_wh": att_wh, "att_scores": att_scores, "att_pt": att_pt, "att_pv": att_pv,
                      "rel_adjt": rel_adjt, "rel_h1": rel_h1, "rel_y1": rel_y1, "rel_hr": rel_hr, "rel_yr": rel_yr,
                      "gru_turn0": gru_turn0, "gru_agg": gru_agg, "gru_hn": gru_hn, "gru_rzh": gru_rzh, "gru_r": gru_r,
                      "gru_z": gru_z, "gru_in": gru_in, "gru_turn": gru_turn, "gru_fin": gru_fin})

        @block.scalar
        def _(act):
            f = nc.scalar.activation

            def att_xt(v, step, kind, u):
                L, i = LAY[kind], slot(v, step, "att_xt", (kind, u), "light")
                take(act, v, step, "xt")
                act.wait_ge(L.xt_psum, nth(v, step, 4, u))
                f(xt_h[:].rearrange("p c n -> p (c n)"), LIGHT[:, i, :], ACT.Copy).then_inc(L.xt_high, 1)

            def att_wh(v, step, kind, u, q):
                L, i = LAY[kind], slot(v, step, "att_wh", (kind, u, q), "light")
                if q == 0:
                    take(act, v, step, "wh")
                w = slot(v, step, "att_wh", (kind, u, 0), "wh")
                act.wait_ge(L.wh_psum, nth(v, step, 8, 2 * u + q))
                f(wh[w][:, q, 0:L.cols], LIGHT[:, i, 0:L.cols], ACT.Copy).then_inc(L.wh_ready, 1)

            def att_scores(v, step, kind, u, q):
                L = LAY[kind]
                w = slot(v, step, "att_wh", (kind, u, 0), "wh")
                act.wait_ge(L.masked, nth(v, step, 4 * L.qs, L.qs * u + q))
                for ti, at, g, h in t_slots(v, step, kind, u):
                    if kind == "post" or g == q:
                        f(t_sc[ti][:, at, :], t_sc[ti][:, at, :], ACT.Identity, bias=wh[w][:, g, D + h:D + h + 1]).then_inc(L.shifted, 1)

            def att_prob(v, step, kind, u):
                L = LAY[kind]
                act.wait_ge(L.neg_ready, nth(v, step, 4, u))
                after(act, L.inv_ready, nth(v, step, 4, u) + -1)
                for ti, at, q, h in t_slots(v, step, kind, u):
                    if at == 0:
                        act.wait_ge(L.leaky, nth(v, step, 4 * L.qs, L.qs * u + (q if L.qs == 2 else 0)))
                    f(t_sc[ti][:, at, :], t_sc[ti][:, at, :], ACT.Exp, bias=L.neg[:, q, h:h + 1],
                      accum_out=L.sum[:, q, h:h + 1]).then_inc(L.prob, 1)

            def att_pt(v, step, kind, u, q):
                if kind == "pre" and q == 1:
                    return
                L, i = LAY[kind], slot(v, step, "att_pt", (kind, u, q), "light")
                pi = take(act, v, step, "pt")
                act.wait_ge(L.pt_psum, nth(v, step, 4 * L.qs, L.qs * u + q))
                n = L.heads if kind == "pre" else 2
                f(pt[pi][:, 0:n, :].rearrange("p h n -> p (h n)"), LIGHT[:, i, 0:n * P], ACT.Copy).then_inc(L.pt_ready, 1)

            def att_exp(v, step, kind, u):
                L = LAY[kind]
                take(act, v, step, "ex")
                act.wait_ge(L.hn_ready, nth(v, step, 4, u))
                f(ex_t[:], hn_t[:], ACT.Exp).then_inc(L.ex_ready, 1)

            def rel_adjt(v, step, u):
                i = slot(v, step, "rel_adjt", (u,), "light")
                take(act, v, step, "adjt")
                act.wait_ge(s_adjt_ps, nth(v, step, 4, u))
                f(adj_t[:], LIGHT[:, i, 0:2 * P], ACT.Copy).then_inc(s_adjt, 1)

            def rel_split(v, step, u):
                take(act, v, step, "x2s")
                b, at = u // 2, 2 * (u % 2)
                act.wait_ge(s_x2[b], nth(v, step, 2, u % 2))
                f(x2_h[:], x2[b][:, at:at + 2, :], ACT.Copy).then_inc(s_x2h, 1)

            def rel_h1(v, step, u):
                i = slot(v, step, "rel_h1", (u,), "light")
                take(act, v, step, "h1")
                act.wait_ge(s_h1_ps, nth(v, step, 4, u))
                f(h1_h[:].rearrange("p c n -> p (c n)"), LIGHT[:, i, :], ACT.Copy).then_inc(s_h1h, 1)

            def rel_hr(v, step, u, r):
                i = slot(v, step, "rel_hr", (u, r), "light")
                take(act, v, step, "hr")
                act.wait_ge(s_hr_ps, nth(v, step, 12, 3 * u + r - 2))
                f(hr_t[:].rearrange("p c n -> p (c n)"), LIGHT[:, i, :], ACT.Copy).then_inc(s_hr, 1)

            def gru_turn0(v, step, b, c):
                i = slot(v, step, "gru_turn0", (b, c), "misc")
                act.wait_ge(s_turn_ps, nth(v, step, 4, 2 * b + c))
                f(ht[b][:, c, :], MISC[:, i, :], ACT.Copy).then_inc(s_ht0, 1)

            def gru_agg(v, step, b, l, c):
                i = slot(v, step, "gru_agg", (b, l, c), "misc")
                if c == 0:
                    take(act, v, step, "agg")
                act.wait_ge(s_ag_ps, nth(v, step, 12, 4 * l + 2 * b + c))
                f(ag_h[:, c, :], MISC[:, i, :], ACT.Copy).then_inc(s_ag_h, 1)

            def gru_hn(v, step, b, l, c):
                act.wait_ge(s_ph, chunk(v, step, b, l, c))
                f(g_hn[c][:], HN_PS, ACT.Identity, bias=bias_hn[:, c:c + 1]).then_inc(s_hnb, 1)

            def gru_r(v, step, b, l, c):
                act.wait_ge(s_pr, chunk(v, step, b, l, c))
                f(g_r[c][:], R_PS, ACT.Tanh, bias=bias_rz[:, c:c + 1], scale=0.5).then_inc(s_r, 1)

            def gru_z(v, step, b, l, c):
                act.wait_ge(s_pz, chunk(v, step, b, l, c))
                f(g_z[c][:], Z_PS, ACT.Tanh, bias=bias_rz[:, 2 + c:3 + c], scale=0.5).then_inc(s_z, 1)

            def gru_in(v, step, b, l, c):
                act.wait_ge(s_t2, chunk(v, step, b, l, c))
                f(g_n[c][:], g_hn[c][:], ACT.Tanh, bias=bias_in[:, c:c + 1]).then_inc(s_n, 1)

            def gru_turn(v, step, b, l, hf):
                i = slot(v, step, "gru_turn", (b, l, hf), "misc")
                if hf == 0:
                    take(act, v, step, "nodes")
                act.wait_ge(s_nd_ps, nth(v, step, 8, 4 * l + 2 * b + hf))
                f(hn_h[:, 2 * hf:2 * hf + 2, :].rearrange("p q d -> p (q d)"), MISC[:, i, :], ACT.Copy).then_inc(s_nd_h, 1)

            walk(act, {"att_xt": att_xt, "att_wh": att_wh, "att_scores": att_scores, "att_prob": att_prob, "att_pt": att_pt, "att_exp": att_exp,
                       "rel_adjt": rel_adjt, "rel_split": rel_split, "rel_h1": rel_h1, "rel_hr": rel_hr,
                       "gru_turn0": gru_turn0, "gru_agg": gru_agg, "gru_hn": gru_hn, "gru_r": gru_r, "gru_z": gru_z,
                       "gru_in": gru_in, "gru_turn": gru_turn})

        @block.vector
        def _(dve):
            tt, stt, ts = nc.vector.tensor_tensor, nc.vector.scalar_tensor_tensor, nc.vector.tensor_scalar

            def att_xt(v, step, kind, u):
                L, i = LAY[kind], slot(v, step, "att_xt", (kind, u), "light")
                dve.wait_ge(L.xt_high, nth(v, step, 4, u))
                tt(xt_l[:].rearrange("p c n -> p (c n)"), LIGHT[:, i, :], xt_h[:].rearrange("p c n -> p (c n)").bitcast(F32),
                   ALU.subtract).then_inc(L.xt_low, 1)

            def att_scores(v, step, kind, u, q):
                L, i = LAY[kind], slot(v, step, "att_scores", (kind, u, q), "light")
                ti = take(dve, v, step, "t")
                pi = slot(v, step, kind + "_load", (u,), "pen")
                dve.wait_ge(L.sc_psum, nth(v, step, 4 * L.qs, L.qs * u + q))
                dve.wait_ge(L.pen_ready, nth(v, step, 4, u))
                stand(dve)
                cells = [(q, h) for h in range(L.heads)] if kind == "pre" else [(0, 0), (1, 0)]
                for k, (g, h) in enumerate(cells):
                    last = nc.vector.tensor_tensor_reduce(out=t_sc[ti][:, k, :], in0=LIGHT[:, i, k * P:(k + 1) * P], in1=pen[pi][:, g, :],
                                                          scale=1.0, scalar=-3.0e38, op0=ALU.add, op1=ALU.max,
                                                          accum_out=L.top[:, g, h:h + 1])
                last.then_inc(L.masked, 1)

            def att_soft(v, step, kind, u):
                L = LAY[kind]
                w = slot(v, step, "att_wh", (kind, u, 0), "wh")
                dve.wait_ge(L.masked, nth(v, step, 4 * L.qs, L.qs * (u + 1) - 1))
                tt(L.top[:], L.top[:], wh[w][:, :, D:D + L.heads], ALU.add).then_inc(L.top_ready, 1)
                n = L.heads if kind == "pre" else 2
                for q in range(L.qs):
                    ti = slot(v, step, "att_scores", (kind, u, q), "t")
                    dve.wait_ge(L.shifted, nth(v, step, 8 * L.heads, 2 * L.heads * u + n * (q + 1) - 1))
                    scores = t_sc[ti][:, 0:n, :].rearrange("p h n -> p (h n)")
                    stt(scores, scores, ALPHA, scores, ALU.mult, ALU.max).then_inc(L.leaky, 1)
                dve.wait_ge(L.top_ready, nth(v, step, 4, u))
                stt(L.peak[:], L.top[:], ALPHA, L.top[:], ALU.mult, ALU.max).then_inc(L.peak_ready, 1)
                dve.wait_ge(L.peak_ready, nth(v, step, 4, u))
                ts(L.neg[:], L.peak[:], -1.0, None, ALU.mult).then_inc(L.neg_ready, 1)

            def att_pt(v, step, kind, u, q):
                if kind == "post" or q == 0:
                    return
                L, i = LAY[kind], slot(v, step, "att_pt", (kind, u, q), "light")
                pi = take(dve, v, step, "pt")
                dve.wait_ge(L.pt_ready, nth(v, step, 8, 2 * u))
                dve.wait_ge(L.pt_psum, nth(v, step, 8, 2 * u + q))
                nc.vector.tensor_copy(pt[pi][:].rearrange("p h n -> p (h n)"), LIGHT[:, i, :]).then_inc(L.pt_ready, 1)

            def att_pv(v, step, kind, u):
                L, i = LAY[kind], slot(v, step, "att_pv", (kind, u), "light")
                dve.wait_ge(L.prob, nth(v, step, 8 * L.heads, 2 * L.heads * (u + 1) - 1))
                nc.vector.reciprocal(L.inv[:], L.sum[:]).then_inc(L.inv_ready, 1)
                take(dve, v, step, "hn")
                dve.wait_ge(L.pv_psum, nth(v, step, 4, u))
                dve.wait_ge(L.inv_ready, nth(v, step, 4, u))
                n = 2 * L.heads
                tt(hn_t[:].rearrange("p (k f) -> p k f", k=n), LIGHT[:, i, :].rearrange("p (k f) -> p k f", k=n),
                   L.inv[:].rearrange("p q h -> p (q h)").unsqueeze(2).to_broadcast([P, n, L.f]), ALU.mult).then_inc(L.hn_ready, 1)

            def row_moments(yi, uses):
                for q in range(2):
                    nc.vector.bn_stats(stats[yi][:, q, :], y_t[yi][:, q, :]).then_inc(s_stats[yi], 1)
                for q in range(2):
                    dve.wait_ge(s_stats[yi], uses * 2 + (q + 1))
                    stand(dve)
                    nc.vector.bn_aggr(moments[yi][:, q, :], stats[yi][:, q, :]).then_inc(s_mom[yi], 1)

            def normalise(yi, uses, dst, semaphore):
                dve.wait_ge(s_rstd[yi], uses + 1)
                for q in range(2):
                    last = ts(dst[:, q, :], y_t[yi][:, q, :], moments[yi][:, q, 0:1], rstd[yi][:, q:q + 1], ALU.subtract, ALU.mult)
                last.then_inc(semaphore, 1)

            def att_res(v, step, kind, u):
                L = LAY[kind]
                yi = take(dve, v, step, "y")
                dve.wait_ge(L.ex_ready, nth(v, step, 4, u))
                res = (x_in[slot(v, step, "pre_load", (u,), "x")] if kind == "pre" else x3)[:].rearrange("p q d -> p (q d)")
                y = y_t[yi][:].rearrange("p q d -> p (q d)")
                stt(y, ex_t[:], 1.0, res, ALU.min, ALU.add).then_inc(L.min_ready, 1)
                dve.wait_ge(L.min_ready, nth(v, step, 4, u))
                stt(y, hn_t[:], 0.0, y, ALU.max, ALU.add).then_inc(L.y_ready, 1)
                dve.wait_ge(L.y_ready, nth(v, step, 4, u))
                row_moments(*ring(v, step, "y"))

            def att_norm(v, step, kind, u):
                yi, uses = ring(v, ("att_res", step[1], (kind, u)), "y")
                if kind == "pre":
                    b, at = u // 2, 2 * (u % 2)
                    after(dve, s_turn_ps, nth(v, step, 4, 2 * b + 1) + -4)
                    after(dve, s_nd_l, nth(v, step, 12, 2 * b + 1) + -12)
                    after(dve, s_x1r, nth(v, step, 2, b) + -2)
                    normalise(yi, uses, x1n[b][:, at:at + 2, :], s_x1n[b])
                else:
                    take(dve, v, step, "out")
                    normalise(yi, uses, out_t, s_outn)

            def rel_h1(v, step, u):
                i = slot(v, step, "rel_h1", (u,), "light")
                dve.wait_ge(s_h1h, nth(v, step, 4, u))
                tt(h1_l[:].rearrange("p c n -> p (c n)"), LIGHT[:, i, :], h1_h[:].rearrange("p c n -> p (c n)").bitcast(F32),
                   ALU.subtract).then_inc(s_h1l, 1)

            def rel_y1(v, step, u):
                i = slot(v, step, "rel_y1", (u,), "light")
                yi = take(dve, v, step, "y")
                b, at = u // 2, 2 * (u % 2)
                dve.wait_ge(s_y_ps, nth(v, step, 16, 4 * u))
                dve.wait_ge(s_x2b, nth(v, step, 4, u))
                tt(y_t[yi][:], LIGHT[:, i, :].rearrange("p (q d) -> p q d", q=2), x2[b][:, at:at + 2, :], ALU.add).then_inc(s_rel_y, 1)

            def rel_yr(v, step, u, r):
                i = slot(v, step, "rel_yr", (u, r), "light")
                yi = slot(v, step, "rel_y1", (u,), "y")
                dve.wait_ge(s_y_ps, nth(v, step, 16, 4 * u + r - 1))
                dve.wait_ge(s_rel_y, nth(v, step, 16, 4 * u + r - 2))
                tt(y_t[yi][:], LIGHT[:, i, :].rearrange("p (q d) -> p q d", q=2), y_t[yi][:], ALU.add).then_inc(s_rel_y, 1)

            def rel_stats(v, step, u):
                dve.wait_ge(s_rel_y, nth(v, step, 16, 4 * u + 3))
                row_moments(*ring(v, ("rel_y1", step[1], (u,)), "y"))

            def rel_norm(v, step, u):
                take(dve, v, step, "x3")
                normalise(*ring(v, ("rel_y1", step[1], (u,)), "y"), x3, s_x3)

            def gru_nodes0(v, step, b):
                take(dve, v, step, "nodes")
                dve.wait_ge(s_x1n[b], nth(v, step, 2, 1))
                nc.vector.tensor_copy(hn_h[:], x1n[b][:]).then_inc(s_nd_h, 2)
                after(dve, s_fin_y, nth(v, step, 4, 2 * b + 1) + -4)
                nc.vector.tensor_copy(x1r[b][:], x1n[b][:]).then_inc(s_x1r, 1)

            def gru_turn0(v, step, b, c):
                if c == 1:
                    dve.wait_ge(s_ht0, nth(v, step, 4, 2 * b + 1))
                    nc.vector.tensor_copy(ht_h[b][:], ht[b][:]).then_inc(s_ht_h, 1)

            def gru_agg(v, step, b, l, c):
                i = slot(v, step, "gru_agg", (b, l, c), "misc")
                dve.wait_ge(s_ag_h, nth(v, step, 12, 4 * l + 2 * b + c))
                tt(ag_l[:, c, :], MISC[:, i, :], ag_h[:, c, :].bitcast(F32), ALU.subtract).then_inc(s_ag_l, 1)

            def gru_r(v, step, b, l, c):
                dve.wait_ge(s_hnb, chunk(v, step, b, l, c))
                dve.wait_ge(s_r, chunk(v, step, b, l, c))
                stt(g_hn[c][:], g_r[c][:], 1.0, g_hn[c][:], ALU.add, ALU.mult).then_inc(s_t1, 1)

            def gru_in(v, step, b, l, c):
                n = chunk(v, step, b, l, c)
                dve.wait_ge(s_t1, n)
                dve.wait_ge(s_pi, n)
                tt(g_hn[c][:], IN_PS, g_hn[c][:], ALU.add).then_inc(s_t2, 1)
                dve.wait_ge(s_d, n)
                dve.wait_ge(s_z, n)
                stt(g_d[:], g_z[c][:], 1.0, g_d[:], ALU.add, ALU.mult).then_inc(s_e, 1)
                dve.wait_ge(s_e, n)
                dve.wait_ge(s_n, n)
                stt(ht[b][:, c, :], g_d[:], 0.5, g_n[c][:], ALU.mult, ALU.add).then_inc(s_hnew, 1)

            def gru_split(v, step, b, l):
                dve.wait_ge(s_hnew, chunk(v, step, b, l, 1))
                nc.vector.tensor_copy(ht_h[b][:], ht[b][:]).then_inc(s_ht_h, 1)

            def gru_turn(v, step, b, l, hf):
                i = slot(v, step, "gru_turn", (b, l, hf), "misc")
                dve.wait_ge(s_nd_h, nth(v, step, 12, 4 * (l + 1) + 2 * b + hf))
                rows = slice(2 * hf, 2 * hf + 2)
                tt(hn_l[:, rows, :].rearrange("p q d -> p (q d)"), MISC[:, i, :], hn_h[:, rows, :].rearrange("p q d -> p (q d)").bitcast(F32),
                   ALU.subtract).then_inc(s_nd_l, 1)

            def gru_fin(v, step, b, hf):
                i = slot(v, step, "gru_fin", (b, hf), "misc")
                yi = take(dve, v, step, "y")
                dve.wait_ge(s_fin_ps, nth(v, step, 4, 2 * b + hf))
                dve.wait_ge(s_x1r, nth(v, step, 2, b))
                tt(y_t[yi][:], MISC[:, i, :].rearrange("p (q d) -> p q d", q=2), x1r[b][:, 2 * hf:2 * hf + 2, :], ALU.add).then_inc(s_fin_y, 1)
                dve.wait_ge(s_fin_y, nth(v, step, 4, 2 * b + hf))
                row_moments(*ring(v, step, "y"))

            def gru_norm(v, step, b, hf):
                after(dve, s_rel_y, nth(v, step, 16, 4 * (2 * b + hf)) + -16)
                normalise(*ring(v, ("gru_fin", step[1], (b, hf)), "y"), x2[b][:, 2 * hf:2 * hf + 2, :], s_x2[b])

            walk(dve, {"att_xt": att_xt, "att_scores": att_scores, "att_soft": att_soft, "att_pt": att_pt, "att_pv": att_pv,
                       "att_res": att_res, "att_norm": att_norm, "rel_h1": rel_h1, "rel_y1": rel_y1, "rel_yr": rel_yr,
                       "rel_stats": rel_stats, "rel_norm": rel_norm, "gru_nodes0": gru_nodes0, "gru_turn0": gru_turn0,
                       "gru_agg": gru_agg, "gru_r": gru_r, "gru_in": gru_in, "gru_split": gru_split, "gru_turn": gru_turn,
                       "gru_fin": gru_fin, "gru_norm": gru_norm})

        @block.gpsimd
        def _(pool):
            ts, tt = nc.gpsimd.tensor_scalar, nc.gpsimd.tensor_tensor
            nc.gpsimd.memset(mhalf[:], -0.5).then_inc(s_half, 1)
            pool.wait_ge(s_half, 1)

            def load(v, step, u, kind):
                L = LAY[kind]
                i, uses = ring(v, step, "adj")
                pi = take(pool, v, step, "pen")
                pool.wait_ge(s_adj[i], uses * 16 + 16)
                stand(pool)
                ts(pen[pi][:], adj_i[i][:], 0, MASKED, ALU.is_le, ALU.mult).then_inc(L.pen_ready, 1)
                if kind == "post":
                    take(pool, v, step, "adjf")
                    stand(pool)
                    nc.gpsimd.tensor_copy(adj_f[:], adj_i[i][:]).then_inc(s_adjf, 1)

            def one_over_deviation(yi, uses):
                pool.wait_ge(s_mom[yi], uses * 2 + 2)
                stand(pool)
                ts(rstd[yi][:], moments[yi][:, :, 1], EPS, None, ALU.add).then_inc(s_eps[yi], 1)
                pool.wait_ge(s_eps[yi], uses + 1)
                tt(rstd[yi][:], rstd[yi][:], mhalf[:], ALU.pow).then_inc(s_rstd[yi], 1)

            def rel_mask(v, step, u):
                take(pool, v, step, "mt")
                pool.wait_ge(s_adjt, nth(v, step, 4, u))
                stand(pool)
                ts(mt1[:].rearrange("p q n -> p (q n)"), adj_t[:], 1.0, None, ALU.is_equal).then_inc(s_mt1, 1)

            def rel_hr(v, step, u, r):
                take(pool, v, step, "mr")
                pool.wait_ge(s_adjt, nth(v, step, 4, u))
                stand(pool)
                ts(mtr[:].rearrange("p q n -> p (q n)"), adj_t[:], float(r), None, ALU.is_equal).then_inc(s_mtr, 1)

            def rel_split(v, step, u):
                b, at = u // 2, 2 * (u % 2)
                pool.wait_ge(s_x2h, nth(v, step, 4, u))
                rows = x2[b][:, at:at + 2, :]
                tt(x2_l[:], rows, x2_h[:].bitcast(F32), ALU.subtract).then_inc(s_x2l, 1)
                pool.wait_ge(s_x2l, nth(v, step, 4, u))
                tt(rows, rows, bias_rel[:].unsqueeze(1).to_broadcast([P, 2, D]), ALU.add).then_inc(s_x2b, 1)

            def gru_load(v, step, b):
                pool.wait_ge(s_adjg, nth(v, step, 2, b) * 16)
                after(pool, s_ag_ps, nth(v, step, 12, 4 * (NL - 1) + 2 * b + 1) + -12)
                stand(pool)
                ts(edges[b][:], adj_g[:], 0, 1, ALU.is_equal, ALU.is_lt).then_inc(s_edges, 1)

            def gru_nodes0(v, step, b):
                pool.wait_ge(s_nd_h, nth(v, step, 12, 2 * b + 1))
                tt(hn_l[:], x1n[b][:], hn_h[:].bitcast(F32), ALU.subtract).then_inc(s_nd_l, 2)

            def low_part(v, step, b, version):
                pool.wait_ge(s_ht_h, nth(v, step, 6, 2 * version + b))
                tt(ht_l[b][:], ht[b][:], ht_h[b][:].bitcast(F32), ALU.subtract).then_inc(s_ht_l, 1)

            def gru_turn0(v, step, b, c):
                if c == 1:
                    low_part(v, step, b, 0)

            def gru_split(v, step, b, l):
                low_part(v, step, b, l + 1)

            def gru_in(v, step, b, l, c):
                n = chunk(v, step, b, l, c)
                pool.wait_ge(s_n, n)
                after(pool, s_hnew, n + -1)
                tt(g_d[:], ht[b][:, c, :], g_n[c][:], ALU.subtract).then_inc(s_d, 1)

            walk(pool, {"pre_load": lambda v, step, u: load(v, step, u, "pre"), "post_load": lambda v, step, u: load(v, step, u, "post"),
                        "att_res": lambda v, step, kind, u: one_over_deviation(*ring(v, step, "y")),
                        "rel_stats": lambda v, step, u: one_over_deviation(*ring(v, ("rel_y1", step[1], (u,)), "y")),
                        "gru_fin": lambda v, step, b, hf: one_over_deviation(*ring(v, step, "y")),
                        "rel_mask": rel_mask, "rel_hr": rel_hr, "rel_split": rel_split, "gru_load": gru_load,
                        "gru_nodes0": gru_nodes0, "gru_turn0": gru_turn0, "gru_split": gru_split, "gru_in": gru_in})


_INS = ["x", "adj", "L0_gnn_W", "L0_gnn_a_src", "L0_gnn_a_dst", "L1_gnn_weight", "L1_gnn_w_ih", "L1_gnn_w_hh",
        "L1_gnn_b_ih", "L1_gnn_b_hh", "L2_gnn_adj", "L2_gnn_weight", "L2_gnn_bias", "L3_gnn_W", "L3_gnn_a"]


def kernel(**inputs):
    import numpy as _np
    import concourse.bacc as _bacc
    from concourse import mybir as _mybir
    from concourse.bass_utils import run_bass_kernel_spmd as _run

    nc = _bacc.Bacc("TRN2", target_bir_lowering=False, num_devices=1)
    arrays, args = {}, []
    for name in _INS:
        a = _np.ascontiguousarray(inputs[name])
        arrays[f"in_{name}_dram"] = a
        args.append(nc.dram_tensor(f"in_{name}_dram", a.shape, _mybir.dt.from_np(a.dtype), kind="ExternalInput").ap())
    shape = tuple(inputs["x"].shape)
    out = nc.dram_tensor("out_0_dram", shape, _mybir.dt.float32, kind="ExternalOutput").ap()
    bass_gnn_stack(nc, *args, out)
    r = _run(nc, [arrays], core_ids=[0])
    return r.results[0]["out_0_dram"]
```

```python
from contextlib import ExitStack

import concourse.bass as bass
from concourse import mybir

F32 = mybir.dt.float32
F32R = mybir.dt.float32r
I32 = mybir.dt.int32
ALU = mybir.AluOpType
ACT = mybir.ActivationFunctionType
AX_X, AX_XY = mybir.AxisListType.X, mybir.AxisListType.XY

P = 128
MASKED = -1.0e30
EPS = 1.0e-5
ALPHA = 0.2


class Segment:

    def __init__(self, order, first, end):
        self.order, self.first, self.end = order, first, end


class Visit:

    def __init__(self, g, seg):
        self.g, self.seg = g, seg


SLOTS = {"light": 2, "misc": 2, "adj": 2, "pen": 2, "x": 2, "xt": 1, "wh": 2, "t": 2, "pt": 2,
         "hn": 2, "ex": 1, "y": 2, "x2s": 1, "h1": 1, "mt": 1, "adjt": 1, "x3": 1,
         "adjg": 1, "nodes": 1, "agg": 1, "adjf": 1, "out": 1, "yr": 1, "yf": 1}
TAKES = {
    "pre_load": ("adj", "x", "pen"), "post_load": ("adj", "pen", "adjf"),
    "att_xt": ("light", "xt"), "att_wh": ("light",), "att_scores": ("light",),
    "att_pt": ("light",), "att_pv": ("light", "hn"), "att_exp": ("ex",), "att_res": ("y",),
    "rel_adjt": ("light", "adjt"), "rel_split": ("x2s",), "rel_mask": ("mt",),
    "rel_h1": ("light", "h1"), "rel_y1": ("light", "yr"),
    "rel_rest": ("light",),
    "gru_load": ("adjg",), "gru_nodes0": ("nodes",), "gru_turn0": ("misc",),
    "gru_agg": ("misc",), "gru_turn": ("misc",), "gru_fin": ("misc", "yf"),
}


def takes(step):
    name, _, args = step
    out = list(TAKES.get(name, ()))
    if name == "att_wh" and args[2] == 0:
        out.append("wh")
    if name == "att_scores" and (args[0] == "pre" or args[2] == 0):
        out.append("t")
    if name == "att_pt" :
        out.append("pt")
    if name == "gru_turn" and args[2] == 0:
        out.append("nodes")
    if name == "gru_agg" and args[2] == 0:
        out.append("agg")
    if name == "rel_norm":
        out.append("x3")
    if name == "att_norm" and args[0] == "post":
        out.append("out")
    return out


def attention_steps(kind, u, off):
    k = (kind, u)
    q_steps = (0, 1)
    out = [("att_xt", off, k)]
    out += [("att_wh", off, k + (q,)) for q in q_steps]
    out += [("att_scores", off, k + (q,)) for q in (q_steps if kind == "pre" else (0,))]
    out += [("att_soft", off, k), ("att_prob", off, k)]
    out += [("att_pt", off, k + (q,)) for q in (q_steps if kind == "pre" else (0,))]
    out += [("att_pv", off, k), ("att_exp", off, k), ("att_res", off, k), ("att_norm", off, k)]
    return out


def pre_steps(u, off):
    return [("pre_load", off, (u,))] + attention_steps("pre", u, off)


def post_steps(u, off):
    out = [("post_load", off, (u,)), ("rel_adjt", off, (u,)), ("rel_split", off, (u,)),
           ("rel_mask", off, (u,)), ("rel_h1", off, (u,)), ("rel_y1", off, (u,))]
    return out + [("rel_rest", off, (u,)), ("rel_norm", off, (u,))] + attention_steps("post", u, off)


def gate_steps(b, l, off, mid):
    out = []
    for c in range(2):
        out += [("gru_hn", off, (b, l, c)), ("gru_rzh", off, (b, l, c)), ("gru_r", off, (b, l, c)),
                ("gru_z", off, (b, l, c)), ("gru_in", off, (b, l, c))]
        if c == 0:
            out += mid
    return out


def init_steps(b, off):
    return [("gru_load", off, (b,)), ("gru_turn0", off, (b, 0)), ("gru_turn0", off, (b, 1)),
            ("gru_nodes0", off, (b,))]


def layer_end(b, l, off):
    if l < 2:
        return [("gru_split", off, (b, l))] + [("gru_turn", off, (b, l, hf)) for hf in range(2)]
    return [s for hf in range(2) for s in (("gru_fin", off, (b, hf)), ("gru_norm", off, (b, hf)))]


def gru_steps(first_mid, last_mid):
    out = []
    for l in range(3):
        for b in range(2):
            mid = layer_end(1, l - 1, 0) if b == 0 and l else layer_end(0, l, 0) if b else first_mid
            if (l, b) == (2, 1):
                mid = mid + last_mid
            out += [("gru_agg", 0, (b, l, 0)), ("gru_agg", 0, (b, l, 1))] + gate_steps(b, l, 0, mid)
    return out


WEIGHT = {"gru_hn": 6, "gru_rzh": 12, "gru_r": 6, "gru_z": 6, "gru_in": 6, "gru_agg": 2}


def spread(main, *chains):
    total = sum(WEIGHT.get(s[0], 0) for s in main)
    extra = sorted(((k + at) / len(c) * total, n, s) for n, (c, at) in enumerate(chains) for k, s in enumerate(c))
    out, time = [], 0
    for s in main:
        while extra and extra[0][0] <= time:
            out.append(extra.pop(0)[2])
        out.append(s)
        time += WEIGHT.get(s[0], 0)
    return out + [s for _, _, s in extra]


PRE_AT, POST_AT = 0.5, 1.5


def trip(first, last):
    before = [] if first else layer_end(1, 2, -1)
    after = [] if last else init_steps(0, 1)
    pre = [] if last else [s for u in range(4) for s in pre_steps(u, 1)]
    post = [] if first else [s for u in range(4) for s in post_steps(u, -1)]
    return spread(gru_steps(before + init_steps(1, 0), after), (pre, PRE_AT), (post, POST_AT))


def make_segments(groups):
    start = [s for u in range(4) for s in pre_steps(u, 0)] + init_steps(0, 0)
    end = layer_end(1, 2, 0) + [s for u in range(4) for s in post_steps(u, 0)]
    return [Segment(start, 0, 1), Segment(trip(True, False), 0, 1), Segment(trip(False, False), 1, 2),
            Segment(trip(False, False), 2, groups - 1), Segment(trip(False, True), groups - 1, groups),
            Segment(end, groups - 1, groups)]


def number_uses(segments):
    before = {r: 0 for r in SLOTS}
    for seg in segments:
        seg.uses, seg.takers = {}, {r: [] for r in SLOTS}
        count = {r: 0 for r in SLOTS}
        for s in seg.order:
            for r in takes(s):
                seg.uses[(r,) + s] = count[r]
                seg.takers[r].append(s)
                count[r] += 1
        seg.before, seg.per = dict(before), count
        for r in SLOTS:
            assert count[r] % SLOTS[r] == 0 and before[r] % SLOTS[r] == 0, r
            before[r] += count[r] * (seg.end - seg.first)


def bass_gnn_stack(nc, x, adj, L0_gnn_W, L0_gnn_a_src, L0_gnn_a_dst, L1_gnn_weight, L1_gnn_w_ih,
                   L1_gnn_w_hh, L1_gnn_b_ih, L1_gnn_b_hh, L2_gnn_adj, L2_gnn_weight, L2_gnn_bias,
                   L3_gnn_W, L3_gnn_a, out):
    B, N, D = x.shape
    R = L2_gnn_weight.shape[0]
    H0, F0 = L0_gnn_a_src.shape
    C = D // P
    G3 = 3 * D
    NL = L1_gnn_weight.shape[0]
    GROUPS = B // 8
    assert N == P and C == 2 and B % 8 == 0 and GROUPS >= 5 and R == 4 and NL == 3
    segments = make_segments(GROUPS)
    number_uses(segments)

    with ExitStack() as ctx:
        def sb(name, shape, dt=F32):
            return ctx.enter_context(nc.sbuf_tensor(name, shape, dt))

        def sem(name):
            return ctx.enter_context(nc.semaphore(name))

        psum = ctx.enter_context(nc.psum_tensor("psum", [P, 8, 512], F32))

        ident = sb("ident", [P, P])
        whh_h, whh_l = sb("whh_h", [P, C, G3], F32R), sb("whh_l", [P, C, G3], F32R)
        wc_h, wc_l = sb("wc_h", [P, NL, C, G3], F32R), sb("wc_l", [P, NL, C, G3], F32R)
        w0_h, w0_l = sb("w0_h", [P, C, D + 2 * H0], F32R), sb("w0_l", [P, C, D + 2 * H0], F32R)
        w3_h, w3_l = sb("w3_h", [P, C, D + 2], F32R), sb("w3_l", [P, C, D + 2], F32R)
        wr1_h, wr1_l = sb("wr1_h", [P, C, D], F32R), sb("wr1_l", [P, C, D], F32R)
        wrs = sb("wrs", [P, R - 1, C, D])
        bias_rel = sb("bias_rel", [P, D])
        bias_rz = sb("bias_rz", [P, 4])
        bias_hn = sb("bias_hn", [P, 2])
        bias_in = sb("bias_in", [P, 2])
        mhalf = sb("mhalf", [P, 2])
        others = sb("others", [1, 1], I32)

        with ExitStack() as early:
            def tmp(name, shape, dt=F32):
                return early.enter_context(nc.sbuf_tensor(name, shape, dt))

            hh_raw, ih_raw = tmp("hh_raw", [P, 6, D]), tmp("ih_raw", [P, 6, D])
            wl_raw = tmp("wl_raw", [P, NL, C, D])
            w0_raw, w3_raw, wr1_raw = tmp("w0_raw", [P, C, D]), tmp("w3_raw", [P, C, D]), tmp("wr1_raw", [P, C, D])
            a_src, a_dst, a3 = tmp("a_src", [P, D]), tmp("a_dst", [P, D]), tmp("a3", [P, 2 * D])
            bi, bh = tmp("bi", [P, 6]), tmp("bh", [P, 6])
            ihT = tmp("ihT", [P, C, G3])
            stage = tmp("stage", [P, C, G3])
            wlT = tmp("wlT", [P, C, D])
            aug0, aug3 = tmp("aug0", [P, C, D + 2 * H0]), tmp("aug3", [P, C, D + 2])
            prod = tmp("prod", [P, C, D])
            SCAN = 16
            PARTS = B // SCAN
            parts = [tmp(f"part{i}", [P, SCAN, N], I32) for i in range(4)]
            tops, top, topT = tmp("tops", [P, PARTS]), tmp("top", [P, 1]), tmp("topT", [1, 1])
            s_part = [sem(f"part_loaded{i}") for i in range(4)]
            s_scan, s_top = sem("parts_scanned"), sem("tops_turned")
            s_w = sem("weights_loaded")
            s_wl = sem("layer_weights_loaded")
            s_id0, s_id = sem("ident_zeroed"), sem("ident_ready")
            s_t, s_c = sem("setup_psum_ready"), sem("setup_dve_done")
            block = early.enter_context(nc.Block())
            W_LOADS = 14

            @block.sync
            def _(sp):
                with nc.allow_non_contiguous_dma(reason="a few bias columns and broadcast rows, once"):
                    for dst, src in (
                        (hh_raw[:], L1_gnn_w_hh.rearrange("(m p) d -> p m d", p=P)),
                        (ih_raw[:], L1_gnn_w_ih.rearrange("(m p) d -> p m d", p=P)),
                        (w3_raw[:], L3_gnn_W.rearrange("(o p) i -> p o i", p=P)),
                        (w0_raw[:], L0_gnn_W.rearrange("(c p) o -> p c o", p=P)),
                        (wl_raw[:], L1_gnn_weight.rearrange("l (c p) e -> p l c e", p=P)),
                        (wr1_raw[:], L2_gnn_weight[0].rearrange("(c p) o -> p c o", p=P)),
                        (wrs[:], L2_gnn_weight[1:R].rearrange("r (c p) o -> p r c o", p=P)),
                        (a_src[:], L0_gnn_a_src.rearrange("(a h) f -> a (h f)", a=1).broadcast_to([P, D])),
                        (a_dst[:], L0_gnn_a_dst.rearrange("(a h) f -> a (h f)", a=1).broadcast_to([P, D])),
                        (a3[:], L3_gnn_a.broadcast_to([P, 2 * D])),
                        (bias_rel[:], L2_gnn_bias.rearrange("(a d) -> a d", a=1).broadcast_to([P, D])),
                        (bi[:], L1_gnn_b_ih.rearrange("(m p) -> p m", p=P)),
                        (bh[:], L1_gnn_b_hh.rearrange("(m p) -> p m", p=P)),
                        (mhalf[:, 0:1], L2_gnn_adj.rearrange("(a d) -> a d", a=1).broadcast_to([P, 1])),
                    ):
                        sp.dma_start(dst, src).then_inc(s_w, 16)
                for k in range(PARTS):
                    if k >= 4:
                        sp.wait_ge(s_scan, k - 3)
                    sp.dma_start(parts[k % 4][:], adj[k * SCAN:(k + 1) * SCAN].rearrange("g n m -> n g m")).then_inc(s_part[k % 4], 16)

            @block.gpsimd
            def _(pool):
                nc.gpsimd.memset(ident[:], 0.0).then_inc(s_id0, 1)
                pool.wait_ge(s_id0, 1)
                nc.gpsimd.affine_select(out=ident[:], in_=ident[:], compare_op=ALU.not_equal, fill=1.0,
                                        base=0, pattern=[[-1, P]], channel_multiplier=1).then_inc(s_id, 1)

            @block.tensor
            def _(pe):
                pe.wait_ge(s_w, 16 * W_LOADS)
                pe.wait_ge(s_id, 1)

                def turn(bank, raw, rows):
                    for c in range(C):
                        flat = psum[:, bank + 2 * c:bank + 2 * c + 2, :].rearrange("p a n -> p (a n)")
                        for m in range(rows):
                            last = nc.tensor.transpose(flat[:, m * P:(m + 1) * P], raw[:, m, c * P:(c + 1) * P], ident[:])
                    last.then_inc(s_t, 1)

                turn(0, hh_raw, 6)
                turn(4, ih_raw, 6)
                pe.wait_ge(s_c, 1)
                turn(0, w3_raw, 2)
                for l in range(NL):
                    pe.wait_ge(s_c, 2 + 2 * l)
                    turn(4, wl_raw[:, l], C)
                    pe.wait_ge(s_c, 3 + 2 * l)
                    for c in range(C):
                        for n0, n1 in ((0, 512), (512, G3)):
                            for e in range(C):
                                last = nc.tensor.matmul(psum[:, 4 + 2 * c + n0 // 512, 0:n1 - n0],
                                                        wlT[:, e, c * P:(c + 1) * P], ihT[:, e, n0:n1],
                                                        start=(e == 0), stop=(e == C - 1))
                    last.then_inc(s_t, 1)
                pe.wait_ge(s_scan, PARTS + 1)
                nc.tensor.transpose(psum[0:1, 0, 0:P], top[:], ident[:]).then_inc(s_top, 1)

            @block.vector
            def _(dve):
                chain = [0]

                def done(ins):
                    chain[0] += 1
                    ins.then_inc(s_wl, 1)
                    dve.wait_ge(s_wl, chain[0])

                def banks(bank, n):
                    return psum[:, bank:bank + 4, :].rearrange("p (c a) n -> p c (a n)", c=C)[:, :, 0:n]

                def split(hi, lo, src):
                    done(nc.vector.tensor_copy(hi, src))
                    done(nc.vector.tensor_tensor(lo, src, hi.bitcast(F32), ALU.subtract))

                def scan(first, end):
                    for k in range(first, end):
                        dve.wait_ge(s_part[k % 4], 16 * (k // 4 + 1))
                        nc.vector.tensor_reduce(tops[:, k:k + 1], parts[k % 4][:], AX_XY, ALU.max).then_inc(s_scan, 1)

                dve.wait_ge(s_w, 16 * W_LOADS)
                done(nc.vector.memset(mhalf[:], -0.5))
                dve.wait_ge(s_t, 1)
                done(nc.vector.tensor_copy(stage[:, :, 0:2 * D], banks(0, 2 * D)))
                done(nc.vector.tensor_scalar(stage[:, :, 2 * D:G3], banks(0, G3)[:, :, 2 * D:G3], 0.5, None, ALU.mult))
                nc.vector.memset(prod[:], 0.0).then_inc(s_c, 1)
                split(whh_h[:], whh_l[:], stage[:])
                dve.wait_ge(s_t, 2)
                done(nc.vector.tensor_copy(ihT[:], banks(4, G3)))
                dve.wait_ge(s_t, 3)
                done(nc.vector.tensor_copy(aug3[:, :, 0:D], banks(0, D)))
                dve.wait_ge(s_c, 1)
                nc.vector.memset(bias_rz[:], 0.0).then_inc(s_c, 1)
                for l in range(NL):
                    dve.wait_ge(s_t, 4 + 2 * l)
                    done(nc.vector.tensor_copy(wlT[:], banks(4, D)))
                    nc.vector.tensor_copy(stage[:, 0, 0:1], wlT[:, 0, 0:1]).then_inc(s_c, 1)
                    scan(PARTS * l // 3, PARTS * (l + 1) // 3)
                    dve.wait_ge(s_t, 5 + 2 * l)
                    for hi, lo in ((wc_h[:, l], wc_l[:, l]),):
                        done(nc.vector.tensor_copy(hi, banks(4, G3)))
                        done(nc.vector.tensor_tensor(lo, banks(4, G3), hi.bitcast(F32), ALU.subtract))
                    nc.vector.tensor_copy(stage[:, 0, 1:2], wlT[:, 0, 0:1]).then_inc(s_c, 1)
                dve.wait_ge(s_scan, PARTS)
                nc.vector.tensor_reduce(top[:], tops[:], AX_X, ALU.max).then_inc(s_scan, 1)
                done(nc.vector.tensor_copy(aug0[:, :, 0:D], w0_raw[:]))
                for k, a in enumerate((a_src, a_dst)):
                    done(nc.vector.tensor_tensor(prod[:], w0_raw[:], a[:].unsqueeze(1).to_broadcast([P, C, D]), ALU.mult))
                    for c in range(C):
                        done(nc.vector.tensor_reduce(aug0[:, c, D + k * H0:D + (k + 1) * H0],
                                                     prod[:, c].rearrange("p (h f) -> p h f", h=H0), AX_X, ALU.add))
                for k in range(2):
                    done(nc.vector.tensor_tensor(prod[:], aug3[:, :, 0:D],
                                                 a3[:, k * D:(k + 1) * D].unsqueeze(1).to_broadcast([P, C, D]), ALU.mult))
                    done(nc.vector.tensor_reduce(aug3[:, :, D + k:D + k + 1], prod[:], AX_X, ALU.add))
                split(w0_h[:], w0_l[:], aug0[:])
                split(w3_h[:], w3_l[:], aug3[:])
                split(wr1_h[:], wr1_l[:], wr1_raw[:])
                done(nc.vector.tensor_tensor(bias_rz[:], bi[:, 0:4], bh[:, 0:4], ALU.add))
                done(nc.vector.tensor_scalar(bias_rz[:], bias_rz[:], 0.5, None, ALU.mult))
                done(nc.vector.tensor_scalar(bias_hn[:], bh[:, 4:6], 0.5, None, ALU.mult))
                done(nc.vector.tensor_copy(bias_in[:], bi[:, 4:6]))
                dve.wait_ge(s_top, 1)
                done(nc.vector.tensor_reduce(topT[:], psum[0:1, 0, 0:P], AX_X, ALU.max))
                done(nc.vector.tensor_scalar(others[:], topT[:], 2.0, None, ALU.is_ge))

        adj_i = [sb(f"adj_i{i}", [P, 2, P], I32) for i in range(2)]
        pen = [sb(f"pen{i}", [P, 2, P]) for i in range(2)]
        x_in = [sb(f"x_in{i}", [P, 2, D]) for i in range(2)]
        xt_h, xt_l = sb("xt_h", [P, C, 2 * P], F32R), sb("xt_l", [P, C, 2 * P], F32R)
        wh = [sb(f"wh{i}", [P, 2, D + 2 * H0]) for i in range(2)]
        t_sc = [sb(f"t_sc{i}", [P, 4, P]) for i in range(2)]
        pt = [sb(f"pt{i}", [P, 4, P]) for i in range(2)]
        hn_t = [sb(f"hn_t{i}", [P, 2 * D]) for i in range(2)]
        ex_t = sb("ex_t", [P, 2 * D])
        y_t = [sb(f"y_t{i}", [P, 2, D]) for i in range(4)]
        stats = [sb(f"stats{i}", [P, 2, 6]) for i in range(4)]
        moments = [sb(f"moments{i}", [P, 2, 2]) for i in range(4)]
        rstd = [sb(f"rstd{i}", [P, 2]) for i in range(4)]
        x3 = sb("x3", [P, 2, D])
        out_t = sb("out_t", [P, 2, D])
        x2_h, x2_l = sb("x2_h", [P, 2, D], F32R), sb("x2_l", [P, 2, D], F32R)
        adj_f, adj_t = sb("adj_f", [P, 2, P]), sb("adj_t", [P, 2 * P])
        mt1, mtr = sb("mt1", [P, 2, P], F32R), sb("mtr", [P, 2, P], F32R)
        h1_h, h1_l = sb("h1_h", [P, C, 2 * P], F32R), sb("h1_l", [P, C, 2 * P], F32R)
        hr_t = sb("hr_t", [P, C, 2 * P])
        adj_g = sb("adj_g", [P, 4, P], I32)
        edges = [sb(f"edges{b}", [P, 4, P], F32R) for b in range(2)]
        x1n = [sb(f"x1n{b}", [P, 4, D]) for b in range(2)]
        x1r = [sb(f"x1r{b}", [P, 4, D]) for b in range(2)]
        x2 = [sb(f"x2{b}", [P, 4, D]) for b in range(2)]
        ht = [sb(f"ht{b}", [P, C, 4 * P]) for b in range(2)]
        ht_h = [sb(f"ht_h{b}", [P, C, 4 * P], F32R) for b in range(2)]
        ht_l = [sb(f"ht_l{b}", [P, C, 4 * P], F32R) for b in range(2)]
        hn_h, hn_l = sb("hn_h", [P, 4, D], F32R), sb("hn_l", [P, 4, D], F32R)
        ag_h, ag_l = sb("ag_h", [P, C, 4 * P], F32R), sb("ag_l", [P, C, 4 * P], F32R)
        g_hn = [sb(f"g_hn{c}", [P, 512]) for c in range(2)]
        g_r, g_n = sb("g_r", [P, 512]), sb("g_n", [P, 512])
        g_z = [sb(f"g_z{c}", [P, 512]) for c in range(2)]

        class Layer:

            def __init__(self, name, heads, w_h, w_l):
                self.heads, self.f, self.cols, self.qs = heads, D // heads, D + 2 * heads, 2 if heads > 1 else 1
                self.w_h, self.w_l = w_h, w_l
                self.top, self.peak, self.neg, self.sum, self.inv = (
                    sb(f"{name}_{what}", [P, 2, heads]) for what in ("top", "peak", "neg", "sum", "inv"))
                self.xt_psum = sem("%s_xt_psum" % name)
                self.xt_high = sem("%s_xt_high" % name)
                self.xt_low = sem("%s_xt_low" % name)
                self.wh_psum = sem("%s_wh_psum" % name)
                self.wh_ready = sem("%s_wh_ready" % name)
                self.sc_psum = sem("%s_sc_psum" % name)
                self.masked = sem("%s_masked" % name)
                self.top_ready = sem("%s_top_ready" % name)
                self.peak_ready = sem("%s_peak_ready" % name)
                self.neg_ready = sem("%s_neg_ready" % name)
                self.shifted = sem("%s_shifted" % name)
                self.leaky = sem("%s_leaky" % name)
                self.prob = sem("%s_prob" % name)
                self.pt_psum = sem("%s_pt_psum" % name)
                self.pt_ready = sem("%s_pt_ready" % name)
                self.pv_psum = sem("%s_pv_psum" % name)
                self.inv_ready = sem("%s_inv_ready" % name)
                self.hn_ready = sem("%s_hn_ready" % name)
                self.ex_ready = sem("%s_ex_ready" % name)
                self.min_ready = sem("%s_min_ready" % name)
                self.y_ready = sem("%s_y_ready" % name)
                self.pen_ready = sem("%s_pen_ready" % name)

        LAY = {"pre": Layer("first", H0, w0_h, w0_l), "post": Layer("last", 1, w3_h, w3_l)}

        s_x = [sem(f"x_loaded{i}") for i in range(2)]
        s_adj = [sem(f"adj_loaded{i}") for i in range(2)]
        s_adjg, s_edges, s_adjf = sem("adjg_loaded"), sem("edges_ready"), sem("adjf_ready")
        s_stats, s_mom, s_eps, s_rstd = ([sem(f"{n}{i}") for i in range(4)] for n in ("stats_ready", "moments_ready", "eps_added", "rstd_ready"))
        s_x1n = [sem(f"x1n_ready{b}") for b in range(2)]
        s_x2 = [sem(f"x2_ready{b}") for b in range(2)]
        s_x1r = sem("x1r_ready")
        s_adjt_ps, s_adjt, s_mt1, s_mtr = sem("adjt_psum"), sem("adjt_ready"), sem("mask1_ready"), sem("maskr_ready")
        s_x2h, s_x2l, s_x2b = sem("x2_high"), sem("x2_low"), sem("x2_biased")
        s_h1_ps, s_h1h, s_h1l = sem("h1_psum"), sem("h1_high"), sem("h1_low")
        s_y_ps, s_rel_y = sem("rel_psum"), sem("rel_y_ready")
        s_hr_ps, s_hr, s_yr_ps, s_yr = sem("hr_psum"), sem("hr_ready"), sem("rest_psum"), sem("rest_added")
        s_x3, s_outn, s_out = sem("x3_ready"), sem("out_ready"), sem("out_stored")
        s_turn_ps, s_ht0, s_ht_h, s_ht_l = sem("turned_psum"), sem("ht_ready"), sem("ht_high"), sem("ht_low")
        s_nd_ps, s_nd_h, s_nd_l = sem("nodes_psum"), sem("nodes_high"), sem("nodes_low")
        s_ag_ps, s_ag_h, s_ag_l = sem("agg_psum"), sem("agg_high"), sem("agg_low")
        s_ph, s_pr, s_pz, s_pi = sem("hn_psum"), sem("r_psum"), sem("z_psum"), sem("in_psum")
        s_hnb, s_r, s_z, s_t1, s_t2, s_n = (sem(n) for n in ("hn_biased", "r_ready", "z_ready", "rh_ready", "cand_sum", "n_ready"))
        s_d, s_e, s_hnew = sem("diff_ready"), sem("zdiff_ready"), sem("h_new")
        s_fin_ps, s_fin_y = sem("final_psum"), sem("final_y")
        s_half = sem("exponent_ready")
        s_stood = sem("waits_stood")

        block = ctx.enter_context(nc.Block())
        LIGHT, MISC = psum[:, 0:2, :], psum[:, 2:4, :]
        HN_PS, R_PS, Z_PS, IN_PS = (psum[:, k, :] for k in range(4, 8))

        def nth(v, step, per, k):
            return v.g * per + (step[1] * per + k + 1)

        def chunk(v, step, b, l, c):
            return nth(v, step, 12, 4 * l + 2 * b + c)

        def ring(v, step, resource):
            k, n = v.seg.uses[(resource,) + step], SLOTS[resource]
            per = v.seg.per[resource] // n
            return k % n, v.g * per + (v.seg.before[resource] // n + k // n - v.seg.first * per)

        def rows_of_rel(v, step, u):
            return 2, ring(v, ("rel_y1", step[1], (u,)), "yr")[1]

        def rows_of_gru(v, step, b, hf):
            return 3, ring(v, ("gru_fin", step[1], (b, hf)), "yf")[1]

        def after(eng, semaphore, value):
            if not isinstance(value, int) or value > 0:
                eng.wait_ge(semaphore, value)

        def stand(eng):
            eng.sem_inc(s_stood, 1)

        def last_read(resource, v, step):
            name, _, a = step
            if name.startswith("att"):
                L, u = LAY[a[0]], a[1]
                qth = nth(v, step, 4 * L.qs, L.qs * u + (a[2] if len(a) > 2 else 0))
                uth = nth(v, step, 4, u)
                b = u // 2
                return {
                    ("light", "att_xt"): (L.xt_low, uth), ("light", "att_scores"): (L.masked, qth),
                    ("light", "att_pt"): (L.pt_ready, qth), ("light", "att_pv"): (L.hn_ready, uth),
                    ("light", "att_wh"): (L.wh_ready, nth(v, step, 8, 2 * u + (a[2] if len(a) > 2 else 0))),
                    ("xt", "att_xt"): (L.wh_psum, nth(v, step, 8, 2 * u + 1)),
                    ("wh", "att_wh"): (L.pv_psum, uth), ("t", "att_scores"): (L.pt_psum, qth),
                    ("pt", "att_pt"): (L.pv_psum, uth), ("hn", "att_pv"): (L.y_ready, uth),
                    ("ex", "att_exp"): (L.min_ready, uth),
                    ("y", "att_res"): (s_x1n[b], nth(v, step, 2, u % 2)) if a[0] == "pre" else (s_outn, uth),
                    ("out", "att_norm"): (s_out, uth * 16),
                }[resource, name]
            if name == "pre_load":
                return {"adj": (LAY["pre"].pen_ready, nth(v, step, 4, a[0])), "x": (LAY["pre"].min_ready, nth(v, step, 4, a[0])),
                        "pen": (LAY["pre"].masked, nth(v, step, 8, 2 * a[0] + 1))}[resource]
            if name == "post_load":
                return {"adj": (s_adjf, nth(v, step, 4, a[0])), "adjf": (s_adjt_ps, nth(v, step, 4, a[0])),
                        "pen": (LAY["post"].masked, nth(v, step, 4, a[0]))}[resource]
            if name.startswith("rel"):
                u = a[0]
                return {
                    ("light", "rel_adjt"): (s_adjt, nth(v, step, 4, u)), ("adjt", "rel_adjt"): (s_mt1, nth(v, step, 4, u)),
                    ("x2s", "rel_split"): (s_h1_ps, nth(v, step, 4, u)), ("mt", "rel_mask"): (s_h1_ps, nth(v, step, 4, u)),
                    ("light", "rel_h1"): (s_h1l, nth(v, step, 4, u)), ("h1", "rel_h1"): (s_y_ps, nth(v, step, 4, u)),
                    ("light", "rel_y1"): (s_rel_y, nth(v, step, 4, u)), ("yr", "rel_y1"): (s_x3, nth(v, step, 4, u)),
                    ("light", "rel_rest"): (s_stats[2], nth(v, step, 8, 2 * u)),
                    ("x3", "rel_norm"): (LAY["post"].min_ready, nth(v, step, 4, u)),
                }[resource, name]
            b = a[0]
            if name == "gru_load":
                return s_edges, nth(v, step, 2, b)
            if name == "gru_turn0":
                return s_ht0, nth(v, step, 4, 2 * b + a[1])
            if name == "gru_nodes0":
                return s_ag_ps, nth(v, step, 12, 2 * b + 1)
            if name == "gru_agg":
                return (s_ag_l, nth(v, step, 12, 4 * a[1] + 2 * b + a[2])) if resource == "misc" else (s_pi, chunk(v, step, b, a[1], 1))
            if name == "gru_turn":
                return (s_nd_l, nth(v, step, 12, 4 * (a[1] + 1) + 2 * b + a[2])) if resource == "misc" else \
                    (s_ag_ps, nth(v, step, 12, 4 * (a[1] + 1) + 2 * b + 1))
            assert name == "gru_fin"
            return (s_fin_y, nth(v, step, 4, 2 * b + a[1])) if resource == "misc" else (s_x2[b], nth(v, step, 2, a[1]))

        def take(eng, v, step, resource):
            seg, n = v.seg, SLOTS[resource]
            k = seg.uses[(resource,) + step]
            takers = seg.takers[resource]
            if k >= n:
                eng.wait_ge(*last_read(resource, v, takers[k - n]))
                return k % n
            earlier = [s for s in segments[:segments.index(seg)] if s.takers[resource]]
            at_end = None
            if earlier:
                tail = earlier[-1]
                at_end = last_read(resource, Visit(tail.end - 1, tail), tail.takers[resource][k - n])
                at_end = (at_end[0], at_end[1])
            if seg.end - seg.first > 1:
                wrapped = takers[k - n]
                eng.wait_ge(*last_read(resource, Visit(v.g + -1, seg), wrapped))
                first = last_read(resource, Visit(seg.first - 1, seg), wrapped)
                if at_end and first[0] is at_end[0] and first[1] == at_end[1]:
                    at_end = None
            if at_end:
                eng.wait_ge(*at_end)
            return k % n

        def walk(eng, shares):
            for seg in segments:
                if seg.end - seg.first == 1:
                    for step in seg.order:
                        if step[0] in shares:
                            shares[step[0]](Visit(seg.first, seg), step, *step[2])
                else:
                    with eng.Fori(seg.first, seg.end) as g:
                        for step in seg.order:
                            if step[0] in shares:
                                shares[step[0]](Visit(g, seg), step, *step[2])

        def slot(v, step, name, args, resource):
            return v.seg.uses[(resource, name, step[1], args)] % SLOTS[resource]

        def t_slots(v, step, kind, u):
            return [(slot(v, step, "att_scores", (kind, u, q if kind == "pre" else 0), "t"), h if kind == "pre" else q, q, h)
                    for q in range(2) for h in range(LAY[kind].heads)]

        @block.sync
        def _(sp):
            def graphs(v, step, first, n):
                at = v.g * 8 + (step[1] * 8 + first)
                return slice(at, at + n) if isinstance(at, int) else bass.ds(at, n)

            def load_adj(v, step, u):
                i = take(sp, v, step, "adj")
                sp.dma_start(adj_i[i][:], adj[graphs(v, step, 2 * u, 2)].rearrange("g n m -> n g m")).then_inc(s_adj[i], 16)

            def pre_load(v, step, u):
                load_adj(v, step, u)
                i = take(sp, v, step, "x")
                sp.dma_start(x_in[i][:], x[graphs(v, step, 2 * u, 2)].rearrange("g n d -> n g d")).then_inc(s_x[i], 16)

            def gru_load(v, step, b):
                take(sp, v, step, "adjg")
                sp.dma_start(adj_g[:], adj[graphs(v, step, 4 * b, 4)].rearrange("g n m -> n g m")).then_inc(s_adjg, 16)

            def att_norm(v, step, kind, u):
                if kind == "post":
                    sp.wait_ge(s_outn, nth(v, step, 4, u))
                    sp.dma_start(out[graphs(v, step, 2 * u, 2)].rearrange("g n d -> n g d"), out_t[:]).then_inc(s_out, 16)

            walk(sp, {"pre_load": pre_load, "post_load": load_adj, "gru_load": gru_load, "att_norm": att_norm})
            sp.wait_ge(s_out, 16 * 4 * GROUPS)

        @block.tensor
        def _(pe):
            mm, turn = nc.tensor.matmul, nc.tensor.transpose
            any_other = pe.value_load(others[0:1, 0:1], min_val=0, max_val=1)

            def three(dst, pairs):
                n = 3 * len(pairs)
                terms = [t for (sh, sl), (mh, ml) in pairs for t in ((sh, mh), (sh, ml), (sl, mh))]
                for k, (s, m) in enumerate(terms):
                    last = mm(dst, s, m, start=(k == 0), stop=(k == n - 1))
                return last

            def att_xt(v, step, kind, u):
                L, i = LAY[kind], take(pe, v, step, "light")
                if kind == "pre":
                    xi, uses = ring(v, ("pre_load", step[1], (u,)), "x")
                    pe.wait_ge(s_x[xi], uses * 16 + 16)
                    src = x_in[xi]
                else:
                    pe.wait_ge(s_x3, nth(v, step, 4, u))
                    src = x3
                for c in range(C):
                    for q in range(2):
                        last = turn(LIGHT[:, i, (2 * c + q) * P:(2 * c + q + 1) * P], src[:, q, c * P:(c + 1) * P], ident[:])
                last.then_inc(L.xt_psum, 1)

            def att_wh(v, step, kind, u, q):
                L, i = LAY[kind], take(pe, v, step, "light")
                if q == 0:
                    pe.wait_ge(L.xt_high, nth(v, step, 4, u))
                    pe.wait_ge(L.xt_low, nth(v, step, 4, u))
                rows = slice(q * P, (q + 1) * P)
                three(LIGHT[:, i, 0:L.cols], [((xt_h[:, c, rows], xt_l[:, c, rows]), (L.w_h[:, c, :], L.w_l[:, c, :]))
                                              for c in range(C)]).then_inc(L.wh_psum, 1)

            def att_scores(v, step, kind, u, q):
                L, i = LAY[kind], take(pe, v, step, "light")
                w = slot(v, step, "att_wh", (kind, u, 0), "wh")
                pe.wait_ge(L.wh_ready, nth(v, step, 8, 2 * u + (q if kind == "pre" else 1)))
                cells = [(q, h) for h in range(L.heads)] if kind == "pre" else [(0, 0), (1, 0)]
                for k, (g, h) in enumerate(cells):
                    col = D + L.heads + h
                    last = turn(LIGHT[:, i, k * P:(k + 1) * P], wh[w][:, g, col:col + 1].to_broadcast([P, P]), ident[:])
                last.then_inc(L.sc_psum, 1)

            def att_pt(v, step, kind, u, q):
                L, i = LAY[kind], take(pe, v, step, "light")
                cells = [s for s in t_slots(v, step, kind, u) if kind == "post" or s[2] == q]
                pe.wait_ge(L.prob, nth(v, step, 8 * L.heads, 2 * L.heads * u + (L.heads * (q + 1) if kind == "pre" else 2) - 1))
                for k, (ti, at, _, _) in enumerate(cells):
                    last = turn(LIGHT[:, i, k * P:(k + 1) * P], t_sc[ti][:, at, :], ident[:])
                last.then_inc(L.pt_psum, 1)

            def att_pv(v, step, kind, u):
                L, i = LAY[kind], take(pe, v, step, "light")
                w = slot(v, step, "att_wh", (kind, u, 0), "wh")
                pe.wait_ge(L.pt_ready, nth(v, step, 4 * L.qs, L.qs * u + L.qs - 1))
                for q in range(2):
                    for h in range(L.heads):
                        pi = slot(v, step, "att_pt", (kind, u, q if kind == "pre" else 0), "pt")
                        at = (q * L.heads + h) * L.f
                        last = mm(LIGHT[:, i, at:at + L.f], pt[pi][:, h if kind == "pre" else q, :],
                                  wh[w][:, q, h * L.f:(h + 1) * L.f], start=True, stop=True)
                last.then_inc(L.pv_psum, 1)

            def rel_adjt(v, step, u):
                i = take(pe, v, step, "light")
                pe.wait_ge(s_adjf, nth(v, step, 4, u))
                for q in range(2):
                    last = turn(LIGHT[:, i, q * P:(q + 1) * P], adj_f[:, q, :], ident[:])
                last.then_inc(s_adjt_ps, 1)

            def neighbours(dst, mask):
                for c in range(C):
                    for q in range(2):
                        at = (2 * c + q) * P
                        mm(dst[:, at:at + P], x2_h[:, q, c * P:(c + 1) * P], mask[:, q, :], start=True, stop=False)
                        last = mm(dst[:, at:at + P], x2_l[:, q, c * P:(c + 1) * P], mask[:, q, :], start=False, stop=True)
                return last

            def rel_h1(v, step, u):
                i = take(pe, v, step, "light")
                pe.wait_ge(s_x2h, nth(v, step, 4, u))
                pe.wait_ge(s_x2l, nth(v, step, 4, u))
                pe.wait_ge(s_mt1, nth(v, step, 4, u))
                neighbours(LIGHT[:, i, :], mt1).then_inc(s_h1_ps, 1)

            def rel_y1(v, step, u):
                i = take(pe, v, step, "light")
                pe.wait_ge(s_h1h, nth(v, step, 4, u))
                pe.wait_ge(s_h1l, nth(v, step, 4, u))
                for q in range(2):
                    rows = slice(q * P, (q + 1) * P)
                    last = three(LIGHT[:, i, q * D:(q + 1) * D], [((h1_h[:, c, rows], h1_l[:, c, rows]), (wr1_h[:, c, :], wr1_l[:, c, :]))
                                                                  for c in range(C)])
                last.then_inc(s_y_ps, 1)

            def rel_rest(v, step, u):
                i = take(pe, v, step, "light")
                with pe.If(any_other > 0):
                    for r in range(2, R + 1):
                        n = nth(v, step, 4 * (R - 1), (R - 1) * u + r - 2)
                        pe.wait_ge(s_mtr, n)
                        if r > 2:
                            pe.wait_ge(s_yr, n + -1)
                        neighbours(LIGHT[:, i, :], mtr).then_inc(s_hr_ps, 1)
                        pe.wait_ge(s_hr, n)
                        for q in range(2):
                            for c in range(C):
                                last = mm(LIGHT[:, i, q * D:(q + 1) * D], hr_t[:, c, q * P:(q + 1) * P], wrs[:, r - 2, c, :],
                                          start=(c == 0), stop=(c == C - 1))
                        last.then_inc(s_yr_ps, 1)

            def gru_turn0(v, step, b, c):
                i = take(pe, v, step, "misc")
                pe.wait_ge(s_x1n[b], nth(v, step, 2, 1))
                for q in range(4):
                    last = turn(MISC[:, i, q * P:(q + 1) * P], x1n[b][:, q, c * P:(c + 1) * P], ident[:])
                last.then_inc(s_turn_ps, 1)

            def gru_agg(v, step, b, l, c):
                i = take(pe, v, step, "misc")
                pe.wait_ge(s_nd_h, nth(v, step, 12, 4 * l + 2 * b + 1))
                pe.wait_ge(s_nd_l, nth(v, step, 12, 4 * l + 2 * b + 1))
                if l == 0:
                    pe.wait_ge(s_edges, nth(v, step, 2, b))
                for q in range(4):
                    dst = MISC[:, i, q * P:(q + 1) * P]
                    mm(dst, hn_h[:, q, c * P:(c + 1) * P], edges[b][:, q, :], start=True, stop=False)
                    last = mm(dst, hn_l[:, q, c * P:(c + 1) * P], edges[b][:, q, :], start=False, stop=True)
                last.then_inc(s_ag_ps, 1)

            def gate_terms(rows, w_h, w_l, m_h, m_l):
                return [((w_h[:, k, rows], w_l[:, k, rows]), (m_h[:, k, :], m_l[:, k, :])) for k in range(C)]

            def rows_of(gate, c):
                return slice(gate * D + c * P, gate * D + (c + 1) * P)

            def accumulate(dst, terms, first, last_part):
                flat = [t for (sh, sl), (mh, ml) in terms for t in ((sh, mh), (sh, ml), (sl, mh))]
                for k, (s, m) in enumerate(flat):
                    last = mm(dst, s, m, start=(first and k == 0), stop=(last_part and k == len(flat) - 1))
                return last

            def gru_hn(v, step, b, l, c):
                pe.wait_ge(s_ht_h, nth(v, step, 6, 2 * l + b))
                pe.wait_ge(s_ht_l, nth(v, step, 6, 2 * l + b))
                after(pe, s_hnb, chunk(v, step, b, l, c) + -1)
                accumulate(HN_PS, gate_terms(rows_of(2, c), whh_h, whh_l, ht_h[b], ht_l[b]), True, True).then_inc(s_ph, 1)

            def gru_rzh(v, step, b, l, c):
                after(pe, s_r, chunk(v, step, b, l, c) + -1)
                accumulate(R_PS, gate_terms(rows_of(0, c), whh_h, whh_l, ht_h[b], ht_l[b]), True, False)
                after(pe, s_z, chunk(v, step, b, l, c) + -1)
                accumulate(Z_PS, gate_terms(rows_of(1, c), whh_h, whh_l, ht_h[b], ht_l[b]), True, False)

            def gru_r(v, step, b, l, c):
                if c == 0:
                    pe.wait_ge(s_ag_h, nth(v, step, 12, 4 * l + 2 * b + 1))
                    pe.wait_ge(s_ag_l, nth(v, step, 12, 4 * l + 2 * b + 1))
                accumulate(R_PS, gate_terms(rows_of(0, c), wc_h[:, l], wc_l[:, l], ag_h, ag_l), False, True).then_inc(s_pr, 1)

            def gru_z(v, step, b, l, c):
                accumulate(Z_PS, gate_terms(rows_of(1, c), wc_h[:, l], wc_l[:, l], ag_h, ag_l), False, True).then_inc(s_pz, 1)

            def gru_in(v, step, b, l, c):
                after(pe, s_t2, chunk(v, step, b, l, c) + -1)
                accumulate(IN_PS, gate_terms(rows_of(2, c), wc_h[:, l], wc_l[:, l], ag_h, ag_l), True, True).then_inc(s_pi, 1)

            def turn_back(v, step, b, hf, semaphore):
                i = take(pe, v, step, "misc")
                for q in range(2):
                    for c in range(C):
                        last = turn(MISC[:, i, q * D + c * P:q * D + (c + 1) * P],
                                    ht[b][:, c, (2 * hf + q) * P:(2 * hf + q + 1) * P], ident[:])
                last.then_inc(semaphore, 1)

            def gru_turn(v, step, b, l, hf):
                pe.wait_ge(s_hnew, chunk(v, step, b, l, 1))
                turn_back(v, step, b, hf, s_nd_ps)

            def gru_fin(v, step, b, hf):
                pe.wait_ge(s_hnew, chunk(v, step, b, NL - 1, 1))
                turn_back(v, step, b, hf, s_fin_ps)

            walk(pe, {"att_xt": att_xt, "att_wh": att_wh, "att_scores": att_scores, "att_pt": att_pt, "att_pv": att_pv,
                      "rel_adjt": rel_adjt, "rel_h1": rel_h1, "rel_y1": rel_y1, "rel_rest": rel_rest,
                      "gru_turn0": gru_turn0, "gru_agg": gru_agg, "gru_hn": gru_hn, "gru_rzh": gru_rzh, "gru_r": gru_r,
                      "gru_z": gru_z, "gru_in": gru_in, "gru_turn": gru_turn, "gru_fin": gru_fin})

        @block.scalar
        def _(act):
            f = nc.scalar.activation
            any_other = act.value_load(others[0:1, 0:1], min_val=0, max_val=1)

            def att_xt(v, step, kind, u):
                L, i = LAY[kind], slot(v, step, "att_xt", (kind, u), "light")
                take(act, v, step, "xt")
                act.wait_ge(L.xt_psum, nth(v, step, 4, u))
                f(xt_h[:].rearrange("p c n -> p (c n)"), LIGHT[:, i, :], ACT.Copy).then_inc(L.xt_high, 1)

            def att_wh(v, step, kind, u, q):
                L, i = LAY[kind], slot(v, step, "att_wh", (kind, u, q), "light")
                if q == 0:
                    take(act, v, step, "wh")
                w = slot(v, step, "att_wh", (kind, u, 0), "wh")
                act.wait_ge(L.wh_psum, nth(v, step, 8, 2 * u + q))
                f(wh[w][:, q, 0:L.cols], LIGHT[:, i, 0:L.cols], ACT.Copy).then_inc(L.wh_ready, 1)

            def att_scores(v, step, kind, u, q):
                L = LAY[kind]
                w = slot(v, step, "att_wh", (kind, u, 0), "wh")
                act.wait_ge(L.masked, nth(v, step, 4 * L.qs, L.qs * u + q))
                for ti, at, g, h in t_slots(v, step, kind, u):
                    if kind == "post" or g == q:
                        f(t_sc[ti][:, at, :], t_sc[ti][:, at, :], ACT.Identity, bias=wh[w][:, g, D + h:D + h + 1]).then_inc(L.shifted, 1)

            def att_prob(v, step, kind, u):
                L = LAY[kind]
                act.wait_ge(L.neg_ready, nth(v, step, 4, u))
                after(act, L.inv_ready, nth(v, step, 4, u) + -1)
                for ti, at, q, h in t_slots(v, step, kind, u):
                    if at == 0:
                        act.wait_ge(L.leaky, nth(v, step, 4 * L.qs, L.qs * u + (q if L.qs == 2 else 0)))
                    f(t_sc[ti][:, at, :], t_sc[ti][:, at, :], ACT.Exp, bias=L.neg[:, q, h:h + 1],
                      accum_out=L.sum[:, q, h:h + 1]).then_inc(L.prob, 1)

            def att_pt(v, step, kind, u, q):
                if kind == "pre" and q == 1:
                    return
                L, i = LAY[kind], slot(v, step, "att_pt", (kind, u, q), "light")
                pi = take(act, v, step, "pt")
                act.wait_ge(L.pt_psum, nth(v, step, 4 * L.qs, L.qs * u + q))
                n = L.heads if kind == "pre" else 2
                f(pt[pi][:, 0:n, :].rearrange("p h n -> p (h n)"), LIGHT[:, i, 0:n * P], ACT.Copy).then_inc(L.pt_ready, 1)

            def att_exp(v, step, kind, u):
                L = LAY[kind]
                take(act, v, step, "ex")
                act.wait_ge(L.hn_ready, nth(v, step, 4, u))
                f(ex_t[:], hn_t[slot(v, step, "att_pv", (kind, u), "hn")][:], ACT.Exp).then_inc(L.ex_ready, 1)

            def rel_adjt(v, step, u):
                i = slot(v, step, "rel_adjt", (u,), "light")
                take(act, v, step, "adjt")
                act.wait_ge(s_adjt_ps, nth(v, step, 4, u))
                f(adj_t[:], LIGHT[:, i, 0:2 * P], ACT.Copy).then_inc(s_adjt, 1)

            def rel_split(v, step, u):
                take(act, v, step, "x2s")
                b, at = u // 2, 2 * (u % 2)
                act.wait_ge(s_x2[b], nth(v, step, 2, u % 2))
                f(x2_h[:], x2[b][:, at:at + 2, :], ACT.Copy).then_inc(s_x2h, 1)

            def rel_h1(v, step, u):
                i = slot(v, step, "rel_h1", (u,), "light")
                take(act, v, step, "h1")
                act.wait_ge(s_h1_ps, nth(v, step, 4, u))
                f(h1_h[:].rearrange("p c n -> p (c n)"), LIGHT[:, i, :], ACT.Copy).then_inc(s_h1h, 1)

            def rel_rest(v, step, u):
                i = slot(v, step, "rel_rest", (u,), "light")
                with act.If(any_other > 0):
                    for r in range(2, R + 1):
                        act.wait_ge(s_hr_ps, nth(v, step, 4 * (R - 1), (R - 1) * u + r - 2))
                        f(hr_t[:].rearrange("p c n -> p (c n)"), LIGHT[:, i, :], ACT.Copy).then_inc(s_hr, 1)

            def gru_turn0(v, step, b, c):
                i = slot(v, step, "gru_turn0", (b, c), "misc")
                act.wait_ge(s_turn_ps, nth(v, step, 4, 2 * b + c))
                f(ht[b][:, c, :], MISC[:, i, :], ACT.Copy).then_inc(s_ht0, 1)

            def gru_agg(v, step, b, l, c):
                i = slot(v, step, "gru_agg", (b, l, c), "misc")
                if c == 0:
                    take(act, v, step, "agg")
                act.wait_ge(s_ag_ps, nth(v, step, 12, 4 * l + 2 * b + c))
                f(ag_h[:, c, :], MISC[:, i, :], ACT.Copy).then_inc(s_ag_h, 1)

            def gru_hn(v, step, b, l, c):
                act.wait_ge(s_ph, chunk(v, step, b, l, c))
                f(g_hn[c][:], HN_PS, ACT.Identity, bias=bias_hn[:, c:c + 1]).then_inc(s_hnb, 1)

            def gru_r(v, step, b, l, c):
                act.wait_ge(s_pr, chunk(v, step, b, l, c))
                after(act, s_t1, chunk(v, step, b, l, c) + -1)
                f(g_r[:], R_PS, ACT.Tanh, bias=bias_rz[:, c:c + 1], scale=0.5).then_inc(s_r, 1)

            def gru_z(v, step, b, l, c):
                act.wait_ge(s_pz, chunk(v, step, b, l, c))
                f(g_z[c][:], Z_PS, ACT.Tanh, bias=bias_rz[:, 2 + c:3 + c], scale=0.5).then_inc(s_z, 1)

            def gru_in(v, step, b, l, c):
                act.wait_ge(s_t2, chunk(v, step, b, l, c))
                after(act, s_hnew, chunk(v, step, b, l, c) + -1)
                f(g_n[:], g_hn[c][:], ACT.Tanh, bias=bias_in[:, c:c + 1]).then_inc(s_n, 1)

            def gru_turn(v, step, b, l, hf):
                i = slot(v, step, "gru_turn", (b, l, hf), "misc")
                if hf == 0:
                    take(act, v, step, "nodes")
                act.wait_ge(s_nd_ps, nth(v, step, 8, 4 * l + 2 * b + hf))
                f(hn_h[:, 2 * hf:2 * hf + 2, :].rearrange("p q d -> p (q d)"), MISC[:, i, :], ACT.Copy).then_inc(s_nd_h, 1)

            walk(act, {"att_xt": att_xt, "att_wh": att_wh, "att_scores": att_scores, "att_prob": att_prob, "att_pt": att_pt, "att_exp": att_exp,
                       "rel_adjt": rel_adjt, "rel_split": rel_split, "rel_h1": rel_h1, "rel_rest": rel_rest,
                       "gru_turn0": gru_turn0, "gru_agg": gru_agg, "gru_hn": gru_hn, "gru_r": gru_r, "gru_z": gru_z,
                       "gru_in": gru_in, "gru_turn": gru_turn})

        @block.vector
        def _(dve):
            tt, stt, ts = nc.vector.tensor_tensor, nc.vector.scalar_tensor_tensor, nc.vector.tensor_scalar
            any_other = dve.value_load(others[0:1, 0:1], min_val=0, max_val=1)

            def att_xt(v, step, kind, u):
                L, i = LAY[kind], slot(v, step, "att_xt", (kind, u), "light")
                dve.wait_ge(L.xt_high, nth(v, step, 4, u))
                tt(xt_l[:].rearrange("p c n -> p (c n)"), LIGHT[:, i, :], xt_h[:].rearrange("p c n -> p (c n)").bitcast(F32),
                   ALU.subtract).then_inc(L.xt_low, 1)

            def att_scores(v, step, kind, u, q):
                L, i = LAY[kind], slot(v, step, "att_scores", (kind, u, q), "light")
                ti = take(dve, v, step, "t")
                pi = slot(v, step, kind + "_load", (u,), "pen")
                dve.wait_ge(L.sc_psum, nth(v, step, 4 * L.qs, L.qs * u + q))
                dve.wait_ge(L.pen_ready, nth(v, step, 4, u))
                stand(dve)
                cells = [(q, h) for h in range(L.heads)] if kind == "pre" else [(0, 0), (1, 0)]
                for k, (g, h) in enumerate(cells):
                    last = nc.vector.tensor_tensor_reduce(out=t_sc[ti][:, k, :], in0=LIGHT[:, i, k * P:(k + 1) * P], in1=pen[pi][:, g, :],
                                                          scale=1.0, scalar=-3.0e38, op0=ALU.add, op1=ALU.max,
                                                          accum_out=L.top[:, g, h:h + 1])
                last.then_inc(L.masked, 1)

            def att_soft(v, step, kind, u):
                L = LAY[kind]
                w = slot(v, step, "att_wh", (kind, u, 0), "wh")
                dve.wait_ge(L.masked, nth(v, step, 4 * L.qs, L.qs * (u + 1) - 1))
                tt(L.top[:], L.top[:], wh[w][:, :, D:D + L.heads], ALU.add).then_inc(L.top_ready, 1)
                n = L.heads if kind == "pre" else 2
                for q in range(L.qs):
                    ti = slot(v, step, "att_scores", (kind, u, q), "t")
                    dve.wait_ge(L.shifted, nth(v, step, 8 * L.heads, 2 * L.heads * u + n * (q + 1) - 1))
                    scores = t_sc[ti][:, 0:n, :].rearrange("p h n -> p (h n)")
                    stt(scores, scores, ALPHA, scores, ALU.mult, ALU.max).then_inc(L.leaky, 1)
                dve.wait_ge(L.top_ready, nth(v, step, 4, u))
                stt(L.peak[:], L.top[:], ALPHA, L.top[:], ALU.mult, ALU.max).then_inc(L.peak_ready, 1)
                dve.wait_ge(L.peak_ready, nth(v, step, 4, u))
                ts(L.neg[:], L.peak[:], -1.0, None, ALU.mult).then_inc(L.neg_ready, 1)

            def att_pt(v, step, kind, u, q):
                if kind == "post" or q == 0:
                    return
                L, i = LAY[kind], slot(v, step, "att_pt", (kind, u, q), "light")
                pi = take(dve, v, step, "pt")
                dve.wait_ge(L.pt_ready, nth(v, step, 8, 2 * u))
                dve.wait_ge(L.pt_psum, nth(v, step, 8, 2 * u + q))
                nc.vector.tensor_copy(pt[pi][:].rearrange("p h n -> p (h n)"), LIGHT[:, i, :]).then_inc(L.pt_ready, 1)

            def att_pv(v, step, kind, u):
                L, i = LAY[kind], slot(v, step, "att_pv", (kind, u), "light")
                dve.wait_ge(L.prob, nth(v, step, 8 * L.heads, 2 * L.heads * (u + 1) - 1))
                nc.vector.reciprocal(L.inv[:], L.sum[:]).then_inc(L.inv_ready, 1)
                hi = take(dve, v, step, "hn")
                dve.wait_ge(L.pv_psum, nth(v, step, 4, u))
                dve.wait_ge(L.inv_ready, nth(v, step, 4, u))
                n = 2 * L.heads
                tt(hn_t[hi][:].rearrange("p (k f) -> p k f", k=n), LIGHT[:, i, :].rearrange("p (k f) -> p k f", k=n),
                   L.inv[:].rearrange("p q h -> p (q h)").unsqueeze(2).to_broadcast([P, n, L.f]), ALU.mult).then_inc(L.hn_ready, 1)

            def row_moments(yi, uses):
                for q in range(2):
                    nc.vector.bn_stats(stats[yi][:, q, :], y_t[yi][:, q, :]).then_inc(s_stats[yi], 1)
                for q in range(2):
                    dve.wait_ge(s_stats[yi], uses * 2 + (q + 1))
                    stand(dve)
                    nc.vector.bn_aggr(moments[yi][:, q, :], stats[yi][:, q, :]).then_inc(s_mom[yi], 1)

            def normalise(yi, uses, dst, semaphore):
                dve.wait_ge(s_rstd[yi], uses + 1)
                for q in range(2):
                    last = ts(dst[:, q, :], y_t[yi][:, q, :], moments[yi][:, q, 0:1], rstd[yi][:, q:q + 1], ALU.subtract, ALU.mult)
                last.then_inc(semaphore, 1)

            def att_res(v, step, kind, u):
                L = LAY[kind]
                yi = take(dve, v, step, "y")
                dve.wait_ge(L.ex_ready, nth(v, step, 4, u))
                res = (x_in[slot(v, step, "pre_load", (u,), "x")] if kind == "pre" else x3)[:].rearrange("p q d -> p (q d)")
                y = y_t[yi][:].rearrange("p q d -> p (q d)")
                stt(y, ex_t[:], 1.0, res, ALU.min, ALU.add).then_inc(L.min_ready, 1)
                dve.wait_ge(L.min_ready, nth(v, step, 4, u))
                stt(y, hn_t[slot(v, step, "att_pv", (kind, u), "hn")][:], 0.0, y, ALU.max, ALU.add).then_inc(L.y_ready, 1)
                dve.wait_ge(L.y_ready, nth(v, step, 4, u))
                row_moments(*ring(v, step, "y"))

            def att_norm(v, step, kind, u):
                yi, uses = ring(v, ("att_res", step[1], (kind, u)), "y")
                if kind == "pre":
                    b, at = u // 2, 2 * (u % 2)
                    after(dve, s_turn_ps, nth(v, step, 4, 2 * b + 1) + -4)
                    after(dve, s_nd_l, nth(v, step, 12, 2 * b + 1) + -12)
                    after(dve, s_x1r, nth(v, step, 2, b) + -2)
                    normalise(yi, uses, x1n[b][:, at:at + 2, :], s_x1n[b])
                else:
                    take(dve, v, step, "out")
                    normalise(yi, uses, out_t, s_outn)

            def rel_h1(v, step, u):
                i = slot(v, step, "rel_h1", (u,), "light")
                dve.wait_ge(s_h1h, nth(v, step, 4, u))
                tt(h1_l[:].rearrange("p c n -> p (c n)"), LIGHT[:, i, :], h1_h[:].rearrange("p c n -> p (c n)").bitcast(F32),
                   ALU.subtract).then_inc(s_h1l, 1)

            def rel_y1(v, step, u):
                i = slot(v, step, "rel_y1", (u,), "light")
                take(dve, v, step, "yr")
                yi = 2
                b, at = u // 2, 2 * (u % 2)
                dve.wait_ge(s_y_ps, nth(v, step, 4, u))
                dve.wait_ge(s_x2b, nth(v, step, 4, u))
                tt(y_t[yi][:], LIGHT[:, i, :].rearrange("p (q d) -> p q d", q=2), x2[b][:, at:at + 2, :], ALU.add).then_inc(s_rel_y, 1)

            def rel_rest(v, step, u):
                i = slot(v, step, "rel_rest", (u,), "light")
                dve.wait_ge(s_rel_y, nth(v, step, 4, u))
                stand(dve)
                with dve.If(any_other > 0):
                    for r in range(2, R + 1):
                        n = nth(v, step, 4 * (R - 1), (R - 1) * u + r - 2)
                        dve.wait_ge(s_yr_ps, n)
                        tt(y_t[2][:], LIGHT[:, i, :].rearrange("p (q d) -> p q d", q=2), y_t[2][:], ALU.add).then_inc(s_yr, 1)
                        dve.wait_ge(s_yr, n)
                        stand(dve)
                row_moments(*rows_of_rel(v, step, u))

            def rel_norm(v, step, u):
                take(dve, v, step, "x3")
                normalise(*rows_of_rel(v, step, u), x3, s_x3)

            def gru_nodes0(v, step, b):
                take(dve, v, step, "nodes")
                dve.wait_ge(s_x1n[b], nth(v, step, 2, 1))
                nc.vector.tensor_copy(hn_h[:], x1n[b][:]).then_inc(s_nd_h, 2)
                after(dve, s_fin_y, nth(v, step, 4, 2 * b + 1) + -4)
                nc.vector.tensor_copy(x1r[b][:], x1n[b][:]).then_inc(s_x1r, 1)

            def gru_turn0(v, step, b, c):
                if c == 1:
                    dve.wait_ge(s_ht0, nth(v, step, 4, 2 * b + 1))
                    nc.vector.tensor_copy(ht_h[b][:], ht[b][:]).then_inc(s_ht_h, 1)

            def gru_agg(v, step, b, l, c):
                i = slot(v, step, "gru_agg", (b, l, c), "misc")
                dve.wait_ge(s_ag_h, nth(v, step, 12, 4 * l + 2 * b + c))
                tt(ag_l[:, c, :], MISC[:, i, :], ag_h[:, c, :].bitcast(F32), ALU.subtract).then_inc(s_ag_l, 1)

            def gru_r(v, step, b, l, c):
                dve.wait_ge(s_hnb, chunk(v, step, b, l, c))
                dve.wait_ge(s_r, chunk(v, step, b, l, c))
                stt(g_hn[c][:], g_r[:], 1.0, g_hn[c][:], ALU.add, ALU.mult).then_inc(s_t1, 1)

            def gru_in(v, step, b, l, c):
                n = chunk(v, step, b, l, c)
                dve.wait_ge(s_t1, n)
                dve.wait_ge(s_pi, n)
                tt(g_hn[c][:], IN_PS, g_hn[c][:], ALU.add).then_inc(s_t2, 1)
                dve.wait_ge(s_d, n)
                dve.wait_ge(s_z, n)
                stt(ht[b][:, c, :], g_z[c][:], 1.0, ht[b][:, c, :], ALU.add, ALU.mult).then_inc(s_e, 1)
                dve.wait_ge(s_e, n)
                dve.wait_ge(s_n, n)
                stt(ht[b][:, c, :], ht[b][:, c, :], 0.5, g_n[:], ALU.mult, ALU.add).then_inc(s_hnew, 1)

            def gru_split(v, step, b, l):
                dve.wait_ge(s_hnew, chunk(v, step, b, l, 1))
                nc.vector.tensor_copy(ht_h[b][:], ht[b][:]).then_inc(s_ht_h, 1)

            def gru_turn(v, step, b, l, hf):
                i = slot(v, step, "gru_turn", (b, l, hf), "misc")
                dve.wait_ge(s_nd_h, nth(v, step, 12, 4 * (l + 1) + 2 * b + hf))
                rows = slice(2 * hf, 2 * hf + 2)
                tt(hn_l[:, rows, :].rearrange("p q d -> p (q d)"), MISC[:, i, :], hn_h[:, rows, :].rearrange("p q d -> p (q d)").bitcast(F32),
                   ALU.subtract).then_inc(s_nd_l, 1)

            def gru_fin(v, step, b, hf):
                i = slot(v, step, "gru_fin", (b, hf), "misc")
                take(dve, v, step, "yf")
                yi = 3
                dve.wait_ge(s_fin_ps, nth(v, step, 4, 2 * b + hf))
                dve.wait_ge(s_x1r, nth(v, step, 2, b))
                tt(y_t[yi][:], MISC[:, i, :].rearrange("p (q d) -> p q d", q=2), x1r[b][:, 2 * hf:2 * hf + 2, :], ALU.add).then_inc(s_fin_y, 1)
                dve.wait_ge(s_fin_y, nth(v, step, 4, 2 * b + hf))
                row_moments(*rows_of_gru(v, step, b, hf))

            def gru_norm(v, step, b, hf):
                after(dve, s_rel_y, nth(v, step, 4, 2 * b + hf) + -4)
                normalise(*rows_of_gru(v, step, b, hf), x2[b][:, 2 * hf:2 * hf + 2, :], s_x2[b])

            walk(dve, {"att_xt": att_xt, "att_scores": att_scores, "att_soft": att_soft, "att_pt": att_pt, "att_pv": att_pv,
                       "att_res": att_res, "att_norm": att_norm, "rel_h1": rel_h1, "rel_y1": rel_y1,
                       "rel_rest": rel_rest, "rel_norm": rel_norm, "gru_nodes0": gru_nodes0, "gru_turn0": gru_turn0,
                       "gru_agg": gru_agg, "gru_r": gru_r, "gru_in": gru_in, "gru_split": gru_split, "gru_turn": gru_turn,
                       "gru_fin": gru_fin, "gru_norm": gru_norm})

        @block.gpsimd
        def _(pool):
            ts, tt = nc.gpsimd.tensor_scalar, nc.gpsimd.tensor_tensor
            any_other = pool.value_load(others[0:1, 0:1], min_val=0, max_val=1)
            nc.gpsimd.memset(mhalf[:], -0.5).then_inc(s_half, 1)
            pool.wait_ge(s_half, 1)

            def load(v, step, u, kind):
                L = LAY[kind]
                i, uses = ring(v, step, "adj")
                pi = take(pool, v, step, "pen")
                pool.wait_ge(s_adj[i], uses * 16 + 16)
                stand(pool)
                ts(pen[pi][:], adj_i[i][:], 0, MASKED, ALU.is_le, ALU.mult).then_inc(L.pen_ready, 1)
                if kind == "post":
                    take(pool, v, step, "adjf")
                    stand(pool)
                    nc.gpsimd.tensor_copy(adj_f[:], adj_i[i][:]).then_inc(s_adjf, 1)

            def one_over_deviation(yi, uses):
                pool.wait_ge(s_mom[yi], uses * 2 + 2)
                stand(pool)
                ts(rstd[yi][:], moments[yi][:, :, 1], EPS, None, ALU.add).then_inc(s_eps[yi], 1)
                pool.wait_ge(s_eps[yi], uses + 1)
                tt(rstd[yi][:], rstd[yi][:], mhalf[:], ALU.pow).then_inc(s_rstd[yi], 1)

            def rel_mask(v, step, u):
                take(pool, v, step, "mt")
                pool.wait_ge(s_adjt, nth(v, step, 4, u))
                stand(pool)
                ts(mt1[:].rearrange("p q n -> p (q n)"), adj_t[:], 1.0, None, ALU.is_equal).then_inc(s_mt1, 1)

            def rel_rest(v, step, u):
                with pool.If(any_other > 0):
                    for r in range(2, R + 1):
                        n = nth(v, step, 4 * (R - 1), (R - 1) * u + r - 2)
                        if r > 2:
                            pool.wait_ge(s_hr_ps, n + -1)
                            stand(pool)
                        ts(mtr[:].rearrange("p q n -> p (q n)"), adj_t[:], float(r), None, ALU.is_equal).then_inc(s_mtr, 1)
                one_over_deviation(*rows_of_rel(v, step, u))

            def rel_split(v, step, u):
                b, at = u // 2, 2 * (u % 2)
                pool.wait_ge(s_x2h, nth(v, step, 4, u))
                rows = x2[b][:, at:at + 2, :]
                tt(x2_l[:], rows, x2_h[:].bitcast(F32), ALU.subtract).then_inc(s_x2l, 1)
                pool.wait_ge(s_x2l, nth(v, step, 4, u))
                tt(rows, rows, bias_rel[:].unsqueeze(1).to_broadcast([P, 2, D]), ALU.add).then_inc(s_x2b, 1)

            def gru_load(v, step, b):
                pool.wait_ge(s_adjg, nth(v, step, 2, b) * 16)
                after(pool, s_ag_ps, nth(v, step, 12, 4 * (NL - 1) + 2 * b + 1) + -12)
                stand(pool)
                ts(edges[b][:], adj_g[:], 0, 1, ALU.is_equal, ALU.is_lt).then_inc(s_edges, 1)

            def gru_nodes0(v, step, b):
                pool.wait_ge(s_nd_h, nth(v, step, 12, 2 * b + 1))
                tt(hn_l[:], x1n[b][:], hn_h[:].bitcast(F32), ALU.subtract).then_inc(s_nd_l, 2)

            def low_part(v, step, b, version):
                pool.wait_ge(s_ht_h, nth(v, step, 6, 2 * version + b))
                tt(ht_l[b][:], ht[b][:], ht_h[b][:].bitcast(F32), ALU.subtract).then_inc(s_ht_l, 1)

            def gru_turn0(v, step, b, c):
                if c == 1:
                    low_part(v, step, b, 0)

            def gru_split(v, step, b, l):
                low_part(v, step, b, l + 1)

            def gru_in(v, step, b, l, c):
                n = chunk(v, step, b, l, c)
                pool.wait_ge(s_n, n)
                tt(ht[b][:, c, :], ht[b][:, c, :], g_n[:], ALU.subtract).then_inc(s_d, 1)

            walk(pool, {"pre_load": lambda v, step, u: load(v, step, u, "pre"), "post_load": lambda v, step, u: load(v, step, u, "post"),
                        "att_res": lambda v, step, kind, u: one_over_deviation(*ring(v, step, "y")),
                        "gru_fin": lambda v, step, b, hf: one_over_deviation(*rows_of_gru(v, step, b, hf)),
                        "rel_mask": rel_mask, "rel_rest": rel_rest, "rel_split": rel_split, "gru_load": gru_load,
                        "gru_nodes0": gru_nodes0, "gru_turn0": gru_turn0, "gru_split": gru_split, "gru_in": gru_in})


_INS = ["x", "adj", "L0_gnn_W", "L0_gnn_a_src", "L0_gnn_a_dst", "L1_gnn_weight", "L1_gnn_w_ih", "L1_gnn_w_hh",
        "L1_gnn_b_ih", "L1_gnn_b_hh", "L2_gnn_adj", "L2_gnn_weight", "L2_gnn_bias", "L3_gnn_W", "L3_gnn_a"]


def kernel(**inputs):
    import numpy as _np
    import concourse.bacc as _bacc
    from concourse import mybir as _mybir
    from concourse.bass_utils import run_bass_kernel_spmd as _run

    nc = _bacc.Bacc("TRN2", target_bir_lowering=False, num_devices=1)
    arrays, args = {}, []
    for name in _INS:
        a = _np.ascontiguousarray(inputs[name])
        arrays[f"in_{name}_dram"] = a
        args.append(nc.dram_tensor(f"in_{name}_dram", a.shape, _mybir.dt.from_np(a.dtype), kind="ExternalInput").ap())
    shape = tuple(inputs["x"].shape)
    out = nc.dram_tensor("out_0_dram", shape, _mybir.dt.float32, kind="ExternalOutput").ap()
    bass_gnn_stack(nc, *args, out)
    r = _run(nc, [arrays], core_ids=[0])
    return r.results[0]["out_0_dram"]
```

```python
from contextlib import ExitStack

import concourse.bass as bass
from concourse import mybir

F32 = mybir.dt.float32
F32R = mybir.dt.float32r
I32 = mybir.dt.int32
ALU = mybir.AluOpType
ACT = mybir.ActivationFunctionType
AX_X, AX_XY = mybir.AxisListType.X, mybir.AxisListType.XY

P = 128
MASKED = -1.0e30
EPS = 1.0e-5
ALPHA = 0.2


class Segment:

    def __init__(self, order, first, end):
        self.order, self.first, self.end = order, first, end


class Visit:

    def __init__(self, g, seg):
        self.g, self.seg = g, seg


SLOTS = {"light": 2, "misc": 2, "adj": 2, "x": 2, "xt": 1, "wh": 2,
         "pre_pen": 1, "pre_t": 2, "pre_pt": 2, "pre_hn": 1, "pre_y": 1,
         "post_pen": 2, "post_t": 1, "post_pt": 1, "post_hn": 1, "post_y": 1, "x2s": 1, "h1": 1, "mt": 1, "adjt": 1, "x3": 1,
         "adjg": 1, "nodes": 1, "agg": 1, "adjf": 1, "out": 1, "yr": 1, "yf": 1}
TAKES = {
    "pre_load": ("adj", "x", "pre_pen"), "post_load": ("adj", "post_pen", "adjf"),
    "att_xt": ("light", "xt"), "att_wh": ("light",), "att_scores": ("light",),
    "att_pt": ("light",), "att_pv": ("light",),
    "rel_adjt": ("light", "adjt"), "rel_split": ("x2s",), "rel_mask": ("mt",),
    "rel_h1": ("light", "h1"), "rel_y1": ("light", "yr"),
    "rel_rest": ("light",),
    "gru_load": ("adjg",), "gru_nodes0": ("nodes",), "gru_turn0": ("misc",),
    "gru_agg": ("misc",), "gru_turn": ("misc",), "gru_fin": ("misc", "yf"),
}


def takes(step):
    name, _, args = step
    out = list(TAKES.get(name, ()))
    if name == "att_wh" and args[2] == 0:
        out.append("wh")
    if name == "att_scores" and (args[0] == "pre" or args[2] == 0):
        out.append(args[0] + "_t")
    if name in ("att_pt", "att_pv", "att_exp"):
        out.append(args[0] + {"att_pt": "_pt", "att_pv": "_hn", "att_exp": "_y"}[name])
    if name == "gru_turn" and args[2] == 0:
        out.append("nodes")
    if name == "gru_agg" and args[2] == 0:
        out.append("agg")
    if name == "rel_norm":
        out.append("x3")
    if name == "att_norm" and args[0] == "post":
        out.append("out")
    return out


PACE = {
    "pre_at": 0.5, "post_at": 0.5,
    "pre_first": 0,
    "turned": {"pre": 1, "post": 1},
    "weighed": {"pre": 0, "post": 0},
    "rel_first": 0, "mask": 0, "sums": 1, "product": 1, "normed": 1,
    "edges_at": 9,
    "ready_at": 2,
    "n_at": 6, "new_at": 8,
    "agg_time": 2, "turn_time": 0,
}


def places(n):
    return [None] * n


def merge(*chains):
    return [s for _, _, _, s in sorted(((k + 0.5) / len(c), n, k, s) for n, c in enumerate(chains) for k, s in enumerate(c))]


def attention_steps(kind, u, off):
    k = (kind, u)
    qs = (0, 1) if kind == "pre" else (0,)
    head = [("att_xt", off, k)] + places(PACE["turned"][kind]) + [("att_wh", off, k + (0,)), ("att_wh", off, k + (1,))]
    soft = [("att_scores", off, k + (q,)) for q in qs] + [("att_soft", off, k), ("att_prob", off, k)] + places(PACE["weighed"][kind])
    soft += [("att_pt", off, k + (q,)) for q in qs]
    return head, soft, [("att_pv", off, k), ("att_exp", off, k), ("att_res", off, k), ("att_norm", off, k)]


def pre_steps(off):
    parts = [attention_steps("pre", u, off) for u in range(4)]
    out = [("pre_load", off, (0,))] + places(PACE["pre_first"]) + parts[0][0]
    for u in range(4):
        _, soft, tail = parts[u]
        if u < 3:
            out += soft[:3] + [("pre_load", off, (u + 1,))] + soft[3:] + merge(tail, parts[u + 1][0])
        else:
            out += soft + tail
    return out


def post_steps(off):
    def relational(u):
        names = (["rel_split", "rel_adjt", "rel_mask"] + places(PACE["mask"]) + ["rel_h1"] + places(PACE["sums"])
                 + ["rel_y1"] + places(PACE["product"]) + ["rel_rest", "rel_norm"] + places(PACE["normed"]))
        return [("post_load", off, (u,)), None] + [name and (name, off, (u,)) for name in names]

    out = relational(0)
    out[2:2] = places(PACE["rel_first"])
    for u in range(4):
        head, soft, tail = attention_steps("post", u, off)
        own = head + soft + tail + [("att_store", off, ("post", u))]
        out += merge(own, relational(u + 1)) if u < 3 else own
    return out


def gate_steps(b, l, off, mid):
    gates = [(name, off, (b, l, c)) for c in range(2) for name in ("gru_hn", "gru_rzh", "gru_r", "gru_z", "gru_in")]
    out = []
    for k, gate in enumerate(gates):
        out += (mid[k - PACE["ready_at"]] if 0 <= k - PACE["ready_at"] < len(mid) else []) + [gate]
    out.insert(out.index(gates[PACE["n_at"]]), ("gru_n", off, (b, l, 0)))
    out.insert(out.index(gates[PACE["new_at"]]), ("gru_new", off, (b, l, 0)))
    return out


def between_layers(b, l, off):
    return [[], [("gru_split", off, (b, l))], [("gru_turn", off, (b, l, 0))], [("gru_turn", off, (b, l, 1))]]


def between_groups(b, old, new):
    def final(name, hf):
        return [] if old is None else [(name, old, (b, hf))]

    def fresh(name, *more):
        return [] if new is None else [(name, new, (b,) + more)]

    return [final("gru_fin", 0), fresh("gru_nodes0"), final("gru_norm", 0) + final("gru_fin", 1),
            fresh("gru_keep") + fresh("gru_turn0", 0), fresh("gru_turn0", 1), final("gru_norm", 1)]


def gru_steps(first, last):
    out = []
    for l in range(3):
        for b in range(2):
            if (l, b) == (0, 0):
                mid = between_groups(1, None if first else -1, 0)
            elif (l, b) == (2, 1):
                mid = between_groups(0, 0, None if last else 1)
                out += [] if last else [("gru_load", 1, (0,))]
            else:
                mid = between_layers(1 - b, l - 1 if b == 0 else l, 0)
            before = [] if (l, b) == (0, 0) else [(name, 0, (1 - b, l - (b == 0), 1)) for name in ("gru_n", "gru_new")]
            out += [("gru_agg", 0, (b, l, 0))] + before[:1] + [("gru_agg", 0, (b, l, 1))] + before[1:] + gate_steps(b, l, 0, mid)
    out.insert(PACE["edges_at"], ("gru_load", 0, (1,)))
    return out + [("gru_n", 0, (1, 2, 1)), ("gru_new", 0, (1, 2, 1))]


WEIGHT = {"gru_hn": 6, "gru_rzh": 12, "gru_r": 6, "gru_z": 6, "gru_in": 6, "gru_agg": PACE["agg_time"],
          "gru_turn": PACE["turn_time"], "gru_fin": PACE["turn_time"], "gru_turn0": PACE["turn_time"]}


def spread(main, *chains):
    total = sum(WEIGHT.get(s[0], 0) for s in main)
    extra = sorted(((k + at) / len(c) * total, n, s) for n, (c, at) in enumerate(chains) for k, s in enumerate(c) if s)
    out, time = [], 0
    for s in main:
        while extra and extra[0][0] <= time:
            out.append(extra.pop(0)[2])
        out.append(s)
        time += WEIGHT.get(s[0], 0)
    return out + [s for _, _, s in extra]


def trip(first, last):
    pre = [] if last else pre_steps(1)
    post = [] if first else post_steps(-1)
    return spread(gru_steps(first, last), (pre, PACE["pre_at"]), (post, PACE["post_at"]))


def flat(lists):
    return [s for steps in lists for s in steps]


def make_segments(groups):
    start = [s for s in pre_steps(0) if s] + [("gru_load", 0, (0,))] + flat(between_groups(0, None, 0))
    end = flat(between_groups(1, 0, None)) + [s for s in post_steps(0) if s]
    return [Segment(start, 0, 1), Segment(trip(True, False), 0, 1), Segment(trip(False, False), 1, 2),
            Segment(trip(False, False), 2, groups - 1), Segment(trip(False, True), groups - 1, groups),
            Segment(end, groups - 1, groups)]


def number_uses(segments):
    before = {r: 0 for r in SLOTS}
    for seg in segments:
        seg.uses, seg.takers = {}, {r: [] for r in SLOTS}
        count = {r: 0 for r in SLOTS}
        for s in seg.order:
            for r in takes(s):
                seg.uses[(r,) + s] = count[r]
                seg.takers[r].append(s)
                count[r] += 1
        seg.before, seg.per = dict(before), count
        for r in SLOTS:
            assert count[r] % SLOTS[r] == 0 and before[r] % SLOTS[r] == 0, r
            before[r] += count[r] * (seg.end - seg.first)


def bass_gnn_stack(nc, x, adj, L0_gnn_W, L0_gnn_a_src, L0_gnn_a_dst, L1_gnn_weight, L1_gnn_w_ih,
                   L1_gnn_w_hh, L1_gnn_b_ih, L1_gnn_b_hh, L2_gnn_adj, L2_gnn_weight, L2_gnn_bias,
                   L3_gnn_W, L3_gnn_a, out):
    B, N, D = x.shape
    R = L2_gnn_weight.shape[0]
    H0, F0 = L0_gnn_a_src.shape
    C = D // P
    G3 = 3 * D
    NL = L1_gnn_weight.shape[0]
    GROUPS = B // 8
    assert N == P and C == 2 and B % 8 == 0 and GROUPS >= 5 and R == 4 and NL == 3
    segments = make_segments(GROUPS)
    number_uses(segments)

    with ExitStack() as ctx:
        def sb(name, shape, dt=F32):
            return ctx.enter_context(nc.sbuf_tensor(name, shape, dt))

        def sem(name):
            return ctx.enter_context(nc.semaphore(name))

        psum = ctx.enter_context(nc.psum_tensor("psum", [P, 8, 512], F32))

        ident = sb("ident", [P, P])
        whh_h, whh_l = sb("whh_h", [P, C, G3], F32R), sb("whh_l", [P, C, G3], F32R)
        wc_h, wc_l = sb("wc_h", [P, NL, C, G3], F32R), sb("wc_l", [P, NL, C, G3], F32R)
        w0_h, w0_l = sb("w0_h", [P, C, D + 2 * H0], F32R), sb("w0_l", [P, C, D + 2 * H0], F32R)
        w3_h, w3_l = sb("w3_h", [P, C, D + 2], F32R), sb("w3_l", [P, C, D + 2], F32R)
        wr1_h, wr1_l = sb("wr1_h", [P, C, D], F32R), sb("wr1_l", [P, C, D], F32R)
        wrs = sb("wrs", [P, R - 1, C, D])
        bias_rel = sb("bias_rel", [P, D])
        bias_rz = sb("bias_rz", [P, 4])
        bias_hn = sb("bias_hn", [P, 2])
        bias_in = sb("bias_in", [P, 2])
        mhalf = sb("mhalf", [P, 2])
        others = sb("others", [1, 1], I32)

        with ExitStack() as early:
            def tmp(name, shape, dt=F32):
                return early.enter_context(nc.sbuf_tensor(name, shape, dt))

            hh_raw, ih_raw = tmp("hh_raw", [P, 6, D]), tmp("ih_raw", [P, 6, D])
            wl_raw = tmp("wl_raw", [P, NL, C, D])
            w0_raw, w3_raw, wr1_raw = tmp("w0_raw", [P, C, D]), tmp("w3_raw", [P, C, D]), tmp("wr1_raw", [P, C, D])
            a_src, a_dst, a3 = tmp("a_src", [P, D]), tmp("a_dst", [P, D]), tmp("a3", [P, 2 * D])
            unused = tmp("unused", [P, 2])
            bi, bh = tmp("bi", [P, 6]), tmp("bh", [P, 6])
            ihT = tmp("ihT", [P, C, G3])
            stage = tmp("stage", [P, C, G3])
            wlT = tmp("wlT", [P, NL, C, D])
            aug0, aug3 = tmp("aug0", [P, C, D + 2 * H0]), tmp("aug3", [P, C, D + 2])
            prod = tmp("prod", [P, C, D])
            SCAN = 16
            PARTS = B // SCAN
            parts = [tmp(f"part{i}", [P, SCAN, N], I32) for i in range(4)]
            tops, top, topT = tmp("tops", [P, PARTS]), tmp("top", [P, 1]), tmp("topT", [1, 1])
            s_part = [sem(f"part_loaded{i}") for i in range(4)]
            s_scan, s_top = sem("parts_scanned"), sem("tops_turned")
            s_hh, s_ih, s_w = sem("w_hh_loaded"), sem("w_ih_loaded"), sem("weights_loaded")
            s_rows = sem("rows_loaded")
            s_high = sem("products_high")
            s_wl = sem("layer_weights_ready")
            s_id0, s_id = sem("ident_zeroed"), sem("ident_ready")
            s_t, s_c = sem("setup_psum_ready"), sem("setup_banks_free")
            block = early.enter_context(nc.Block())

            @block.sync
            def _(sp):
                sp.dma_start(hh_raw[:], L1_gnn_w_hh.rearrange("(m p) d -> p m d", p=P)).then_inc(s_hh, 16)
                sp.dma_start(ih_raw[:], L1_gnn_w_ih.rearrange("(m p) d -> p m d", p=P)).then_inc(s_ih, 16)
                for dst, src in (
                    (w3_raw[:], L3_gnn_W.rearrange("(o p) i -> p o i", p=P)),
                    (wl_raw[:], L1_gnn_weight.rearrange("l (c p) e -> p l c e", p=P)),
                    (w0_raw[:], L0_gnn_W.rearrange("(c p) o -> p c o", p=P)),
                    (wr1_raw[:], L2_gnn_weight[0].rearrange("(c p) o -> p c o", p=P)),
                    (wrs[:], L2_gnn_weight[1:R].rearrange("r (c p) o -> p r c o", p=P)),
                ):
                    sp.dma_start(dst, src).then_inc(s_w, 16)
                for k in range(PARTS):
                    if k >= 4:
                        sp.wait_ge(s_scan, k - 3)
                    sp.dma_start(parts[k % 4][:], adj[k * SCAN:(k + 1) * SCAN].rearrange("g n m -> n g m")).then_inc(s_part[k % 4], 16)

            @block.scalar
            def _(act):
                with nc.allow_non_contiguous_dma(reason="a few bias columns and broadcast rows, once"):
                    for dst, src in (
                        (a_src[:], L0_gnn_a_src.rearrange("(a h) f -> a (h f)", a=1).broadcast_to([P, D])),
                        (a_dst[:], L0_gnn_a_dst.rearrange("(a h) f -> a (h f)", a=1).broadcast_to([P, D])),
                        (a3[:], L3_gnn_a.broadcast_to([P, 2 * D])),
                        (bias_rel[:], L2_gnn_bias.rearrange("(a d) -> a d", a=1).broadcast_to([P, D])),
                        (bi[:], L1_gnn_b_ih.rearrange("(m p) -> p m", p=P)),
                        (bh[:], L1_gnn_b_hh.rearrange("(m p) -> p m", p=P)),
                        (unused[:, 0:1], L2_gnn_adj.rearrange("(a d) -> a d", a=1).broadcast_to([P, 1])),
                    ):
                        act.dma_start(dst, src).then_inc(s_rows, 16)
                for l in range(NL):
                    act.wait_ge(s_t, 5 + l)
                    bank = 4 * (l % 2)
                    nc.scalar.activation(wc_h[:, l], psum[:, bank:bank + 4, :].rearrange("p (c a) n -> p c (a n)", c=C)[:, :, 0:G3],
                                         ACT.Copy).then_inc(s_high, 1)

            @block.gpsimd
            def _(pool):
                nc.gpsimd.memset(ident[:], 0.0).then_inc(s_id0, 1)
                pool.wait_ge(s_id0, 1)
                nc.gpsimd.affine_select(out=ident[:], in_=ident[:], compare_op=ALU.not_equal, fill=1.0,
                                        base=0, pattern=[[-1, P]], channel_multiplier=1).then_inc(s_id, 1)

            @block.tensor
            def _(pe):
                def turn(bank, raw, rows):
                    for c in range(C):
                        flat = psum[:, bank + 2 * c:bank + 2 * c + 2, :].rearrange("p a n -> p (a n)")
                        for m in range(rows):
                            last = nc.tensor.transpose(flat[:, m * P:(m + 1) * P], raw[:, m, c * P:(c + 1) * P], ident[:])
                    return last

                def turn_pair(bank, raws):
                    for k, raw in enumerate(raws):
                        for c in range(C):
                            for m in range(C):
                                last = nc.tensor.transpose(psum[:, bank + 2 * c + k, m * P:(m + 1) * P],
                                                           raw[:, m, c * P:(c + 1) * P], ident[:])
                    return last

                pe.wait_ge(s_id, 1)
                pe.wait_ge(s_hh, 16)
                turn(0, hh_raw, 6).then_inc(s_t, 1)
                pe.wait_ge(s_ih, 16)
                turn(4, ih_raw, 6).then_inc(s_t, 1)
                pe.wait_ge(s_w, 16 * 5)
                pe.wait_ge(s_c, 1)
                turn_pair(0, (w3_raw, wl_raw[:, 0])).then_inc(s_t, 1)
                pe.wait_ge(s_c, 2)
                turn_pair(4, (wl_raw[:, 1], wl_raw[:, 2])).then_inc(s_t, 1)
                for l in range(NL):
                    pe.wait_ge(s_c, 3 + l)
                    for c in range(C):
                        for n0, n1 in ((0, 512), (512, G3)):
                            for e in range(C):
                                last = nc.tensor.matmul(psum[:, 4 * (l % 2) + 2 * c + n0 // 512, 0:n1 - n0],
                                                        wlT[:, l, e, c * P:(c + 1) * P], ihT[:, e, n0:n1],
                                                        start=(e == 0), stop=(e == C - 1))
                    last.then_inc(s_t, 1)
                pe.wait_ge(s_scan, PARTS + 1)
                pe.wait_ge(s_c, 4 + 2)
                nc.tensor.transpose(psum[0:1, 4, 0:P], top[:], ident[:]).then_inc(s_top, 1)

            @block.vector
            def _(dve):
                chain = [0]

                def done(ins):
                    chain[0] += 1
                    ins.then_inc(s_wl, 1)
                    dve.wait_ge(s_wl, chain[0])

                def free():
                    nc.vector.memset(unused[:, 1:2], 0.0).then_inc(s_c, 1)

                def banks(bank, n):
                    return psum[:, bank:bank + 4, :].rearrange("p (c a) n -> p c (a n)", c=C)[:, :, 0:n]

                def pair(bank, k):
                    return psum[:, bank:bank + 4, :].rearrange("p (c a) n -> p c a n", c=C)[:, :, k, 0:D]

                def split(hi, lo, src):
                    done(nc.vector.tensor_copy(hi, src))
                    done(nc.vector.tensor_tensor(lo, src, hi.bitcast(F32), ALU.subtract))

                def scan(first, end):
                    for k in range(first, end):
                        dve.wait_ge(s_part[k % 4], 16 * (k // 4 + 1))
                        nc.vector.tensor_reduce(tops[:, k:k + 1], parts[k % 4][:], AX_XY, ALU.max).then_inc(s_scan, 1)

                def product_out(l):
                    dve.wait_ge(s_high, 1 + l)
                    done(nc.vector.tensor_tensor(wc_l[:, l], banks(4 * (l % 2), G3), wc_h[:, l].bitcast(F32), ALU.subtract))

                dve.wait_ge(s_t, 1)
                done(nc.vector.tensor_copy(stage[:, :, 0:2 * D], banks(0, 2 * D)))
                done(nc.vector.tensor_scalar(stage[:, :, 2 * D:G3], banks(0, G3)[:, :, 2 * D:G3], 0.5, None, ALU.mult))
                free()
                dve.wait_ge(s_t, 2)
                done(nc.vector.tensor_copy(ihT[:], banks(4, G3)))
                free()
                dve.wait_ge(s_t, 3)
                done(nc.vector.tensor_copy(aug3[:, :, 0:D], pair(0, 0)))
                done(nc.vector.tensor_copy(wlT[:, 0], pair(0, 1)))
                free()
                dve.wait_ge(s_t, 4)
                done(nc.vector.tensor_copy(wlT[:, 1], pair(4, 0)))
                done(nc.vector.tensor_copy(wlT[:, 2], pair(4, 1)))
                free()
                split(whh_h[:], whh_l[:], stage[:])
                scan(0, PARTS // 3)
                product_out(0)
                free()
                dve.wait_ge(s_w, 16 * 5)
                dve.wait_ge(s_rows, 16 * 7)
                done(nc.vector.tensor_copy(aug0[:, :, 0:D], w0_raw[:]))
                for k, a in enumerate((a_src, a_dst)):
                    done(nc.vector.tensor_tensor(prod[:], w0_raw[:], a[:].unsqueeze(1).to_broadcast([P, C, D]), ALU.mult))
                    for c in range(C):
                        done(nc.vector.tensor_reduce(aug0[:, c, D + k * H0:D + (k + 1) * H0],
                                                     prod[:, c].rearrange("p (h f) -> p h f", h=H0), AX_X, ALU.add))
                scan(PARTS // 3, 2 * PARTS // 3)
                product_out(1)
                free()
                for k in range(2):
                    done(nc.vector.tensor_tensor(prod[:], aug3[:, :, 0:D],
                                                 a3[:, k * D:(k + 1) * D].unsqueeze(1).to_broadcast([P, C, D]), ALU.mult))
                    done(nc.vector.tensor_reduce(aug3[:, :, D + k:D + k + 1], prod[:], AX_X, ALU.add))
                scan(2 * PARTS // 3, PARTS)
                dve.wait_ge(s_scan, PARTS)
                nc.vector.tensor_reduce(top[:], tops[:], AX_X, ALU.max).then_inc(s_scan, 1)
                split(w0_h[:], w0_l[:], aug0[:])
                split(w3_h[:], w3_l[:], aug3[:])
                split(wr1_h[:], wr1_l[:], wr1_raw[:])
                done(nc.vector.tensor_tensor(bias_rz[:], bi[:, 0:4], bh[:, 0:4], ALU.add))
                done(nc.vector.tensor_scalar(bias_rz[:], bias_rz[:], 0.5, None, ALU.mult))
                done(nc.vector.tensor_scalar(bias_hn[:], bh[:, 4:6], 0.5, None, ALU.mult))
                done(nc.vector.tensor_copy(bias_in[:], bi[:, 4:6]))
                product_out(2)
                dve.wait_ge(s_top, 1)
                done(nc.vector.tensor_reduce(topT[:], psum[0:1, 4, 0:P], AX_X, ALU.max))
                done(nc.vector.tensor_scalar(others[:], topT[:], 2.0, None, ALU.is_ge))

        adj_i = [sb(f"adj_i{i}", [P, 2, P], I32) for i in range(2)]
        x_in = [sb(f"x_in{i}", [P, 2, D]) for i in range(2)]
        xt_h, xt_l = sb("xt_h", [P, C, 2 * P], F32R), sb("xt_l", [P, C, 2 * P], F32R)
        wh = [sb(f"wh{i}", [P, 2, D + 2 * H0]) for i in range(2)]
        y_t = [sb(f"y_t{i}", [P, 2, D]) for i in range(4)]
        stats = [sb(f"stats{i}", [P, 2, 6]) for i in range(4)]
        moments = [sb(f"moments{i}", [P, 2, 2]) for i in range(4)]
        rstd = [sb(f"rstd{i}", [P, 2]) for i in range(4)]
        x3 = sb("x3", [P, 2, D])
        out_t = sb("out_t", [P, 2, D])
        x2_h, x2_l = sb("x2_h", [P, 2, D], F32R), sb("x2_l", [P, 2, D], F32R)
        adj_f, adj_t = sb("adj_f", [P, 2, P]), sb("adj_t", [P, 2 * P])
        mt1, mtr = sb("mt1", [P, 2, P], F32R), sb("mtr", [P, 2, P], F32R)
        h1_h, h1_l = sb("h1_h", [P, C, 2 * P], F32R), sb("h1_l", [P, C, 2 * P], F32R)
        hr_t = sb("hr_t", [P, C, 2 * P])
        adj_g = sb("adj_g", [P, 4, P], I32)
        edges = [sb(f"edges{b}", [P, 4, P], F32R) for b in range(2)]
        x1n = [sb(f"x1n{b}", [P, 4, D]) for b in range(2)]
        x1r = [sb(f"x1r{b}", [P, 4, D]) for b in range(2)]
        x2 = [sb(f"x2{b}", [P, 4, D]) for b in range(2)]
        ht = [sb(f"ht{b}", [P, C, 4 * P]) for b in range(2)]
        ht_h = [sb(f"ht_h{b}", [P, C, 4 * P], F32R) for b in range(2)]
        ht_l = [sb(f"ht_l{b}", [P, C, 4 * P], F32R) for b in range(2)]
        hn_h, hn_l = sb("hn_h", [P, 4, D], F32R), sb("hn_l", [P, 4, D], F32R)
        ag_h, ag_l = sb("ag_h", [P, C, 4 * P], F32R), sb("ag_l", [P, C, 4 * P], F32R)
        g_hn = [sb(f"g_hn{c}", [P, 512]) for c in range(2)]
        g_r, g_n = sb("g_r", [P, 512]), sb("g_n", [P, 512])
        g_z = [sb(f"g_z{c}", [P, 512]) for c in range(2)]

        Y_OF = {"pre": 0, "post": 1}

        class Layer:

            def __init__(self, kind, name, heads, w_h, w_l):
                self.heads, self.f, self.cols, self.qs = heads, D // heads, D + 2 * heads, 2 if heads > 1 else 1
                self.w_h, self.w_l = w_h, w_l
                cells = heads if heads > 1 else 2
                self.pen = [sb(f"{name}_pen{i}", [P, 2, P]) for i in range(SLOTS[kind + "_pen"])]
                self.scores = [sb(f"{name}_scores{i}", [P, cells, P]) for i in range(SLOTS[kind + "_t"])]
                self.turned = [sb(f"{name}_turned{i}", [P, cells, P]) for i in range(SLOTS[kind + "_pt"])]
                self.hn = sb(f"{name}_hn", [P, 2 * D])
                self.top, self.peak, self.neg, self.sum, self.inv = (
                    sb(f"{name}_{what}", [P, 2, heads]) for what in ("top", "peak", "neg", "sum", "inv"))
                self.xt_psum = sem("%s_xt_psum" % name)
                self.xt_high = sem("%s_xt_high" % name)
                self.xt_low = sem("%s_xt_low" % name)
                self.wh_psum = sem("%s_wh_psum" % name)
                self.wh_ready = sem("%s_wh_ready" % name)
                self.sc_psum = sem("%s_sc_psum" % name)
                self.masked = sem("%s_masked" % name)
                self.top_ready = sem("%s_top_ready" % name)
                self.peak_ready = sem("%s_peak_ready" % name)
                self.neg_ready = sem("%s_neg_ready" % name)
                self.shifted = sem("%s_shifted" % name)
                self.leaky = sem("%s_leaky" % name)
                self.prob = sem("%s_prob" % name)
                self.pt_psum = sem("%s_pt_psum" % name)
                self.pt_ready = sem("%s_pt_ready" % name)
                self.pv_psum = sem("%s_pv_psum" % name)
                self.inv_ready = sem("%s_inv_ready" % name)
                self.hn_ready = sem("%s_hn_ready" % name)
                self.ex_ready = sem("%s_ex_ready" % name)
                self.min_ready = sem("%s_min_ready" % name)
                self.y_ready = sem("%s_y_ready" % name)
                self.pen_ready = sem("%s_pen_ready" % name)

        LAY = {"pre": Layer("pre", "first", H0, w0_h, w0_l), "post": Layer("post", "last", 1, w3_h, w3_l)}

        s_x = [sem(f"x_loaded{i}") for i in range(2)]
        s_adj = [sem(f"adj_loaded{i}") for i in range(2)]
        s_adjg, s_edges, s_adjf = sem("adjg_loaded"), sem("edges_ready"), sem("adjf_ready")
        s_stats, s_mom, s_eps, s_rstd = ([sem(f"{n}{i}") for i in range(4)] for n in ("stats_ready", "moments_ready", "eps_added", "rstd_ready"))
        s_x1n = [sem(f"x1n_ready{b}") for b in range(2)]
        s_x2 = [sem(f"x2_ready{b}") for b in range(2)]
        s_x1r = sem("x1r_ready")
        s_adjt_ps, s_adjt, s_mt1, s_mtr = sem("adjt_psum"), sem("adjt_ready"), sem("mask1_ready"), sem("maskr_ready")
        s_x2h, s_x2l, s_x2b = sem("x2_high"), sem("x2_low"), sem("x2_biased")
        s_h1_ps, s_h1h, s_h1l = sem("h1_psum"), sem("h1_high"), sem("h1_low")
        s_y_ps, s_rel_y = sem("rel_psum"), sem("rel_y_ready")
        s_hr_ps, s_hr, s_yr_ps, s_yr = sem("hr_psum"), sem("hr_ready"), sem("rest_psum"), sem("rest_added")
        s_x3, s_outn, s_out = sem("x3_ready"), sem("out_ready"), sem("out_stored")
        s_turn_ps, s_ht0, s_ht_h, s_ht_l = sem("turned_psum"), sem("ht_ready"), sem("ht_high"), sem("ht_low")
        s_nd_ps, s_nd_h, s_nd_l = sem("nodes_psum"), sem("nodes_high"), sem("nodes_low")
        s_ag_ps, s_ag_h, s_ag_l = sem("agg_psum"), sem("agg_high"), sem("agg_low")
        s_ph, s_pr, s_pz, s_pi = sem("hn_psum"), sem("r_psum"), sem("z_psum"), sem("in_psum")
        s_hnb, s_r, s_z, s_t1, s_t2, s_n = (sem(n) for n in ("hn_biased", "r_ready", "z_ready", "rh_ready", "cand_sum", "n_ready"))
        s_d, s_e, s_hnew = sem("diff_ready"), sem("zdiff_ready"), sem("h_new")
        s_fin_ps, s_fin_y = sem("final_psum"), sem("final_y")
        s_rested = sem("relations_added")
        s_half = sem("exponent_ready")
        s_stood = sem("waits_stood")

        block = ctx.enter_context(nc.Block())
        LIGHT, MISC = psum[:, 0:2, :], psum[:, 2:4, :]
        HN_PS, R_PS, Z_PS, IN_PS = (psum[:, k, :] for k in range(4, 8))

        def nth(v, step, per, k):
            return v.g * per + (step[1] * per + k + 1)

        def chunk(v, step, b, l, c):
            return nth(v, step, 12, 4 * l + 2 * b + c)

        def ring(v, step, resource):
            k, n = v.seg.uses[(resource,) + step], SLOTS[resource]
            per = v.seg.per[resource] // n
            return k % n, v.g * per + (v.seg.before[resource] // n + k // n - v.seg.first * per)

        def rows_of_att(v, step, kind, u):
            return Y_OF[kind], ring(v, ("att_exp", step[1], (kind, u)), kind + "_y")[1]

        def rows_of_rel(v, step, u):
            return 2, ring(v, ("rel_y1", step[1], (u,)), "yr")[1]

        def rows_of_gru(v, step, b, hf):
            return 3, ring(v, ("gru_fin", step[1], (b, hf)), "yf")[1]

        def after(eng, semaphore, value):
            if not isinstance(value, int) or value > 0:
                eng.wait_ge(semaphore, value)

        def stand(eng):
            eng.sem_inc(s_stood, 1)

        def last_read(resource, v, step):
            name, _, a = step
            if name.startswith("att"):
                L, u = LAY[a[0]], a[1]
                qth = nth(v, step, 4 * L.qs, L.qs * u + (a[2] if len(a) > 2 else 0))
                uth = nth(v, step, 4, u)
                b = u // 2
                resource = resource.removeprefix(a[0] + "_")
                return {
                    ("light", "att_xt"): (L.xt_low, uth), ("light", "att_scores"): (L.masked, qth),
                    ("light", "att_pt"): (L.pt_ready, qth), ("light", "att_pv"): (L.hn_ready, uth),
                    ("light", "att_wh"): (L.wh_ready, nth(v, step, 8, 2 * u + (a[2] if len(a) > 2 else 0))),
                    ("xt", "att_xt"): (L.wh_psum, nth(v, step, 8, 2 * u + 1)),
                    ("wh", "att_wh"): (L.pv_psum, uth), ("t", "att_scores"): (L.pt_psum, qth),
                    ("pt", "att_pt"): (L.pv_psum, uth), ("hn", "att_pv"): (L.y_ready, uth),
                    ("y", "att_exp"): (s_x1n[b], nth(v, step, 2, u % 2)) if a[0] == "pre" else (s_outn, uth),
                    ("out", "att_norm"): (s_out, uth * 16),
                }[resource, name]
            if name == "pre_load":
                return {"adj": (LAY["pre"].pen_ready, nth(v, step, 4, a[0])), "x": (LAY["pre"].min_ready, nth(v, step, 4, a[0])),
                        "pre_pen": (LAY["pre"].masked, nth(v, step, 8, 2 * a[0] + 1))}[resource]
            if name == "post_load":
                return {"adj": (LAY["post"].pen_ready, nth(v, step, 4, a[0])), "adjf": (s_adjt_ps, nth(v, step, 4, a[0])),
                        "post_pen": (LAY["post"].masked, nth(v, step, 4, a[0]))}[resource]
            if name.startswith("rel"):
                u = a[0]
                return {
                    ("light", "rel_adjt"): (s_adjt, nth(v, step, 4, u)), ("adjt", "rel_adjt"): (s_mt1, nth(v, step, 4, u)),
                    ("x2s", "rel_split"): (s_h1_ps, nth(v, step, 4, u)), ("mt", "rel_mask"): (s_h1_ps, nth(v, step, 4, u)),
                    ("light", "rel_h1"): (s_h1l, nth(v, step, 4, u)), ("h1", "rel_h1"): (s_y_ps, nth(v, step, 4, u)),
                    ("light", "rel_y1"): (s_rel_y, nth(v, step, 4, u)), ("yr", "rel_y1"): (s_x3, nth(v, step, 4, u)),
                    ("light", "rel_rest"): (s_rested, nth(v, step, 4, u)),
                    ("x3", "rel_norm"): (LAY["post"].min_ready, nth(v, step, 4, u)),
                }[resource, name]
            b = a[0]
            if name == "gru_load":
                return s_edges, nth(v, step, 2, b)
            if name == "gru_turn0":
                return s_ht_l, nth(v, step, 12, 2 * b + a[1])
            if name == "gru_nodes0":
                return s_ag_ps, nth(v, step, 12, 2 * b + 1)
            if name == "gru_agg":
                return (s_ag_l, nth(v, step, 12, 4 * a[1] + 2 * b + a[2])) if resource == "misc" else (s_pi, chunk(v, step, b, a[1], 1))
            if name == "gru_turn":
                return (s_nd_l, nth(v, step, 12, 4 * (a[1] + 1) + 2 * b + a[2])) if resource == "misc" else \
                    (s_ag_ps, nth(v, step, 12, 4 * (a[1] + 1) + 2 * b + 1))
            assert name == "gru_fin"
            return (s_fin_y, nth(v, step, 4, 2 * b + a[1])) if resource == "misc" else (s_x2[b], nth(v, step, 2, a[1]))

        def take(eng, v, step, resource):
            seg, n = v.seg, SLOTS[resource]
            k = seg.uses[(resource,) + step]
            takers = seg.takers[resource]
            if k >= n:
                eng.wait_ge(*last_read(resource, v, takers[k - n]))
                return k % n
            earlier = [s for s in segments[:segments.index(seg)] if s.takers[resource]]
            at_end = None
            if earlier:
                tail = earlier[-1]
                at_end = last_read(resource, Visit(tail.end - 1, tail), tail.takers[resource][k - n])
                at_end = (at_end[0], at_end[1])
            if seg.end - seg.first > 1:
                wrapped = takers[k - n]
                eng.wait_ge(*last_read(resource, Visit(v.g + -1, seg), wrapped))
                first = last_read(resource, Visit(seg.first - 1, seg), wrapped)
                if at_end and first[0] is at_end[0] and first[1] == at_end[1]:
                    at_end = None
            if at_end:
                eng.wait_ge(*at_end)
            return k % n

        def walk(eng, shares):
            for seg in segments:
                if seg.end - seg.first == 1:
                    for step in seg.order:
                        if step[0] in shares:
                            shares[step[0]](Visit(seg.first, seg), step, *step[2])
                else:
                    with eng.Fori(seg.first, seg.end) as g:
                        for step in seg.order:
                            if step[0] in shares:
                                shares[step[0]](Visit(g, seg), step, *step[2])

        def slot(v, step, name, args, resource):
            return v.seg.uses[(resource, name, step[1], args)] % SLOTS[resource]

        def t_slots(v, step, kind, u):
            return [(slot(v, step, "att_scores", (kind, u, q if kind == "pre" else 0), kind + "_t"), h if kind == "pre" else q, q, h)
                    for q in range(2) for h in range(LAY[kind].heads)]

        def graphs(v, step, first, n):
            at = v.g * 8 + (step[1] * 8 + first)
            return slice(at, at + n) if isinstance(at, int) else bass.ds(at, n)

        @block.sync
        def _(sp):
            def load_adj(v, step, u):
                i = take(sp, v, step, "adj")
                sp.dma_start(adj_i[i][:], adj[graphs(v, step, 2 * u, 2)].rearrange("g n m -> n g m")).then_inc(s_adj[i], 16)

            def pre_load(v, step, u):
                load_adj(v, step, u)
                i = take(sp, v, step, "x")
                sp.dma_start(x_in[i][:], x[graphs(v, step, 2 * u, 2)].rearrange("g n d -> n g d")).then_inc(s_x[i], 16)

            def gru_load(v, step, b):
                take(sp, v, step, "adjg")
                sp.dma_start(adj_g[:], adj[graphs(v, step, 4 * b, 4)].rearrange("g n m -> n g m")).then_inc(s_adjg, 16)

            walk(sp, {"pre_load": pre_load, "post_load": load_adj, "gru_load": gru_load})
            sp.wait_ge(s_out, 16 * 4 * GROUPS)

        @block.tensor
        def _(pe):
            mm, turn = nc.tensor.matmul, nc.tensor.transpose
            any_other = pe.value_load(others[0:1, 0:1], min_val=0, max_val=1)

            def three(dst, pairs):
                n = 3 * len(pairs)
                terms = [t for (sh, sl), (mh, ml) in pairs for t in ((sh, mh), (sh, ml), (sl, mh))]
                for k, (s, m) in enumerate(terms):
                    last = mm(dst, s, m, start=(k == 0), stop=(k == n - 1))
                return last

            def att_xt(v, step, kind, u):
                L, i = LAY[kind], take(pe, v, step, "light")
                if kind == "pre":
                    xi, uses = ring(v, ("pre_load", step[1], (u,)), "x")
                    pe.wait_ge(s_x[xi], uses * 16 + 16)
                    src = x_in[xi]
                else:
                    pe.wait_ge(s_x3, nth(v, step, 4, u))
                    src = x3
                for c in range(C):
                    for q in range(2):
                        last = turn(LIGHT[:, i, (2 * c + q) * P:(2 * c + q + 1) * P], src[:, q, c * P:(c + 1) * P], ident[:])
                last.then_inc(L.xt_psum, 1)

            def att_wh(v, step, kind, u, q):
                L, i = LAY[kind], take(pe, v, step, "light")
                if q == 0:
                    pe.wait_ge(L.xt_low, nth(v, step, 4, u))
                rows = slice(q * P, (q + 1) * P)
                three(LIGHT[:, i, 0:L.cols], [((xt_h[:, c, rows], xt_l[:, c, rows]), (L.w_h[:, c, :], L.w_l[:, c, :]))
                                              for c in range(C)]).then_inc(L.wh_psum, 1)

            def att_scores(v, step, kind, u, q):
                L, i = LAY[kind], take(pe, v, step, "light")
                w = slot(v, step, "att_wh", (kind, u, 0), "wh")
                pe.wait_ge(L.wh_ready, nth(v, step, 8, 2 * u + (q if kind == "pre" else 1)))
                cells = [(q, h) for h in range(L.heads)] if kind == "pre" else [(0, 0), (1, 0)]
                for k, (g, h) in enumerate(cells):
                    col = D + L.heads + h
                    last = turn(LIGHT[:, i, k * P:(k + 1) * P], wh[w][:, g, col:col + 1].to_broadcast([P, P]), ident[:])
                last.then_inc(L.sc_psum, 1)

            def att_pt(v, step, kind, u, q):
                L, i = LAY[kind], take(pe, v, step, "light")
                cells = [s for s in t_slots(v, step, kind, u) if kind == "post" or s[2] == q]
                pe.wait_ge(L.prob, nth(v, step, 8 * L.heads, 2 * L.heads * u + (L.heads * (q + 1) if kind == "pre" else 2) - 1))
                for k, (ti, at, _, _) in enumerate(cells):
                    last = turn(LIGHT[:, i, k * P:(k + 1) * P], L.scores[ti][:, at, :], ident[:])
                last.then_inc(L.pt_psum, 1)

            def att_pv(v, step, kind, u):
                L, i = LAY[kind], take(pe, v, step, "light")
                w = slot(v, step, "att_wh", (kind, u, 0), "wh")
                pe.wait_ge(L.pt_ready, nth(v, step, 4 * L.qs, L.qs * u + L.qs - 1))
                for q in range(2):
                    for h in range(L.heads):
                        pi = slot(v, step, "att_pt", (kind, u, q if kind == "pre" else 0), kind + "_pt")
                        at = (q * L.heads + h) * L.f
                        last = mm(LIGHT[:, i, at:at + L.f], L.turned[pi][:, h if kind == "pre" else q, :],
                                  wh[w][:, q, h * L.f:(h + 1) * L.f], start=True, stop=True)
                last.then_inc(L.pv_psum, 1)

            def rel_adjt(v, step, u):
                i = take(pe, v, step, "light")
                pe.wait_ge(s_adjf, nth(v, step, 4, u))
                for q in range(2):
                    last = turn(LIGHT[:, i, q * P:(q + 1) * P], adj_f[:, q, :], ident[:])
                last.then_inc(s_adjt_ps, 1)

            def neighbours(dst, mask):
                for c in range(C):
                    for q in range(2):
                        at = (2 * c + q) * P
                        mm(dst[:, at:at + P], x2_h[:, q, c * P:(c + 1) * P], mask[:, q, :], start=True, stop=False)
                        last = mm(dst[:, at:at + P], x2_l[:, q, c * P:(c + 1) * P], mask[:, q, :], start=False, stop=True)
                return last

            def rel_h1(v, step, u):
                i = take(pe, v, step, "light")
                pe.wait_ge(s_x2l, nth(v, step, 4, u))
                pe.wait_ge(s_mt1, nth(v, step, 4, u))
                neighbours(LIGHT[:, i, :], mt1).then_inc(s_h1_ps, 1)

            def rel_y1(v, step, u):
                i = take(pe, v, step, "light")
                pe.wait_ge(s_h1l, nth(v, step, 4, u))
                for q in range(2):
                    rows = slice(q * P, (q + 1) * P)
                    last = three(LIGHT[:, i, q * D:(q + 1) * D], [((h1_h[:, c, rows], h1_l[:, c, rows]), (wr1_h[:, c, :], wr1_l[:, c, :]))
                                                                  for c in range(C)])
                last.then_inc(s_y_ps, 1)

            def rel_rest(v, step, u):
                i = take(pe, v, step, "light")
                with pe.If(any_other > 0):
                    for r in range(2, R + 1):
                        n = nth(v, step, 4 * (R - 1), (R - 1) * u + r - 2)
                        pe.wait_ge(s_mtr, n)
                        if r > 2:
                            pe.wait_ge(s_yr, n + -1)
                        neighbours(LIGHT[:, i, :], mtr).then_inc(s_hr_ps, 1)
                        pe.wait_ge(s_hr, n)
                        for q in range(2):
                            for c in range(C):
                                last = mm(LIGHT[:, i, q * D:(q + 1) * D], hr_t[:, c, q * P:(q + 1) * P], wrs[:, r - 2, c, :],
                                          start=(c == 0), stop=(c == C - 1))
                        last.then_inc(s_yr_ps, 1)

            def gru_turn0(v, step, b, c):
                i = take(pe, v, step, "misc")
                pe.wait_ge(s_x1n[b], nth(v, step, 2, 1))
                for q in range(4):
                    last = turn(MISC[:, i, q * P:(q + 1) * P], x1n[b][:, q, c * P:(c + 1) * P], ident[:])
                last.then_inc(s_turn_ps, 1)

            def gru_agg(v, step, b, l, c):
                i = take(pe, v, step, "misc")
                pe.wait_ge(s_nd_l, nth(v, step, 12, 4 * l + 2 * b + 1))
                if l == 0:
                    pe.wait_ge(s_edges, nth(v, step, 2, b))
                for q in range(4):
                    dst = MISC[:, i, q * P:(q + 1) * P]
                    mm(dst, hn_h[:, q, c * P:(c + 1) * P], edges[b][:, q, :], start=True, stop=False)
                    last = mm(dst, hn_l[:, q, c * P:(c + 1) * P], edges[b][:, q, :], start=False, stop=True)
                last.then_inc(s_ag_ps, 1)

            def gate_terms(rows, w_h, w_l, m_h, m_l):
                return [((w_h[:, k, rows], w_l[:, k, rows]), (m_h[:, k, :], m_l[:, k, :])) for k in range(C)]

            def rows_of(gate, c):
                return slice(gate * D + c * P, gate * D + (c + 1) * P)

            def accumulate(dst, terms, first, last_part):
                flat = [t for (sh, sl), (mh, ml) in terms for t in ((sh, mh), (sh, ml), (sl, mh))]
                for k, (s, m) in enumerate(flat):
                    last = mm(dst, s, m, start=(first and k == 0), stop=(last_part and k == len(flat) - 1))
                return last

            def gru_hn(v, step, b, l, c):
                pe.wait_ge(s_ht_l, nth(v, step, 12, 4 * l + 2 * b + 1))
                after(pe, s_hnb, chunk(v, step, b, l, c) + -1)
                accumulate(HN_PS, gate_terms(rows_of(2, c), whh_h, whh_l, ht_h[b], ht_l[b]), True, True).then_inc(s_ph, 1)

            def gru_rzh(v, step, b, l, c):
                after(pe, s_r, chunk(v, step, b, l, c) + -1)
                accumulate(R_PS, gate_terms(rows_of(0, c), whh_h, whh_l, ht_h[b], ht_l[b]), True, False)
                after(pe, s_z, chunk(v, step, b, l, c) + -1)
                accumulate(Z_PS, gate_terms(rows_of(1, c), whh_h, whh_l, ht_h[b], ht_l[b]), True, False)

            def gru_r(v, step, b, l, c):
                if c == 0:
                    pe.wait_ge(s_ag_l, nth(v, step, 12, 4 * l + 2 * b + 1))
                accumulate(R_PS, gate_terms(rows_of(0, c), wc_h[:, l], wc_l[:, l], ag_h, ag_l), False, True).then_inc(s_pr, 1)

            def gru_z(v, step, b, l, c):
                accumulate(Z_PS, gate_terms(rows_of(1, c), wc_h[:, l], wc_l[:, l], ag_h, ag_l), False, True).then_inc(s_pz, 1)

            def gru_in(v, step, b, l, c):
                after(pe, s_t2, chunk(v, step, b, l, c) + -1)
                accumulate(IN_PS, gate_terms(rows_of(2, c), wc_h[:, l], wc_l[:, l], ag_h, ag_l), True, True).then_inc(s_pi, 1)

            def turn_back(v, step, b, hf, semaphore):
                i = take(pe, v, step, "misc")
                for q in range(2):
                    for c in range(C):
                        last = turn(MISC[:, i, q * D + c * P:q * D + (c + 1) * P],
                                    ht[b][:, c, (2 * hf + q) * P:(2 * hf + q + 1) * P], ident[:])
                last.then_inc(semaphore, 1)

            def gru_turn(v, step, b, l, hf):
                pe.wait_ge(s_hnew, chunk(v, step, b, l, 1))
                turn_back(v, step, b, hf, s_nd_ps)

            def gru_fin(v, step, b, hf):
                pe.wait_ge(s_hnew, chunk(v, step, b, NL - 1, 1))
                turn_back(v, step, b, hf, s_fin_ps)

            walk(pe, {"att_xt": att_xt, "att_wh": att_wh, "att_scores": att_scores, "att_pt": att_pt, "att_pv": att_pv,
                      "rel_adjt": rel_adjt, "rel_h1": rel_h1, "rel_y1": rel_y1, "rel_rest": rel_rest,
                      "gru_turn0": gru_turn0, "gru_agg": gru_agg, "gru_hn": gru_hn, "gru_rzh": gru_rzh, "gru_r": gru_r,
                      "gru_z": gru_z, "gru_in": gru_in, "gru_turn": gru_turn, "gru_fin": gru_fin})

        @block.scalar
        def _(act):
            f = nc.scalar.activation
            any_other = act.value_load(others[0:1, 0:1], min_val=0, max_val=1)

            def att_xt(v, step, kind, u):
                L, i = LAY[kind], slot(v, step, "att_xt", (kind, u), "light")
                take(act, v, step, "xt")
                act.wait_ge(L.xt_psum, nth(v, step, 4, u))
                f(xt_h[:].rearrange("p c n -> p (c n)"), LIGHT[:, i, :], ACT.Copy).then_inc(L.xt_high, 1)

            def att_wh(v, step, kind, u, q):
                L, i = LAY[kind], slot(v, step, "att_wh", (kind, u, q), "light")
                if q == 0:
                    take(act, v, step, "wh")
                w = slot(v, step, "att_wh", (kind, u, 0), "wh")
                act.wait_ge(L.wh_psum, nth(v, step, 8, 2 * u + q))
                f(wh[w][:, q, 0:L.cols], LIGHT[:, i, 0:L.cols], ACT.Copy).then_inc(L.wh_ready, 1)

            def att_scores(v, step, kind, u, q):
                L = LAY[kind]
                w = slot(v, step, "att_wh", (kind, u, 0), "wh")
                act.wait_ge(L.masked, nth(v, step, 4 * L.qs, L.qs * u + q))
                for ti, at, g, h in t_slots(v, step, kind, u):
                    if kind == "post" or g == q:
                        f(L.scores[ti][:, at, :], L.scores[ti][:, at, :], ACT.Identity, bias=wh[w][:, g, D + h:D + h + 1]).then_inc(L.shifted, 1)

            def att_prob(v, step, kind, u):
                L = LAY[kind]
                act.wait_ge(L.neg_ready, nth(v, step, 4, u))
                after(act, L.inv_ready, nth(v, step, 4, u) + -1)
                for ti, at, q, h in t_slots(v, step, kind, u):
                    if at == 0:
                        act.wait_ge(L.leaky, nth(v, step, 4 * L.qs, L.qs * u + (q if L.qs == 2 else 0)))
                    f(L.scores[ti][:, at, :], L.scores[ti][:, at, :], ACT.Exp, bias=L.neg[:, q, h:h + 1],
                      accum_out=L.sum[:, q, h:h + 1]).then_inc(L.prob, 1)

            def att_pt(v, step, kind, u, q):
                if kind == "pre" and q == 1:
                    return
                L, i = LAY[kind], slot(v, step, "att_pt", (kind, u, q), "light")
                pi = take(act, v, step, kind + "_pt")
                act.wait_ge(L.pt_psum, nth(v, step, 4 * L.qs, L.qs * u + q))
                n = L.heads if kind == "pre" else 2
                f(L.turned[pi][:, 0:n, :].rearrange("p h n -> p (h n)"), LIGHT[:, i, 0:n * P], ACT.Copy).then_inc(L.pt_ready, 1)

            def att_exp(v, step, kind, u):
                L = LAY[kind]
                take(act, v, step, kind + "_y")
                act.wait_ge(L.hn_ready, nth(v, step, 4, u))
                f(y_t[Y_OF[kind]][:].rearrange("p q d -> p (q d)"), L.hn[:], ACT.Exp).then_inc(L.ex_ready, 1)

            def rel_adjt(v, step, u):
                i = slot(v, step, "rel_adjt", (u,), "light")
                take(act, v, step, "adjt")
                act.wait_ge(s_adjt_ps, nth(v, step, 4, u))
                f(adj_t[:], LIGHT[:, i, 0:2 * P], ACT.Copy).then_inc(s_adjt, 1)

            def rel_split(v, step, u):
                take(act, v, step, "x2s")
                b, at = u // 2, 2 * (u % 2)
                act.wait_ge(s_x2[b], nth(v, step, 2, u % 2))
                f(x2_h[:], x2[b][:, at:at + 2, :], ACT.Copy).then_inc(s_x2h, 1)

            def rel_h1(v, step, u):
                i = slot(v, step, "rel_h1", (u,), "light")
                take(act, v, step, "h1")
                act.wait_ge(s_h1_ps, nth(v, step, 4, u))
                f(h1_h[:].rearrange("p c n -> p (c n)"), LIGHT[:, i, :], ACT.Copy).then_inc(s_h1h, 1)

            def rel_rest(v, step, u):
                i = slot(v, step, "rel_rest", (u,), "light")
                with act.If(any_other > 0):
                    for r in range(2, R + 1):
                        act.wait_ge(s_hr_ps, nth(v, step, 4 * (R - 1), (R - 1) * u + r - 2))
                        f(hr_t[:].rearrange("p c n -> p (c n)"), LIGHT[:, i, :], ACT.Copy).then_inc(s_hr, 1)

            def gru_turn0(v, step, b, c):
                i = slot(v, step, "gru_turn0", (b, c), "misc")
                act.wait_ge(s_turn_ps, nth(v, step, 4, 2 * b + c))
                f(ht[b][:, c, :], MISC[:, i, :], ACT.Copy).then_inc(s_ht0, 1)

            def gru_agg(v, step, b, l, c):
                i = slot(v, step, "gru_agg", (b, l, c), "misc")
                if c == 0:
                    take(act, v, step, "agg")
                act.wait_ge(s_ag_ps, nth(v, step, 12, 4 * l + 2 * b + c))
                f(ag_h[:, c, :], MISC[:, i, :], ACT.Copy).then_inc(s_ag_h, 1)

            def gru_hn(v, step, b, l, c):
                act.wait_ge(s_ph, chunk(v, step, b, l, c))
                f(g_hn[c][:], HN_PS, ACT.Identity, bias=bias_hn[:, c:c + 1]).then_inc(s_hnb, 1)

            def gru_r(v, step, b, l, c):
                act.wait_ge(s_pr, chunk(v, step, b, l, c))
                after(act, s_t1, chunk(v, step, b, l, c) + -1)
                f(g_r[:], R_PS, ACT.Tanh, bias=bias_rz[:, c:c + 1], scale=0.5).then_inc(s_r, 1)

            def gru_z(v, step, b, l, c):
                act.wait_ge(s_pz, chunk(v, step, b, l, c))
                f(g_z[c][:], Z_PS, ACT.Tanh, bias=bias_rz[:, 2 + c:3 + c], scale=0.5).then_inc(s_z, 1)

            def gru_n(v, step, b, l, c):
                act.wait_ge(s_t2, chunk(v, step, b, l, c))
                after(act, s_hnew, chunk(v, step, b, l, c) + -1)
                f(g_n[:], g_hn[c][:], ACT.Tanh, bias=bias_in[:, c:c + 1]).then_inc(s_n, 1)

            def gru_turn(v, step, b, l, hf):
                i = slot(v, step, "gru_turn", (b, l, hf), "misc")
                if hf == 0:
                    take(act, v, step, "nodes")
                act.wait_ge(s_nd_ps, nth(v, step, 8, 4 * l + 2 * b + hf))
                f(hn_h[:, 2 * hf:2 * hf + 2, :].rearrange("p q d -> p (q d)"), MISC[:, i, :], ACT.Copy).then_inc(s_nd_h, 1)

            def att_store(v, step, kind, u):
                act.wait_ge(s_outn, nth(v, step, 4, u))
                act.dma_start(out[graphs(v, step, 2 * u, 2)].rearrange("g n d -> n g d"), out_t[:]).then_inc(s_out, 16)

            walk(act, {"att_store": att_store, "att_xt": att_xt, "att_wh": att_wh, "att_scores": att_scores, "att_prob": att_prob, "att_pt": att_pt, "att_exp": att_exp,
                       "rel_adjt": rel_adjt, "rel_split": rel_split, "rel_h1": rel_h1, "rel_rest": rel_rest,
                       "gru_turn0": gru_turn0, "gru_agg": gru_agg, "gru_hn": gru_hn, "gru_r": gru_r, "gru_z": gru_z,
                       "gru_n": gru_n, "gru_turn": gru_turn})

        @block.vector
        def _(dve):
            tt, stt, ts = nc.vector.tensor_tensor, nc.vector.scalar_tensor_tensor, nc.vector.tensor_scalar
            any_other = dve.value_load(others[0:1, 0:1], min_val=0, max_val=1)

            def att_xt(v, step, kind, u):
                L, i = LAY[kind], slot(v, step, "att_xt", (kind, u), "light")
                dve.wait_ge(L.xt_high, nth(v, step, 4, u))
                tt(xt_l[:].rearrange("p c n -> p (c n)"), LIGHT[:, i, :], xt_h[:].rearrange("p c n -> p (c n)").bitcast(F32),
                   ALU.subtract).then_inc(L.xt_low, 1)

            def att_scores(v, step, kind, u, q):
                L, i = LAY[kind], slot(v, step, "att_scores", (kind, u, q), "light")
                ti = take(dve, v, step, kind + "_t")
                pi = slot(v, step, kind + "_load", (u,), kind + "_pen")
                dve.wait_ge(L.sc_psum, nth(v, step, 4 * L.qs, L.qs * u + q))
                dve.wait_ge(L.pen_ready, nth(v, step, 4, u))
                stand(dve)
                cells = [(q, h) for h in range(L.heads)] if kind == "pre" else [(0, 0), (1, 0)]
                for k, (g, h) in enumerate(cells):
                    last = nc.vector.tensor_tensor_reduce(out=L.scores[ti][:, k, :], in0=LIGHT[:, i, k * P:(k + 1) * P], in1=L.pen[pi][:, g, :],
                                                          scale=1.0, scalar=-3.0e38, op0=ALU.add, op1=ALU.max,
                                                          accum_out=L.top[:, g, h:h + 1])
                last.then_inc(L.masked, 1)

            def att_soft(v, step, kind, u):
                L = LAY[kind]
                w = slot(v, step, "att_wh", (kind, u, 0), "wh")
                dve.wait_ge(L.masked, nth(v, step, 4 * L.qs, L.qs * (u + 1) - 1))
                tt(L.top[:], L.top[:], wh[w][:, :, D:D + L.heads], ALU.add).then_inc(L.top_ready, 1)
                n = L.heads if kind == "pre" else 2
                for q in range(L.qs):
                    ti = slot(v, step, "att_scores", (kind, u, q), kind + "_t")
                    dve.wait_ge(L.shifted, nth(v, step, 8 * L.heads, 2 * L.heads * u + n * (q + 1) - 1))
                    scores = L.scores[ti][:, 0:n, :].rearrange("p h n -> p (h n)")
                    stt(scores, scores, ALPHA, scores, ALU.mult, ALU.max).then_inc(L.leaky, 1)
                dve.wait_ge(L.top_ready, nth(v, step, 4, u))
                stt(L.peak[:], L.top[:], ALPHA, L.top[:], ALU.mult, ALU.max).then_inc(L.peak_ready, 1)
                dve.wait_ge(L.peak_ready, nth(v, step, 4, u))
                ts(L.neg[:], L.peak[:], -1.0, None, ALU.mult).then_inc(L.neg_ready, 1)

            def att_pt(v, step, kind, u, q):
                if kind == "post" or q == 0:
                    return
                L, i = LAY[kind], slot(v, step, "att_pt", (kind, u, q), "light")
                pi = take(dve, v, step, kind + "_pt")
                dve.wait_ge(L.pt_ready, nth(v, step, 8, 2 * u))
                dve.wait_ge(L.pt_psum, nth(v, step, 8, 2 * u + q))
                nc.vector.tensor_copy(L.turned[pi][:].rearrange("p h n -> p (h n)"), LIGHT[:, i, :]).then_inc(L.pt_ready, 1)

            def att_pv(v, step, kind, u):
                L, i = LAY[kind], slot(v, step, "att_pv", (kind, u), "light")
                dve.wait_ge(L.prob, nth(v, step, 8 * L.heads, 2 * L.heads * (u + 1) - 1))
                nc.vector.reciprocal(L.inv[:], L.sum[:]).then_inc(L.inv_ready, 1)
                take(dve, v, step, kind + "_hn")
                dve.wait_ge(L.pv_psum, nth(v, step, 4, u))
                dve.wait_ge(L.inv_ready, nth(v, step, 4, u))
                n = 2 * L.heads
                tt(L.hn[:].rearrange("p (k f) -> p k f", k=n), LIGHT[:, i, :].rearrange("p (k f) -> p k f", k=n),
                   L.inv[:].rearrange("p q h -> p (q h)").unsqueeze(2).to_broadcast([P, n, L.f]), ALU.mult).then_inc(L.hn_ready, 1)

            def row_moments(yi, uses):
                for q in range(2):
                    nc.vector.bn_stats(stats[yi][:, q, :], y_t[yi][:, q, :]).then_inc(s_stats[yi], 1)
                for q in range(2):
                    dve.wait_ge(s_stats[yi], uses * 2 + (q + 1))
                    stand(dve)
                    nc.vector.bn_aggr(moments[yi][:, q, :], stats[yi][:, q, :]).then_inc(s_mom[yi], 1)

            def normalise(yi, uses, dst, semaphore):
                dve.wait_ge(s_rstd[yi], uses + 1)
                for q in range(2):
                    last = ts(dst[:, q, :], y_t[yi][:, q, :], moments[yi][:, q, 0:1], rstd[yi][:, q:q + 1], ALU.subtract, ALU.mult)
                last.then_inc(semaphore, 1)

            def att_res(v, step, kind, u):
                L = LAY[kind]
                dve.wait_ge(L.ex_ready, nth(v, step, 4, u))
                res = (x_in[slot(v, step, "pre_load", (u,), "x")] if kind == "pre" else x3)[:].rearrange("p q d -> p (q d)")
                y = y_t[Y_OF[kind]][:].rearrange("p q d -> p (q d)")
                stt(y, y, 1.0, res, ALU.min, ALU.add).then_inc(L.min_ready, 1)
                dve.wait_ge(L.min_ready, nth(v, step, 4, u))
                stt(y, L.hn[:], 0.0, y, ALU.max, ALU.add).then_inc(L.y_ready, 1)
                dve.wait_ge(L.y_ready, nth(v, step, 4, u))
                row_moments(*rows_of_att(v, step, kind, u))

            def att_norm(v, step, kind, u):
                yi, uses = rows_of_att(v, step, kind, u)
                if kind == "pre":
                    b, at = u // 2, 2 * (u % 2)
                    after(dve, s_turn_ps, nth(v, step, 4, 2 * b + 1) + -4)
                    after(dve, s_nd_l, nth(v, step, 12, 2 * b + 1) + -12)
                    after(dve, s_x1r, nth(v, step, 2, b) + -2)
                    normalise(yi, uses, x1n[b][:, at:at + 2, :], s_x1n[b])
                else:
                    take(dve, v, step, "out")
                    normalise(yi, uses, out_t, s_outn)

            def rel_h1(v, step, u):
                i = slot(v, step, "rel_h1", (u,), "light")
                dve.wait_ge(s_h1h, nth(v, step, 4, u))
                tt(h1_l[:].rearrange("p c n -> p (c n)"), LIGHT[:, i, :], h1_h[:].rearrange("p c n -> p (c n)").bitcast(F32),
                   ALU.subtract).then_inc(s_h1l, 1)

            def rel_y1(v, step, u):
                i = slot(v, step, "rel_y1", (u,), "light")
                take(dve, v, step, "yr")
                yi = 2
                b, at = u // 2, 2 * (u % 2)
                dve.wait_ge(s_y_ps, nth(v, step, 4, u))
                dve.wait_ge(s_x2b, nth(v, step, 4, u))
                tt(y_t[yi][:], LIGHT[:, i, :].rearrange("p (q d) -> p q d", q=2), x2[b][:, at:at + 2, :], ALU.add).then_inc(s_rel_y, 1)

            def rel_rest(v, step, u):
                i = slot(v, step, "rel_rest", (u,), "light")
                dve.wait_ge(s_rel_y, nth(v, step, 4, u))
                stand(dve)
                with dve.If(any_other > 0):
                    for r in range(2, R + 1):
                        n = nth(v, step, 4 * (R - 1), (R - 1) * u + r - 2)
                        dve.wait_ge(s_yr_ps, n)
                        tt(y_t[2][:], LIGHT[:, i, :].rearrange("p (q d) -> p q d", q=2), y_t[2][:], ALU.add).then_inc(s_yr, 1)
                        dve.wait_ge(s_yr, n)
                        stand(dve)
                dve.sem_inc(s_rested, 1)
                row_moments(*rows_of_rel(v, step, u))

            def rel_norm(v, step, u):
                take(dve, v, step, "x3")
                normalise(*rows_of_rel(v, step, u), x3, s_x3)

            def gru_nodes0(v, step, b):
                take(dve, v, step, "nodes")
                dve.wait_ge(s_x1n[b], nth(v, step, 2, 1))
                nc.vector.tensor_copy(hn_h[:], x1n[b][:]).then_inc(s_nd_h, 2)

            def gru_keep(v, step, b):
                dve.wait_ge(s_x1n[b], nth(v, step, 2, 1))
                after(dve, s_fin_y, nth(v, step, 4, 2 * b + 1) + -4)
                nc.vector.tensor_copy(x1r[b][:], x1n[b][:]).then_inc(s_x1r, 1)

            def gru_turn0(v, step, b, c):
                i = slot(v, step, "gru_turn0", (b, c), "misc")
                dve.wait_ge(s_ht0, nth(v, step, 4, 2 * b + c))
                nc.vector.tensor_copy(ht_h[b][:, c, :], ht[b][:, c, :]).then_inc(s_ht_h, 1)
                dve.wait_ge(s_ht_h, nth(v, step, 12, 2 * b + c))
                tt(ht_l[b][:, c, :], MISC[:, i, :], ht_h[b][:, c, :].bitcast(F32), ALU.subtract).then_inc(s_ht_l, 1)

            def gru_agg(v, step, b, l, c):
                i = slot(v, step, "gru_agg", (b, l, c), "misc")
                dve.wait_ge(s_ag_h, nth(v, step, 12, 4 * l + 2 * b + c))
                tt(ag_l[:, c, :], MISC[:, i, :], ag_h[:, c, :].bitcast(F32), ALU.subtract).then_inc(s_ag_l, 1)

            def gru_z(v, step, b, l, c):
                dve.wait_ge(s_hnb, chunk(v, step, b, l, c))
                dve.wait_ge(s_r, chunk(v, step, b, l, c))
                stt(g_hn[c][:], g_r[:], 1.0, g_hn[c][:], ALU.add, ALU.mult).then_inc(s_t1, 1)

            def gru_in(v, step, b, l, c):
                n = chunk(v, step, b, l, c)
                dve.wait_ge(s_t1, n)
                dve.wait_ge(s_pi, n)
                tt(g_hn[c][:], IN_PS, g_hn[c][:], ALU.add).then_inc(s_t2, 1)

            def gru_new(v, step, b, l, c):
                n = chunk(v, step, b, l, c)
                dve.wait_ge(s_d, n)
                dve.wait_ge(s_z, n)
                stt(ht[b][:, c, :], g_z[c][:], 1.0, ht[b][:, c, :], ALU.add, ALU.mult).then_inc(s_e, 1)
                dve.wait_ge(s_e, n)
                dve.wait_ge(s_n, n)
                stt(ht[b][:, c, :], ht[b][:, c, :], 0.5, g_n[:], ALU.mult, ALU.add).then_inc(s_hnew, 1)

            def gru_split(v, step, b, l):
                dve.wait_ge(s_hnew, chunk(v, step, b, l, 1))
                nc.vector.tensor_copy(ht_h[b][:], ht[b][:]).then_inc(s_ht_h, 2)

            def gru_turn(v, step, b, l, hf):
                i = slot(v, step, "gru_turn", (b, l, hf), "misc")
                dve.wait_ge(s_nd_h, nth(v, step, 12, 4 * (l + 1) + 2 * b + hf))
                rows = slice(2 * hf, 2 * hf + 2)
                tt(hn_l[:, rows, :].rearrange("p q d -> p (q d)"), MISC[:, i, :], hn_h[:, rows, :].rearrange("p q d -> p (q d)").bitcast(F32),
                   ALU.subtract).then_inc(s_nd_l, 1)

            def gru_fin(v, step, b, hf):
                i = slot(v, step, "gru_fin", (b, hf), "misc")
                take(dve, v, step, "yf")
                yi = 3
                dve.wait_ge(s_fin_ps, nth(v, step, 4, 2 * b + hf))
                dve.wait_ge(s_x1r, nth(v, step, 2, b))
                tt(y_t[yi][:], MISC[:, i, :].rearrange("p (q d) -> p q d", q=2), x1r[b][:, 2 * hf:2 * hf + 2, :], ALU.add).then_inc(s_fin_y, 1)
                dve.wait_ge(s_fin_y, nth(v, step, 4, 2 * b + hf))
                row_moments(*rows_of_gru(v, step, b, hf))

            def gru_norm(v, step, b, hf):
                after(dve, s_rel_y, nth(v, step, 4, 2 * b + hf) + -4)
                normalise(*rows_of_gru(v, step, b, hf), x2[b][:, 2 * hf:2 * hf + 2, :], s_x2[b])

            walk(dve, {"att_xt": att_xt, "att_scores": att_scores, "att_soft": att_soft, "att_pt": att_pt, "att_pv": att_pv,
                       "att_res": att_res, "att_norm": att_norm, "rel_h1": rel_h1, "rel_y1": rel_y1,
                       "rel_rest": rel_rest, "rel_norm": rel_norm, "gru_nodes0": gru_nodes0, "gru_turn0": gru_turn0,
                       "gru_agg": gru_agg, "gru_z": gru_z, "gru_in": gru_in, "gru_new": gru_new, "gru_split": gru_split, "gru_turn": gru_turn,
                       "gru_fin": gru_fin, "gru_norm": gru_norm, "gru_keep": gru_keep})

        @block.gpsimd
        def _(pool):
            ts, tt = nc.gpsimd.tensor_scalar, nc.gpsimd.tensor_tensor
            any_other = pool.value_load(others[0:1, 0:1], min_val=0, max_val=1)
            nc.gpsimd.memset(mhalf[:], -0.5).then_inc(s_half, 1)
            pool.wait_ge(s_half, 1)

            def load(v, step, u, kind):
                L = LAY[kind]
                i, uses = ring(v, step, "adj")
                pool.wait_ge(s_adj[i], uses * 16 + 16)
                if kind == "post":
                    take(pool, v, step, "adjf")
                    stand(pool)
                    nc.gpsimd.tensor_copy(adj_f[:], adj_i[i][:]).then_inc(s_adjf, 1)
                pi = take(pool, v, step, kind + "_pen")
                stand(pool)
                ts(L.pen[pi][:], adj_i[i][:], 0, MASKED, ALU.is_le, ALU.mult).then_inc(L.pen_ready, 1)

            def one_over_deviation(yi, uses):
                pool.wait_ge(s_mom[yi], uses * 2 + 2)
                stand(pool)
                ts(rstd[yi][:], moments[yi][:, :, 1], EPS, None, ALU.add).then_inc(s_eps[yi], 1)
                pool.wait_ge(s_eps[yi], uses + 1)
                tt(rstd[yi][:], rstd[yi][:], mhalf[:], ALU.pow).then_inc(s_rstd[yi], 1)

            def rel_mask(v, step, u):
                take(pool, v, step, "mt")
                pool.wait_ge(s_adjt, nth(v, step, 4, u))
                stand(pool)
                ts(mt1[:].rearrange("p q n -> p (q n)"), adj_t[:], 1.0, None, ALU.is_equal).then_inc(s_mt1, 1)

            def rel_rest(v, step, u):
                with pool.If(any_other > 0):
                    for r in range(2, R + 1):
                        n = nth(v, step, 4 * (R - 1), (R - 1) * u + r - 2)
                        if r > 2:
                            pool.wait_ge(s_hr_ps, n + -1)
                            stand(pool)
                        ts(mtr[:].rearrange("p q n -> p (q n)"), adj_t[:], float(r), None, ALU.is_equal).then_inc(s_mtr, 1)
                one_over_deviation(*rows_of_rel(v, step, u))

            def rel_split(v, step, u):
                b, at = u // 2, 2 * (u % 2)
                pool.wait_ge(s_x2h, nth(v, step, 4, u))
                rows = x2[b][:, at:at + 2, :]
                tt(x2_l[:], rows, x2_h[:].bitcast(F32), ALU.subtract).then_inc(s_x2l, 1)
                pool.wait_ge(s_x2l, nth(v, step, 4, u))
                tt(rows, rows, bias_rel[:].unsqueeze(1).to_broadcast([P, 2, D]), ALU.add).then_inc(s_x2b, 1)

            def gru_load(v, step, b):
                pool.wait_ge(s_adjg, nth(v, step, 2, b) * 16)
                after(pool, s_ag_ps, nth(v, step, 12, 4 * (NL - 1) + 2 * b + 1) + -12)
                stand(pool)
                ts(edges[b][:], adj_g[:], 0, 1, ALU.is_equal, ALU.is_lt).then_inc(s_edges, 1)

            def gru_nodes0(v, step, b):
                pool.wait_ge(s_nd_h, nth(v, step, 12, 2 * b + 1))
                tt(hn_l[:], x1n[b][:], hn_h[:].bitcast(F32), ALU.subtract).then_inc(s_nd_l, 2)

            def gru_split(v, step, b, l):
                pool.wait_ge(s_ht_h, nth(v, step, 12, 4 * (l + 1) + 2 * b + 1))
                tt(ht_l[b][:], ht[b][:], ht_h[b][:].bitcast(F32), ALU.subtract).then_inc(s_ht_l, 2)

            def gru_n(v, step, b, l, c):
                n = chunk(v, step, b, l, c)
                pool.wait_ge(s_n, n)
                tt(ht[b][:, c, :], ht[b][:, c, :], g_n[:], ALU.subtract).then_inc(s_d, 1)

            walk(pool, {"pre_load": lambda v, step, u: load(v, step, u, "pre"), "post_load": lambda v, step, u: load(v, step, u, "post"),
                        "att_res": lambda v, step, kind, u: one_over_deviation(*rows_of_att(v, step, kind, u)),
                        "gru_fin": lambda v, step, b, hf: one_over_deviation(*rows_of_gru(v, step, b, hf)),
                        "rel_mask": rel_mask, "rel_rest": rel_rest, "rel_split": rel_split, "gru_load": gru_load,
                        "gru_nodes0": gru_nodes0, "gru_split": gru_split, "gru_n": gru_n})


_INS = ["x", "adj", "L0_gnn_W", "L0_gnn_a_src", "L0_gnn_a_dst", "L1_gnn_weight", "L1_gnn_w_ih", "L1_gnn_w_hh",
        "L1_gnn_b_ih", "L1_gnn_b_hh", "L2_gnn_adj", "L2_gnn_weight", "L2_gnn_bias", "L3_gnn_W", "L3_gnn_a"]


def kernel(**inputs):
    import numpy as _np
    import concourse.bacc as _bacc
    from concourse import mybir as _mybir
    from concourse.bass_utils import run_bass_kernel_spmd as _run

    nc = _bacc.Bacc("TRN2", target_bir_lowering=False, num_devices=1)
    arrays, args = {}, []
    for name in _INS:
        a = _np.ascontiguousarray(inputs[name])
        arrays[f"in_{name}_dram"] = a
        args.append(nc.dram_tensor(f"in_{name}_dram", a.shape, _mybir.dt.from_np(a.dtype), kind="ExternalInput").ap())
    shape = tuple(inputs["x"].shape)
    out = nc.dram_tensor("out_0_dram", shape, _mybir.dt.float32, kind="ExternalOutput").ap()
    bass_gnn_stack(nc, *args, out)
    r = _run(nc, [arrays], core_ids=[0])
    return r.results[0]["out_0_dram"]
```
